# Optimizing a Trainium2 kernel written in Bass

```python
import numpy as np
import jax
import jax.numpy as jnp

def _softmax(x, axis=-1):
    return jax.nn.softmax(x, axis=axis)

def _gelu(x):
    return jax.nn.gelu(x, approximate=True)

def _silu(x):
    return jax.nn.silu(x)

def _sigmoid(x):
    return jax.nn.sigmoid(x)

def _layernorm(x, axis=-1, eps=1e-05):
    m = jnp.mean(x, axis=axis, keepdims=True)
    v = jnp.var(x, axis=axis, keepdims=True)
    return (x - m) / jnp.sqrt(v + eps)

def _scatter_add(tgt, idx, src, axis=0):
    return tgt.at[idx].add(src)

def _segment_sum(src, seg, n):
    return jax.ops.segment_sum(src, seg, n)
kernel_name = 'mk_gps_d1_gnn_r8_ab289f'

def setup_inputs(seed: int=0):
    np.random.seed(seed)
    _w = jnp.asarray

    def _rec_inputs():
        import jax
        import jax.numpy as jnp
        _gk = jax.random.key(seed)
        x = -0.0002117 + 1 * jax.random.normal(jax.random.fold_in(_gk, 1), (6250, 256), jnp.float32)
        src = jax.random.randint(jax.random.fold_in(_gk, 2), (100000,), 0, 6250, jnp.int32)
        dst = jnp.minimum((6250 * jax.random.uniform(jax.random.fold_in(_gk, 3), (100000,)) ** 2.0).astype(jnp.int32), 49999)
        _o = jnp.argsort(dst, stable=True)
        src = src[_o]
        dst = dst[_o]
        return (x, src, dst)
    x, src, dst = _rec_inputs()

    def _L0_gnn_setup():
        import jax, jax.numpy as jnp
        import numpy as np
        N_NODES = 12500
        N_EDGES = 400000
        D_IN = 256
        D_OUT = 256
        LEAKY_SLOPE = 0.01
        key = jax.random.key(seed)
        ks = jax.random.split(key, 8)
        s_in = 1.0 / np.sqrt(D_IN)
        s_out = 1.0 / np.sqrt(D_OUT)
        return {'features': jax.random.normal(ks[0], (N_NODES, D_IN), dtype=jnp.float32), 'indices': jax.random.randint(ks[1], (2, N_EDGES), 0, N_NODES, dtype=jnp.int64), 'W_layer': jax.random.uniform(ks[2], (D_OUT, D_IN), jnp.float32, -s_in, s_in), 'b_layer': jax.random.uniform(ks[3], (D_OUT,), jnp.float32, -s_in, s_in), 'w_a1': jax.random.uniform(ks[4], (1, D_OUT), jnp.float32, -s_out, s_out), 'b_a1': jax.random.uniform(ks[5], (1,), jnp.float32, -s_out, s_out), 'w_a2': jax.random.uniform(ks[6], (1, D_OUT), jnp.float32, -s_out, s_out), 'b_a2': jax.random.uniform(ks[7], (1,), jnp.float32, -s_out, s_out)}
    _L0_gnn_all = _L0_gnn_setup()
    _L0_gnn_in = {k: v for k, v in _L0_gnn_all.items() if k in ('W_layer', 'b_layer', 'w_a1', 'b_a1', 'w_a2', 'b_a2')}
    del _L0_gnn_all

    def _L0_mix_setup():
        import jax, jax.numpy as jnp
        import numpy as np
        D_MODEL = 256
        NUM_HEADS = 8
        DEPTH = D_MODEL // NUM_HEADS
        B, L = (32, 512)

        def _feature_map(x):
            return jax.nn.elu(x) + 1.0
        key = jax.random.key(seed)
        ks = jax.random.split(key, 9)
        sc = 1.0 / np.sqrt(D_MODEL)
        return {'x': jax.random.normal(ks[0], (B, L, D_MODEL), dtype=jnp.float32), 'wq': jax.random.normal(ks[1], (D_MODEL, D_MODEL), dtype=jnp.float32) * sc, 'bq': jnp.zeros((D_MODEL,), dtype=jnp.float32), 'wk': jax.random.normal(ks[2], (D_MODEL, D_MODEL), dtype=jnp.float32) * sc, 'bk': jnp.zeros((D_MODEL,), dtype=jnp.float32), 'wv': jax.random.normal(ks[3], (D_MODEL, D_MODEL), dtype=jnp.float32) * sc, 'bv': jnp.zeros((D_MODEL,), dtype=jnp.float32), 'wo': jax.random.normal(ks[4], (D_MODEL, D_MODEL), dtype=jnp.float32) * sc, 'bo': jnp.zeros((D_MODEL,), dtype=jnp.float32)}
    _L0_mix_all = _L0_mix_setup()
    _L0_mix_in = {k: v for k, v in _L0_mix_all.items() if k in ('wq', 'bq', 'wk', 'bk', 'wv', 'bv', 'wo', 'bo')}
    del _L0_mix_all

    def _L0_ffn_setup():
        import jax, jax.numpy as jnp
        import numpy as np
        DIM = 256
        H = 8
        D = 64
        G = 64
        INNER = H * D
        SCALE = D ** (-0.5)
        key = jax.random.key(seed)
        ks = jax.random.split(key, 12)
        B, N = (4, 2048)
        x = jax.random.normal(ks[0], (B, N, DIM), dtype=jnp.float32)
        s = lambda fan_in: 1.0 / np.sqrt(fan_in)
        W_fx = jax.random.normal(ks[1], (DIM, INNER), dtype=jnp.float32) * s(DIM)
        b_fx = jnp.zeros((INNER,), dtype=jnp.float32)
        W_x = jax.random.normal(ks[2], (DIM, INNER), dtype=jnp.float32) * s(DIM)
        b_x = jnp.zeros((INNER,), dtype=jnp.float32)
        A = jax.random.normal(ks[3], (G, D), dtype=jnp.float32)
        Q, _ = jnp.linalg.qr(A.T)
        W_slice = Q[:, :G].astype(jnp.float32)
        b_slice = jnp.zeros((G,), dtype=jnp.float32)
        W_q = jax.random.normal(ks[4], (D, D), dtype=jnp.float32) * s(D)
        W_k = jax.random.normal(ks[5], (D, D), dtype=jnp.float32) * s(D)
        W_v = jax.random.normal(ks[6], (D, D), dtype=jnp.float32) * s(D)
        W_out = jax.random.normal(ks[7], (INNER, DIM), dtype=jnp.float32) * s(INNER)
        b_out = jnp.zeros((DIM,), dtype=jnp.float32)
        temperature = jnp.ones((1, H, 1, 1), dtype=jnp.float32) * 0.5
        return {'x': x, 'W_fx': W_fx, 'b_fx': b_fx, 'W_x': W_x, 'b_x': b_x, 'W_slice': W_slice, 'b_slice': b_slice, 'W_q': W_q, 'W_k': W_k, 'W_v': W_v, 'W_out': W_out, 'b_out': b_out, 'temperature': temperature}
    _L0_ffn_all = _L0_ffn_setup()
    _L0_ffn_in = {k: v for k, v in _L0_ffn_all.items() if k in ('W_fx', 'b_fx', 'W_x', 'b_x', 'W_slice', 'b_slice', 'W_q', 'W_k', 'W_v', 'W_out', 'b_out', 'temperature')}
    del _L0_ffn_all
    return {'x': x, 'src': src, 'dst': dst, 'L0_gnn_W_layer': _L0_gnn_in['W_layer'], 'L0_gnn_b_layer': _L0_gnn_in['b_layer'], 'L0_gnn_w_a1': _L0_gnn_in['w_a1'], 'L0_gnn_b_a1': _L0_gnn_in['b_a1'], 'L0_gnn_w_a2': _L0_gnn_in['w_a2'], 'L0_gnn_b_a2': _L0_gnn_in['b_a2'], 'L0_mix_wq': _L0_mix_in['wq'], 'L0_mix_bq': _L0_mix_in['bq'], 'L0_mix_wk': _L0_mix_in['wk'], 'L0_mix_bk': _L0_mix_in['bk'], 'L0_mix_wv': _L0_mix_in['wv'], 'L0_mix_bv': _L0_mix_in['bv'], 'L0_mix_wo': _L0_mix_in['wo'], 'L0_mix_bo': _L0_mix_in['bo'], 'L0_ffn_W_fx': _L0_ffn_in['W_fx'], 'L0_ffn_b_fx': _L0_ffn_in['b_fx'], 'L0_ffn_W_x': _L0_ffn_in['W_x'], 'L0_ffn_b_x': _L0_ffn_in['b_x'], 'L0_ffn_W_slice': _L0_ffn_in['W_slice'], 'L0_ffn_b_slice': _L0_ffn_in['b_slice'], 'L0_ffn_W_q': _L0_ffn_in['W_q'], 'L0_ffn_W_k': _L0_ffn_in['W_k'], 'L0_ffn_W_v': _L0_ffn_in['W_v'], 'L0_ffn_W_out': _L0_ffn_in['W_out'], 'L0_ffn_b_out': _L0_ffn_in['b_out'], 'L0_ffn_temperature': _L0_ffn_in['temperature']}

def reference(x, src, dst, L0_gnn_W_layer, L0_gnn_b_layer, L0_gnn_w_a1, L0_gnn_b_a1, L0_gnn_w_a2, L0_gnn_b_a2, L0_mix_wq, L0_mix_bq, L0_mix_wk, L0_mix_bk, L0_mix_wv, L0_mix_bv, L0_mix_wo, L0_mix_bo, L0_ffn_W_fx, L0_ffn_b_fx, L0_ffn_W_x, L0_ffn_b_x, L0_ffn_W_slice, L0_ffn_b_slice, L0_ffn_W_q, L0_ffn_W_k, L0_ffn_W_v, L0_ffn_W_out, L0_ffn_b_out, L0_ffn_temperature):
    import jax
    import jax.numpy as jnp

    def _L0_gnn_ref(features, indices, W_layer, b_layer, w_a1, b_a1, w_a2, b_a2):
        import jax, jax.numpy as jnp
        import numpy as np
        N_NODES = 12500
        N_EDGES = 400000
        D_IN = 256
        D_OUT = 256
        LEAKY_SLOPE = 0.01
        n = features.shape[0]
        h = features @ W_layer.T + b_layer
        a1 = (h @ w_a1.T + b_a1)[:, 0]
        a2 = (h @ w_a2.T + b_a2)[:, 0]
        row = indices[0]
        col = indices[1]
        v = jax.nn.leaky_relu(a1[row] + a2[col], negative_slope=LEAKY_SLOPE)
        m = jax.ops.segment_max(v, row, num_segments=n)
        ev = jnp.exp(v - m[row])
        s = jax.ops.segment_sum(ev, row, num_segments=n)
        att = ev / s[row]
        out = jax.ops.segment_sum(att[:, None] * h[col], row, num_segments=n)
        return out

    def _L0_mix_ref(x, wq, bq, wk, bk, wv, bv, wo, bo):
        import jax, jax.numpy as jnp
        import numpy as np
        D_MODEL = 256
        NUM_HEADS = 8
        DEPTH = D_MODEL // NUM_HEADS
        B, L = (32, 512)

        def _feature_map(x):
            return jax.nn.elu(x) + 1.0
        b, l, _ = x.shape
        q = (x @ wq + bq).reshape(b, l, NUM_HEADS, DEPTH)
        k = (x @ wk + bk).reshape(b, l, NUM_HEADS, DEPTH)
        v = (x @ wv + bv).reshape(b, l, NUM_HEADS, DEPTH)
        q = _feature_map(q)
        k = _feature_map(k)
        kv = jnp.einsum('blhd,blhe->bhde', k, v)
        k_sum = jnp.sum(k, axis=1)
        qkv = jnp.einsum('blhd,bhde->blhe', q, kv)
        normalizer = jnp.einsum('blhd,bhd->blh', q, k_sum) + 1e-06
        out = qkv / normalizer[..., None]
        out = out.reshape(b, l, D_MODEL)
        return out @ wo + bo

    def _L0_ffn_ref(x, W_fx, b_fx, W_x, b_x, W_slice, b_slice, W_q, W_k, W_v, W_out, b_out, temperature):
        import jax, jax.numpy as jnp
        import numpy as np
        DIM = 256
        H = 8
        D = 64
        G = 64
        INNER = H * D
        SCALE = D ** (-0.5)
        B, N, _ = x.shape
        fx_mid = (x @ W_fx + b_fx).reshape(B, N, H, D).transpose(0, 2, 1, 3)
        x_mid = (x @ W_x + b_x).reshape(B, N, H, D).transpose(0, 2, 1, 3)
        temp = jnp.clip(temperature, 0.1, 5.0)
        slice_weights = jax.nn.softmax((x_mid @ W_slice + b_slice) / temp, axis=-1)
        slice_norm = slice_weights.sum(axis=2)
        slice_token = jnp.einsum('bhnc,bhng->bhgc', fx_mid, slice_weights)
        slice_token = slice_token / (slice_norm[..., None] + 1e-05)
        q = slice_token @ W_q
        k = slice_token @ W_k
        v = slice_token @ W_v
        attn = jax.nn.softmax(jnp.einsum('bhgc,bhkc->bhgk', q, k) * SCALE, axis=-1)
        out_slice = jnp.einsum('bhgk,bhkc->bhgc', attn, v)
        out_x = jnp.einsum('bhgc,bhng->bhnc', out_slice, slice_weights)
        out_x = out_x.transpose(0, 2, 1, 3).reshape(B, N, INNER)
        return out_x @ W_out + b_out
    edge_index = jnp.stack([src, dst])
    xn = _layernorm(x, axis=-1)
    x = x + _L0_gnn_ref(xn, edge_index, L0_gnn_W_layer, L0_gnn_b_layer, L0_gnn_w_a1, L0_gnn_b_a1, L0_gnn_w_a2, L0_gnn_b_a2) + _L0_mix_ref(xn[None], L0_mix_wq, L0_mix_bq, L0_mix_wk, L0_mix_bk, L0_mix_wv, L0_mix_bv, L0_mix_wo, L0_mix_bo)[0]
    x = x + _L0_ffn_ref(_layernorm(x, axis=-1)[None], L0_ffn_W_fx, L0_ffn_b_fx, L0_ffn_W_x, L0_ffn_b_x, L0_ffn_W_slice, L0_ffn_b_slice, L0_ffn_W_q, L0_ffn_W_k, L0_ffn_W_v, L0_ffn_W_out, L0_ffn_b_out, L0_ffn_temperature)[0]
    return x

_drawn_inputs = setup_inputs


def setup_inputs(seed=0):
    import zlib

    import numpy as np

    out = dict(_drawn_inputs(seed))
    spreads = {'L0_mix_bq': (0.0, 2.0),
     'L0_mix_bk': (0.0, 2.0),
     'L0_mix_bv': (0.0, 0.1),
     'L0_mix_bo': (0.0, 0.1),
     'L0_ffn_b_fx': (0.0, 0.1),
     'L0_ffn_b_x': (0.0, 0.8),
     'L0_ffn_b_slice': (0.0, 2.0),
     'L0_ffn_b_out': (0.0, 0.1),
     'L0_ffn_temperature': (0.5, 0.6)}
    factors = {'L0_gnn_w_a1': 3.868,
     'L0_mix_wq': 8.0,
     'L0_mix_wk': 5.018,
     'L0_mix_wv': 3.007,
     'L0_ffn_W_x': 8.0,
     'L0_ffn_W_slice': 8.0,
     'L0_ffn_W_q': 8.0,
     'L0_ffn_W_k': 8.0}
    for name, (base, spread) in spreads.items():
        noise = np.random.default_rng([zlib.crc32(name.encode()), seed]).standard_normal(out[name].shape)
        drawn = base * np.exp(spread * noise) if base else spread * noise
        out[name] = jnp.asarray(drawn.astype(out[name].dtype))
    for name, factor in factors.items():
        out[name] = (out[name] * factor).astype(out[name].dtype)
    return out
```

```python
from contextlib import ExitStack

import concourse.bass as bass
from concourse import mybir

F32 = mybir.dt.float32
I32 = mybir.dt.int32
U8 = mybir.dt.uint8
ALU = mybir.AluOpType
ACT = mybir.ActivationFunctionType
AX = mybir.AxisListType.X

N = 6250
D = 256
E = 100000
R = 125
T = N // R
DC = D // 128
EP = 125
EJ = E // EP
TW = D + 2
Q = 17
CH = Q * 128
ITEMS = T + E // CH + 1
ITEMS += ITEMS % 2
NOBODY = 200
SB = 20
HEADS = 8
HD = D // HEADS
FH = 8
G = 64
INNER = FH * G
IC = INNER // 128
EPS = 1e-5
LN_EPS = 1e-5
NORM_EPS = 1e-6
SLICE_SCALE = G ** -0.5


class Arena:

    def __init__(self, tensor, start, end):
        self.tensor, self.at, self.end = tensor, start, end

    def take(self, partitions, *shape, dtype=F32):
        n = 1
        for s in shape:
            n *= s
        words = n if dtype in (F32, I32) else (n + 3) // 4
        assert self.at + words <= self.end, (self.at, words, self.end)
        ap = self.tensor[0:partitions, self.at:self.at + words]
        self.at += words
        if dtype != F32:
            ap = ap.bitcast(dtype)
        if len(shape) == 2:
            ap = ap.rearrange("p (a b) -> p a b", a=shape[0])
        if len(shape) == 3:
            ap = ap.rearrange("p (a b c) -> p a b c", a=shape[0], b=shape[1])
        return ap


def bass_gps(nc, x, src, dst, gnn_W, gnn_b, gnn_wa1, gnn_ba1, gnn_wa2, gnn_ba2,
             mix_wq, mix_bq, mix_wk, mix_bk, mix_wv, mix_bv, mix_wo, mix_bo,
             W_fx, b_fx, W_x, b_x, W_slice, b_slice, W_q, W_k, W_v, W_out, b_out, temperature, out):
    ctx = ExitStack()
    with ctx:
        def sem(name):
            return ctx.enter_context(nc.semaphore(name))

        def row(v):
            return v.rearrange("(a d) -> a d", a=1)

        bank = [ctx.enter_context(nc.psum_tensor(f"bank{i}", [128, 512], F32)) for i in range(8)]
        X = ctx.enter_context(nc.sbuf_tensor("X", [R, T, D], F32))
        BIG_W = T * INNER
        REST_W = 12400
        big = ctx.enter_context(nc.sbuf_tensor("big", [128, BIG_W], F32))
        rest = ctx.enter_context(nc.sbuf_tensor("rest", [128, REST_W], F32))

        table = nc.dram_tensor("node_table", [N, TW], F32, kind="Internal").ap()
        slots = nc.dram_tensor("edge_slots", [(ITEMS) * CH, 2], I32, kind="Internal").ap()

        keep = Arena(rest, 0, REST_W)
        ident = keep.take(128, 128)
        ones = keep.take(128, 128)
        iota_r = keep.take(128, 128)
        A12 = keep.take(R, T, 2)
        amax = keep.take(R, T + 1)
        item_tile = keep.take(1, ITEMS, dtype=I32)
        pairs = keep.take(1, 1, dtype=I32)
        a2min = keep.take(128, 1)
        eps = keep.take(128, 1)
        rest_at = keep.at

        with ExitStack() as _:
            a = Arena(rest, rest_at, REST_W)
            payload = a.take(EP, EJ, 2, dtype=I32)
            place = a.take(EP, EJ, dtype=I32)
            after_rank = a.at
            before = a.take(128, 128)
            iota_i = a.take(128, 128, dtype=I32)
            counts = a.take(EP, T)
            first = a.take(EP, T)
            total = a.take(EP, T)
            chunks = a.take(EP, T)
            begun = a.take(EP, T)
            fullness = a.take(EP, T, ITEMS - T)
            item_row = a.take(1, ITEMS)
            scal = a.take(1, 4)
            iota2 = a.take(128, ITEMS)
            iota2_i = a.take(128, ITEMS, dtype=I32)
            b = Arena(big, 0, BIG_W)
            masks = b.take(EP, 2, EJ, dtype=U8)
            is_tile = b.take(EP, 2, EJ, dtype=U8)
            pick = b.take(EP, 2, EJ)
            srci = b.take(EP, EJ, dtype=I32)
            dsti = b.take(EP, EJ, dtype=I32)
            srcf = b.take(EP, EJ)
            tile_i = b.take(EP, EJ, dtype=I32)
            tile_f = b.take(EP, EJ)
            scanned = b.take(EP, 2, EJ)
            placef = b.take(EP, EJ)
            one_row = b.take(EP, EJ)
            cmp = b.take(1, ITEMS, T)
            empty = b.take(128, Q, 2, dtype=I32)

            edges_in, x_in, slots_empty = sem("edges_in"), sem("x_in"), sem("slots_empty")
            pool_made, empty_made = sem("pool_made"), sem("empty_made")
            rk = sem("rank_step")
            counted, prefixed = sem("counted"), sem("prefixed")
            masked, scanned_s, picked, pick_free = sem("masked"), sem("scanned"), sem("picked"), sem("pick_free")

            with nc.Block() as block:
                @block.sync
                def _(sp):
                    sp.dma_start(srci, src.rearrange("(p j) -> p j", p=EP)).then_inc(edges_in, 16)
                    sp.dma_start(dsti, dst.rearrange("(p j) -> p j", p=EP)).then_inc(edges_in, 16)
                    xv = x.rearrange("(t p) d -> p t d", p=R)
                    for lo, hi in ((0, 112), (112, R)):
                        sp.dma_start(X[lo:hi], xv[lo:hi]).then_inc(x_in, 16)
                    sp.wait_ge(empty_made, 2)
                    sp.dma_start(slots.rearrange("(c p q) w -> p c (q w)", p=128, q=Q),
                                 empty.rearrange("p q w -> p (q w)").unsqueeze(1).to_broadcast([128, ITEMS, Q * 2])
                                 ).then_inc(slots_empty, 16)
                    sp.wait_ge(x_in, 32)
                    sp.wait_ge(slots_empty, 16)

                @block.gpsimd
                def _(pool):
                    pool.iota(iota_i, [[1, 128]], base=0, channel_multiplier=0).then_inc(pool_made, 1)
                    pool.iota(iota2_i, [[1, ITEMS]], base=0, channel_multiplier=0).then_inc(pool_made, 1)
                    pool.memset(ident, 0.0).then_inc(pool_made, 1)
                    pool.memset(before, 1.0).then_inc(pool_made, 1)
                    pool.memset(ones, 1.0).then_inc(pool_made, 1)
                    pool.wait_ge(pool_made, 5)
                    pool.affine_select(out=ident, in_=ident, compare_op=ALU.not_equal, fill=1.0, base=0,
                                       pattern=[[-1, 128]], channel_multiplier=1).then_inc(pool_made, 1)
                    pool.affine_select(out=before, in_=before, compare_op=ALU.is_gt, fill=0.0, base=0,
                                       pattern=[[1, 128]], channel_multiplier=-1).then_inc(pool_made, 1)
                    pool.memset(empty[:, :, 0], 0).then_inc(empty_made, 1)
                    pool.memset(empty[:, :, 1], NOBODY).then_inc(empty_made, 1)
                    pool.memset(placef, 0.0).then_inc(pick_free, 2)
                    with pool.Fori(0, T // 2) as k:
                        for half in range(2):
                            pool.wait_ge(picked, 2 * k + (half + 1))
                            pool.wait_ge(pick_free, 2 * k + (half + 2))
                            pool.tensor_tensor(placef, placef, pick[:, half], ALU.add).then_inc(pick_free, 1)

                @block.tensor
                def _(pe):
                    pe.wait_ge(pool_made, 7)
                    pe.wait_ge(counted, 2 + T)
                    pe.matmul(bank[0][0:EP, 0:T], before[0:EP, 0:EP], counts, start=True, stop=True)
                    pe.matmul(bank[1][0:EP, 0:T], ones[0:EP, 0:EP], counts, start=True, stop=True).then_inc(prefixed, 1)

                @block.vector
                def _(dve):
                    n = [0]

                    def step(ins):
                        n[0] += 1
                        ins.then_inc(rk, 1)
                        dve.wait_ge(rk, n[0])

                    dve.wait_ge(pool_made, 5)
                    step(dve.tensor_copy(iota_r, iota_i))
                    step(dve.tensor_copy(iota2, iota2_i))
                    dve.memset(one_row, 1.0).then_inc(counted, 1)
                    dve.memset(eps, EPS).then_inc(counted, 1)
                    dve.wait_ge(edges_in, 32)
                    step(dve.tensor_copy(srcf, srci))
                    step(dve.tensor_scalar(tile_i, srcf, 1.0 / R, 0.5 / R - 0.5, ALU.mult, ALU.add))
                    step(dve.tensor_copy(tile_f, tile_i))
                    step(dve.scalar_tensor_tensor(payload[:, :, 1], tile_f, -float(R), srcf, ALU.mult, ALU.add))
                    step(dve.tensor_copy(payload[:, :, 0], dsti))
                    with dve.Fori(0, T // 2) as k:
                        for half in range(2):
                            t = 2 * k + half
                            dve.wait_ge(counted, t + 1)
                            dve.tensor_scalar(is_tile[:, half, :], tile_f, iota_r[0:EP, bass.ds(t, 1)], 0.0,
                                              ALU.is_equal, ALU.add, accum_out=counts[:, bass.ds(t, 1)]
                                              ).then_inc(counted, 1)
                    dve.wait_ge(prefixed, 1)
                    step(dve.tensor_copy(first, bank[0][0:EP, 0:T]))
                    step(dve.tensor_copy(total, bank[1][0:EP, 0:T]))
                    step(dve.tensor_scalar(iota2[:, 0:ITEMS - T], iota2[:, 0:ITEMS - T], float(CH), None, ALU.mult))
                    step(dve.tensor_tensor(fullness, total.unsqueeze(2).to_broadcast([EP, T, ITEMS - T]),
                                           iota2[0:EP, 0:ITEMS - T].unsqueeze(1).to_broadcast([EP, T, ITEMS - T]),
                                           ALU.is_gt))
                    step(dve.tensor_reduce(chunks, fullness, AX, ALU.add))
                    step(dve.tensor_tensor_scan(begun, one_row[:, 0:T], chunks, 0.0, ALU.mult, ALU.add))
                    step(dve.tensor_tensor(total, begun, chunks, ALU.subtract))
                    step(dve.tensor_scalar(total, total, float(CH), -1.0, ALU.mult, ALU.add))
                    step(dve.tensor_tensor(first, first, total, ALU.add))
                    step(dve.tensor_copy(iota2, iota2_i))
                    step(dve.tensor_tensor(cmp, begun[0:1].unsqueeze(1).to_broadcast([1, ITEMS, T]),
                                           iota2[0:1].unsqueeze(2).to_broadcast([1, ITEMS, T]), ALU.is_le))
                    step(dve.tensor_reduce(item_row, cmp, AX, ALU.add))
                    step(dve.tensor_copy(item_tile, item_row))
                    ev = ITEMS // 2
                    step(dve.tensor_scalar(item_row[:, 0:ev], iota2[0:1, 0:ev], 2.0, None, ALU.mult))
                    step(dve.tensor_scalar(item_row[:, 0:ev], item_row[:, 0:ev], begun[0:1, T - 1:T], None, ALU.is_lt))
                    step(dve.tensor_reduce(scal[:, 0:1], item_row[:, 0:ev], AX, ALU.add))
                    step(dve.tensor_copy(pairs, scal[:, 0:1]))
                    with dve.Fori(0, T // 2) as k:
                        t = 2 * k
                        for half in range(2):
                            mask, run = masks[:, half, :], scanned[:, half]
                            dve.wait_ge(picked, t + half)
                            dve.tensor_scalar(mask, tile_f, iota_r[0:EP, bass.ds(t + half, 1)], None,
                                              ALU.is_equal).then_inc(masked, 1)
                            dve.wait_ge(masked, t + (half + 1))
                            dve.tensor_tensor_scan(run, one_row, mask, first[:, bass.ds(t + half, 1)],
                                                   ALU.mult, ALU.add).then_inc(scanned_s, 1)
                            dve.wait_ge(scanned_s, t + (half + 1))
                            dve.wait_ge(pick_free, t + (half + 1))
                            dve.tensor_tensor(pick[:, half], mask, run, ALU.mult).then_inc(picked, 1)
                    dve.wait_ge(pick_free, T + 2)
                    step(dve.tensor_copy(place, placef))

        with ExitStack() as _:
            a = Arena(rest, after_rank, REST_W)
            same_head = a.take(128, 128)
            slot_buf = a.take(EP, 2, SB, dtype=I32)
            edge_buf = a.take(EP, 2, SB, 2, dtype=I32)
            stats = a.take(R, T, 6)
            mean, var, rstd, shift = a.take(R, T), a.take(R, T), a.take(R, T), a.take(R, T)
            xn = a.take(R, TW)
            xnT = a.take(128, DC, R)
            kb, km, ks = a.take(R, D), a.take(R, D), a.take(R, D)
            qm, qr = a.take(128, DC, R), a.take(128, DC, R)
            qn = a.take(128, DC, R)
            zero_row = a.take(1, 512)
            mins = a.take(128, 4)
            b = Arena(big, 0, BIG_W)
            QT = b.take(128, DC, N)
            wq, wk, wv, wo = (b.take(128, DC, D) for _ in range(4))
            W = b.take(128, DC, D)
            wa = b.take(128, DC, 2)
            va = b.take(128, DC, 2)
            bq, gb = b.take(128, DC), b.take(128, DC)
            ba, ca = b.take(128, 2), b.take(128, 2)
            bk = b.take(R, D)
            bv, bo = b.take(1, D), b.take(1, D)
            kx = b.take(128, DC, D + 1)
            kxT = b.take(128, DC, D)
            ksum = b.take(1, D)
            kvT = b.take(128, DC, 128)
            M = b.take(128, DC, D)
            B = b.take(128, DC, 128)

            weights_in, mix_made, ra = sem("weights_in"), sem("mix_made"), sem("dve_setup_step")
            copied, scattered = [sem("copied0"), sem("copied1")], [sem("scattered0"), sem("scattered1")]
            va_psum, va_done, stats_done, std_done = sem("va_psum"), sem("va_done"), sem("stats_done"), sem("std_done")
            xn_done, xnT_psum, xnT_done = sem("xn_done"), sem("xnT_psum"), sem("xnT_done")
            av_psum, av_done, table_out = sem("av_psum"), sem("av_done"), sem("table_out")
            k_psum, kb_done, km_done, ke_done, ks_done = (sem(n) for n in ("k_psum", "kb_done", "km_done", "ke_done", "ks_done"))
            q_psum, qm_done, qe_done, q_done = (sem(n) for n in ("q_psum", "qm_done", "qe_done", "q_done"))
            kx_psum = sem("kx_psum")
            head_psum, head_done = sem("head_psum"), sem("head_done")
            norm_psum, norm_eps, norm_inv, qn_done = (sem(n) for n in ("norm_psum", "norm_eps", "norm_inv", "qn_done"))
            mix_psum, mixed = sem("mix_psum"), sem("mixed")

            with nc.Block() as block:
                @block.sync
                def _(sp):
                    def chunked(w):
                        return w.rearrange("(c p) n -> p c n", p=128)

                    def column(v):
                        return v.rearrange("(c p) -> p c", p=128)

                    loads = [(wq, chunked(mix_wq)), (wk, chunked(mix_wk)), (wv, chunked(mix_wv)), (wo, chunked(mix_wo)),
                             (W, chunked(gnn_W)), (wa[:, :, 0], column(gnn_wa1.rearrange("a d -> (a d)"))),
                             (wa[:, :, 1], column(gnn_wa2.rearrange("a d -> (a d)"))), (bq, column(mix_bq)),
                             (gb, column(gnn_b)), (ba[:, 0:1], row(gnn_ba1).to_broadcast([128, 1])),
                             (ba[:, 1:2], row(gnn_ba2).to_broadcast([128, 1])),
                             (bk, row(mix_bk).to_broadcast([R, D])), (bv, row(mix_bv)), (bo, row(mix_bo))]
                    with nc.allow_non_contiguous_dma(reason="columns of small vectors"):
                        for to, of in loads:
                            sp.dma_start(to, of).then_inc(weights_in, 16)
                    assert len(loads) == 14
                    with sp.Fori(0, T) as t:
                        sp.wait_ge(av_done, 2 * t + 2)
                        sp.dma_start(table[bass.ds(t * R, R), :], xn).then_inc(table_out, 16)
                    sp.wait_ge(table_out, 16 * T)

                @block.gpsimd
                def _(pool):
                    pool.memset(zero_row, 0.0).then_inc(mix_made, 1)
                    pool.memset(same_head, 0.0).then_inc(mix_made, 1)
                    pool.wait_ge(mix_made, 2)
                    for h in range(128 // HD):
                        pool.memset(same_head[h * HD:(h + 1) * HD, h * HD:(h + 1) * HD], 1.0).then_inc(mix_made, 1)
                    pool.wait_ge(mix_made, 2 + 128 // HD)
                    with pool.Fori(0, EJ // (2 * SB)) as k:
                        for u in range(2):
                            at = (2 * k + u) * SB
                            pool.wait_ge(scattered[u], 16 * SB * k)
                            pool.tensor_copy(slot_buf[:, u], place[:, bass.ds(at, SB)]).then_inc(copied[u], 1)
                            pool.tensor_copy(edge_buf[:, u], payload[:, bass.ds(at, SB), :]).then_inc(copied[u], 1)
                            pool.wait_ge(copied[u], 2)
                            pool.sem_clear(copied[u])
                            for j in range(SB):
                                pool.indirect_dma_start(
                                    slots, bass.IndirectOffsetOnAxis(ap=slot_buf[:, u, j:j + 1], axis=0),
                                    edge_buf[:, u, j, :], None).then_inc(scattered[u], 16)
                    for u in range(2):
                        pool.wait_ge(scattered[u], 16 * EJ // 2)

                @block.tensor
                def _(pe):
                    pe.wait_ge(weights_in, 16 * 14)
                    for c in range(DC):
                        for o in range(DC):
                            pe.matmul(bank[0][:, 2 * c:2 * c + 2], W[:, o, c * 128:(c + 1) * 128], wa[:, o, :],
                                      start=o == 0, stop=o == DC - 1)
                    for o in range(DC):
                        mm = pe.matmul(bank[0][:, 8:10], gb[:, o:o + 1].to_broadcast([128, 128]), wa[:, o, :],
                                       start=o == 0, stop=o == DC - 1)
                    mm.then_inc(va_psum, 1)
                    pe.wait_ge(mix_made, 2)
                    for c in range(DC):
                        pe.matmul(bank[6 + c][:, 0:D + 1], zero_row[:, 0:128], zero_row[:, 0:D + 1], start=True,
                                  stop=False, skip_group_check=True)
                    pe.wait_ge(va_done, 2)
                    with pe.Fori(0, T) as t:
                        pe.wait_ge(xn_done, t + 1)
                        pe.wait_ge(xnT_done, t)
                        for c in range(DC):
                            mm = pe.transpose(bank[0][:, c * R:(c + 1) * R], xn[:, c * 128:(c + 1) * 128],
                                              ident[0:R, 0:R])
                        mm.then_inc(xnT_psum, 1)
                        pe.wait_ge(xnT_done, t + 1)
                        pe.wait_ge(av_done, 2 * t)
                        for c in range(DC):
                            mm = pe.matmul(bank[1][0:R, 0:2], xnT[:, c, :], va[:, c, :], start=c == 0, stop=c == DC - 1)
                        mm.then_inc(av_psum, 1)
                        pe.wait_ge(kb_done, t)
                        for c in range(DC):
                            mm = pe.matmul(bank[2][0:R, 0:D], xnT[:, c, :], wk[:, c, :], start=c == 0, stop=c == DC - 1)
                        mm.then_inc(k_psum, 1)
                        pe.wait_ge(qm_done, 2 * t)
                        pe.wait_ge(qe_done, 3 * t)
                        for i in range(DC):
                            for c in range(DC):
                                mm = pe.matmul(bank[3][:, i * R:(i + 1) * R], wq[:, c, i * 128:(i + 1) * 128],
                                               xnT[:, c, :], start=c == 0, stop=c == DC - 1)
                        mm.then_inc(q_psum, 1)
                        pe.wait_ge(ks_done, t + 1)
                        for c in range(DC):
                            mm = pe.matmul(bank[6 + c][:, 0:D + 1], ks[:, c * 128:(c + 1) * 128], xn[:, 0:D + 1],
                                           start=False, stop=False, skip_group_check=True)
                        mm.then_inc(kx_psum, 1)
                    for c in range(DC):
                        mm = pe.matmul(bank[6 + c][:, 0:D + 1], zero_row[:, 0:128], zero_row[:, 0:D + 1], start=False,
                                       stop=True, skip_group_check=True)
                    mm.then_inc(head_psum, 1)
                    pe.wait_ge(head_done, 2)
                    for i in range(DC):
                        for c in range(DC):
                            pe.transpose(bank[0][:, (c * DC + i) * 128:(c * DC + i + 1) * 128],
                                         kx[:, i, c * 128:(c + 1) * 128], ident)
                        mm = pe.transpose(bank[1][0:1, i * 128:(i + 1) * 128], kx[:, i, D:D + 1], ident)
                    mm.then_inc(head_psum, 1)
                    pe.wait_ge(head_done, 4)
                    for c in range(DC):
                        o = bank[2][:, c * 128:(c + 1) * 128]
                        for d in range(DC):
                            pe.matmul(o, wv[:, d, c * 128:(c + 1) * 128], kxT[:, d, c * 128:(c + 1) * 128],
                                      start=d == 0, stop=False)
                        mm = pe.matmul(o, bv[:, c * 128:(c + 1) * 128], ksum[:, c * 128:(c + 1) * 128],
                                       start=False, stop=True)
                    mm.then_inc(head_psum, 1)
                    pe.wait_ge(head_done, 8)
                    for c in range(DC):
                        mm = pe.matmul(bank[3][:, c * D:(c + 1) * D], kvT[:, c, :], wo[:, c, :], start=True, stop=True)
                    mm.then_inc(head_psum, 1)
                    pe.wait_ge(head_done, 9)
                    with pe.Fori(0, T) as t:
                        pe.wait_ge(norm_eps, t)
                        for c in range(DC):
                            mm = pe.matmul(bank[0][:, c * R:(c + 1) * R], B[:, c, :], QT[:, c, bass.ds(t * R, R)],
                                           start=True, stop=True)
                        mm.then_inc(norm_psum, 1)
                        pe.wait_ge(mixed, t)
                        pe.wait_ge(qn_done, t + 1)
                        for c in range(DC):
                            pe.matmul(bank[1][0:R, 0:D], qn[:, c, :], M[:, c, :], start=c == 0, stop=False)
                        pe.matmul(bank[1][0:R, 0:D], ones[0:1, 0:R], bo, start=False, stop=True).then_inc(mix_psum, 1)
                    pe.wait_ge(head_done, 10)
                    pe.transpose(bank[2][0:1, 0:R], mins[0:R, 0:1], ident[0:R, 0:R]).then_inc(head_psum, 1)
                    pe.wait_ge(head_done, 11)
                    pe.matmul(bank[3][:, 0:1], ones[0:1, :], mins[0:1, 1:2], start=True, stop=True).then_inc(head_psum, 1)

                @block.scalar
                def _(act):
                    act.wait_ge(stats_done, 1)
                    act.activation(rstd, var, ACT.Sqrt).then_inc(std_done, 1)
                    with act.Fori(0, T) as t:
                        act.wait_ge(xnT_psum, t + 1)
                        act.wait_ge(q_psum, t)
                        act.copy(xnT.rearrange("p c r -> p (c r)"), bank[0][:, 0:DC * R]).then_inc(xnT_done, 1)
                        act.wait_ge(km_done, t + 1)
                        act.activation(km, km, ACT.Exp).then_inc(ke_done, 1)
                        act.wait_ge(q_done, t)
                        act.wait_ge(qm_done, 2 * t + 2)
                        for c in range(DC):
                            act.activation(qr[:, c, :], bank[3][:, c * R:(c + 1) * R], ACT.Relu,
                                           bias=bq[:, c:c + 1]).then_inc(qe_done, 1)
                        act.activation(qm.rearrange("p c r -> p (c r)"), qm.rearrange("p c r -> p (c r)"),
                                       ACT.Exp).then_inc(qe_done, 1)

                @block.vector
                def _(dve):
                    n = [0]

                    def step(ins):
                        n[0] += 1
                        ins.then_inc(ra, 1)
                        dve.wait_ge(ra, n[0])

                    with dve.Fori(0, T) as t:
                        dve.bn_stats(stats[:, t, :], X[:, t, :]).then_inc(ra, 1)
                    n[0] = T
                    dve.wait_ge(ra, T)
                    mo, me = stats[:, :, 4], stats[:, :, 1]
                    step(dve.tensor_tensor(mean, me, mo, ALU.add))
                    step(dve.tensor_tensor(shift, me, mo, ALU.subtract))
                    step(dve.tensor_scalar(mean, mean, 0.5, None, ALU.mult))
                    step(dve.tensor_tensor(shift, shift, shift, ALU.mult))
                    step(dve.tensor_tensor(var, stats[:, :, 2], stats[:, :, 5], ALU.add))
                    step(dve.tensor_scalar(var, var, 1.0 / D, LN_EPS, ALU.mult, ALU.add))
                    step(dve.scalar_tensor_tensor(var, shift, 0.25, var, ALU.mult, ALU.add))
                    dve.memset(xn[:, D:D + 1], 1.0).then_inc(stats_done, 1)
                    dve.wait_ge(std_done, 1)
                    step(dve.reciprocal(rstd, rstd))
                    step(dve.tensor_tensor(shift, rstd, rstd, ALU.mult))
                    step(dve.tensor_tensor(shift, shift, var, ALU.mult))
                    step(dve.tensor_scalar(shift, shift, -0.5, 1.5, ALU.mult, ALU.add))
                    step(dve.tensor_tensor(rstd, rstd, shift, ALU.mult))
                    step(dve.scalar_tensor_tensor(shift, mean, -1.0, rstd, ALU.mult, ALU.mult))
                    dve.wait_ge(va_psum, 1)
                    dve.tensor_copy(va.rearrange("p c w -> p (c w)"), bank[0][:, 0:2 * DC]).then_inc(va_done, 1)
                    dve.tensor_tensor(ca, bank[0][:, 8:10], ba, ALU.add).then_inc(va_done, 1)
                    with dve.Fori(0, T) as t:
                        dve.wait_ge(table_out, 16 * t)
                        dve.wait_ge(kx_psum, t)
                        dve.tensor_scalar(xn[:, 0:D], X[:, t, :], rstd[:, bass.ds(t, 1)], shift[:, bass.ds(t, 1)],
                                          ALU.mult, ALU.add).then_inc(xn_done, 1)
                        dve.wait_ge(av_psum, t + 1)
                        dve.tensor_tensor(A12[:, t, :], bank[1][0:R, 0:2], ca[0:R], ALU.add).then_inc(av_done, 1)
                        dve.wait_ge(av_done, 2 * t + 1)
                        dve.tensor_copy(xn[:, D + 1:D + 2], A12[:, t, 1:2]).then_inc(av_done, 1)
                        dve.wait_ge(k_psum, t + 1)
                        dve.tensor_tensor(kb, bank[2][0:R, 0:D], bk, ALU.add).then_inc(kb_done, 1)
                        dve.wait_ge(kb_done, t + 1)
                        dve.tensor_scalar(km, kb, 0.0, None, ALU.min).then_inc(km_done, 1)
                        dve.wait_ge(ke_done, t + 1)
                        dve.scalar_tensor_tensor(ks, kb, 0.0, km, ALU.max, ALU.add).then_inc(ks_done, 1)
                        dve.wait_ge(q_psum, t + 1)
                        dve.wait_ge(q_done, t)
                        for c in range(DC):
                            dve.tensor_scalar(qm[:, c, :], bank[3][:, c * R:(c + 1) * R], bq[:, c:c + 1], 0.0,
                                              ALU.add, ALU.min).then_inc(qm_done, 1)
                        dve.wait_ge(qe_done, 3 * t + 3)
                        dve.tensor_tensor(QT[:, :, bass.ds(t * R, R)], qr, qm, ALU.add).then_inc(q_done, 1)
                    dve.wait_ge(head_psum, 1)
                    for c in range(DC):
                        dve.tensor_copy(kx[:, c, :], bank[6 + c][:, 0:D + 1]).then_inc(head_done, 1)
                    dve.wait_ge(head_psum, 2)
                    dve.tensor_copy(kxT.rearrange("p c n -> p (c n)"), bank[0][:, :]).then_inc(head_done, 1)
                    dve.tensor_copy(ksum, bank[1][0:1, 0:D]).then_inc(head_done, 1)
                    dve.wait_ge(mix_made, 2 + 128 // HD)
                    dve.wait_ge(head_psum, 3)
                    for c in range(DC):
                        dve.tensor_tensor(kvT[:, c, :], bank[2][:, c * 128:(c + 1) * 128], same_head,
                                          ALU.mult).then_inc(head_done, 1)
                    for c in range(DC):
                        dve.tensor_scalar(B[:, c, :], same_head, kx[:, c, D:D + 1], None, ALU.mult).then_inc(head_done, 1)
                    dve.wait_ge(head_psum, 4)
                    dve.tensor_copy(M.rearrange("p c n -> p (c n)"), bank[3][:, :]).then_inc(head_done, 1)
                    with dve.Fori(0, T) as t:
                        dve.wait_ge(norm_psum, t + 1)
                        dve.wait_ge(qn_done, t)
                        dve.tensor_scalar(qr.rearrange("p c r -> p (c r)"), bank[0][:, 0:DC * R], NORM_EPS, None,
                                          ALU.add).then_inc(norm_eps, 1)
                        dve.wait_ge(norm_eps, t + 1)
                        dve.reciprocal(qr, qr).then_inc(norm_inv, 1)
                        dve.wait_ge(norm_inv, t + 1)
                        dve.wait_ge(mix_psum, t)
                        dve.tensor_tensor(qn, QT[:, :, bass.ds(t * R, R)], qr, ALU.mult).then_inc(qn_done, 1)
                        dve.wait_ge(mix_psum, t + 1)
                        dve.tensor_tensor(X[:, t, :], X[:, t, :], bank[1][0:R, 0:D], ALU.add).then_inc(mixed, 1)
                    dve.tensor_reduce(mins[0:R, 0:1], A12[:, :, 1], AX, ALU.min).then_inc(head_done, 1)
                    dve.wait_ge(head_psum, 5)
                    dve.tensor_reduce(mins[0:1, 1:2], bank[2][0:1, 0:R], AX, ALU.min).then_inc(head_done, 1)
                    dve.wait_ge(head_psum, 6)
                    dve.tensor_scalar(a2min, bank[3][:, 0:1], -1.0, None, ALU.add).then_inc(head_done, 1)

        with ExitStack() as _:
            b = Arena(big, 0, BIG_W)
            AGG = b.take(128, T + 1, TW)
            Gt = b.take(128, 2, Q * TW)
            a = Arena(rest, rest_at, REST_W)
            V = a.take(128, 2, Q, R)
            Z = a.take(128, Q, R)
            item = a.take(128, 2, Q * 2, dtype=I32)
            score, local = a.take(128, 2, Q), a.take(128, 2, Q)
            most = a.take(128, 128)
            diag = a.take(R, 2, R)
            new, base, zn, zo, mn, mo, fade = (a.take(R, 1) for _ in range(7))
            PER = 16 * Q

            item_in, gathered, used = ([sem(f"{n}{u}") for u in range(2)] for n in ("item_in", "gathered", "used"))
            agg_zero, s_score, s_v, s_most, s_mostT = (sem(n) for n in ("agg_zero", "s_score", "s_v", "s_most", "s_mostT"))
            s_small, s_fade, s_rows, s_z, s_leaky, s_zm, s_exp = (sem(n) for n in (
                "s_small", "s_fade", "s_rows", "s_z", "s_leaky", "s_zm", "s_exp"))
            s_w, s_agg, s_kept = sem("s_w"), sem("s_agg"), sem("s_kept")
            s_own = sem("s_own")
            own = a.take(R, T + 1)
            SM = 10

            with nc.Block() as block:
                @block.sync
                def _(sp):
                    n = sp.value_load(pairs, min_val=1, max_val=ITEMS // 2)
                    view = slots.rearrange("(c p q) w -> c p (q w)", p=128, q=Q)
                    with sp.Fori(0, n) as k:
                        for u in range(2):
                            sp.wait_ge(used[u], k + 1)
                            sp.dma_start(item[:, u, :], view[bass.ds(2 * k + u, 1)].rearrange("c p f -> (c p) f")
                                         ).then_inc(item_in[u], 16)

                @block.gpsimd
                def _(pool):
                    n = pool.value_load(pairs, min_val=1, max_val=ITEMS // 2)
                    pool.memset(AGG, 0.0).then_inc(agg_zero, 1)
                    with pool.Fori(0, n) as k:
                        for u in range(2):
                            pool.wait_ge(item_in[u], 16)
                            pool.sem_clear(item_in[u])
                            for q in range(Q):
                                pool.indirect_dma_start(
                                    Gt[:, u, q * TW:(q + 1) * TW], None, table,
                                    bass.IndirectOffsetOnAxis(ap=item[:, u, 2 * q:2 * q + 1], axis=0)
                                ).then_inc(gathered[u], 16)

                @block.tensor
                def _(pe):
                    n = pe.value_load(pairs, min_val=1, max_val=ITEMS // 2)
                    with pe.Fori(0, n) as k:
                        for u in range(2):
                            i = 2 * k + u
                            pe.wait_ge(s_most, i + 1)
                            pe.transpose(bank[0][0:R, 0:128], most[:, 0:R], ident).then_inc(s_mostT, 1)
                            pe.wait_ge(s_small, SM * i + SM)
                            pe.matmul(bank[1][:, 0:2 * R], ones[0:R, :], diag.rearrange("p a r -> p (a r)"), start=True,
                                      stop=True).then_inc(s_rows, 1)
                            pe.wait_ge(s_w, i + 1)
                            pe.wait_ge(gathered[u], PER * k + PER)
                            pe.wait_ge(s_agg, k * 2 + u)
                            for q in range(Q):
                                mm = pe.matmul(bank[2][0:R, 0:D + 1], V[:, u, q, :], Gt[:, u, q * TW:q * TW + D + 1],
                                               start=q == 0, stop=q == Q - 1)
                            mm.then_inc(used[u], 1)

                @block.scalar
                def _(act):
                    n = act.value_load(pairs, min_val=1, max_val=ITEMS // 2)
                    flat = Z.rearrange("p q r -> p (q r)")
                    with act.Fori(0, n) as k:
                        for u in range(2):
                            i = 2 * k + u
                            act.wait_ge(s_agg, i)
                            act.wait_ge(s_small, SM * i + SM)
                            act.activation(fade, mo, ACT.Exp).then_inc(s_fade, 1)
                            act.wait_ge(s_zm, i + 1)
                            act.activation(flat, flat, ACT.Exp).then_inc(s_exp, 1)

                @block.vector
                def _(dve):
                    n = dve.value_load(pairs, min_val=1, max_val=ITEMS // 2)
                    dve.memset(amax, 0.0).then_inc(used[0], 1)
                    dve.memset(most, 0.0).then_inc(used[1], 1)
                    dve.memset(own, 0.0).then_inc(s_own, 1)
                    dve.wait_ge(s_own, 1)
                    dve.tensor_copy(own[:, 0:T], A12[:, :, 0]).then_inc(s_own, 1)
                    dve.wait_ge(s_own, 2)
                    with dve.Fori(0, n) as k:
                        for u in range(2):
                            i = 2 * k + u
                            tile = dve.value_load(item_tile[0:1, bass.ds(i, 1)], min_val=0, max_val=T)
                            dve.wait_ge(gathered[u], PER * k + PER)
                            rows = Gt[:, u, :].rearrange("p (q w) -> p q w", q=Q)
                            dve.tensor_scalar(score[:, u, :], rows[:, :, D + 1], a2min, None,
                                              ALU.subtract).then_inc(s_score, 1)
                            dve.tensor_copy(local[:, u, :], item[:, u, :].rearrange("p (q w) -> p q w", w=2)[:, :, 1]
                                            ).then_inc(s_score, 1)
                            dve.wait_ge(s_score, 2 * i + 2)
                            for q in range(Q):
                                dve.tensor_scalar(V[:, u, q, :], iota_r[:, 0:R], local[:, u, q:q + 1], score[:, u, q:q + 1],
                                                  ALU.is_equal, ALU.mult).then_inc(s_v, 1)
                            dve.wait_ge(s_v, Q * i + Q)
                            dve.tensor_reduce(most[:, 0:R], V[:, u].rearrange("p q r -> p r q"), AX, ALU.max).then_inc(s_most, 1)
                            dve.wait_ge(s_mostT, i + 1)
                            m = SM * i

                            def small(j, ins):
                                ins.then_inc(s_small, 1)
                                dve.wait_ge(s_small, m + j)

                            at = bass.ds(tile, 1)
                            small(1, dve.tensor_reduce(new, bank[0][0:R, 0:128], AX, ALU.max))
                            small(2, dve.tensor_tensor(new, new, amax[:, at], ALU.max))
                            small(3, dve.tensor_scalar(base, own[:, at], a2min[0:R], None, ALU.add))
                            small(4, dve.tensor_tensor(zo, base, amax[:, at], ALU.add))
                            small(5, dve.tensor_tensor(zn, base, new, ALU.add))
                            small(6, dve.scalar_tensor_tensor(mn, zn, 0.01, zn, ALU.mult, ALU.max))
                            dve.scalar_tensor_tensor(mo, zo, 0.01, zo, ALU.mult, ALU.max).then_inc(s_small, 1)
                            dve.tensor_scalar(diag[:, 0, :], ident[0:R, 0:R], base, None, ALU.mult).then_inc(s_small, 1)
                            dve.tensor_scalar(diag[:, 1, :], ident[0:R, 0:R], mn, None, ALU.mult).then_inc(s_small, 1)
                            dve.wait_ge(s_small, m + 7)
                            small(10, dve.tensor_tensor(mo, mo, mn, ALU.subtract))
                            dve.wait_ge(s_rows, i + 1)
                            dve.tensor_tensor(Z, V[:, u], bank[1][:, 0:R].unsqueeze(1).to_broadcast([128, Q, R]),
                                              ALU.add).then_inc(s_z, 1)
                            dve.wait_ge(s_z, i + 1)
                            flat = Z.rearrange("p q r -> p (q r)")
                            dve.scalar_tensor_tensor(flat, flat, 0.01, flat, ALU.mult, ALU.max).then_inc(s_leaky, 1)
                            dve.wait_ge(s_leaky, i + 1)
                            dve.tensor_tensor(Z, Z, bank[1][:, R:2 * R].unsqueeze(1).to_broadcast([128, Q, R]),
                                              ALU.subtract).then_inc(s_zm, 1)
                            dve.wait_ge(s_exp, i + 1)
                            dve.scalar_tensor_tensor(V[:, u], V[:, u], 0.0, Z, ALU.is_gt, ALU.mult).then_inc(s_w, 1)
                            dve.tensor_copy(amax[:, at], new).then_inc(s_kept, 1)
                            dve.wait_ge(used[u], k + 2)
                            dve.wait_ge(s_fade, i + 1)
                            dve.wait_ge(agg_zero, 1)
                            dve.scalar_tensor_tensor(AGG[0:R, tile, 0:D + 1], AGG[0:R, tile, 0:D + 1], fade,
                                                     bank[2][0:R, 0:D + 1], ALU.mult, ALU.add).then_inc(s_agg, 1)

        with ExitStack() as _:
            b = Arena(big, 0, BIG_W)
            AGG = b.take(128, T + 1, TW)
            a = Arena(rest, rest_at, REST_W)
            stats2 = a.take(R, T, 6)
            after_stats = a.at
            W = a.take(128, DC, D)
            WT = a.take(128, DC, D)
            gb = a.take(1, D)
            sinv = a.take(R, T)
            An = a.take(R, 2, D + 1)
            AnT = a.take(128, 2, DC, R)
            flagT = a.take(1, 2, R)
            gw_in, gw_psum, gw_done = sem("gw_in"), sem("gw_psum"), sem("gw_done")
            g_inv, an_done, anT_psum, anT_done, g_psum, g_added, g_stats = (sem(n) for n in (
                "g_inv", "an_done", "anT_psum", "anT_done", "g_psum", "g_added", "g_stats"))
            with nc.Block() as block:
                @block.sync
                def _(sp):
                    sp.dma_start(W, gnn_W.rearrange("(c p) n -> p c n", p=128)).then_inc(gw_in, 16)
                    sp.dma_start(gb, row(gnn_b)).then_inc(gw_in, 16)

                @block.tensor
                def _(pe):
                    pe.wait_ge(gw_in, 32)
                    for o in range(DC):
                        for c in range(DC):
                            mm = pe.transpose(bank[0][:, (c * DC + o) * 128:(c * DC + o + 1) * 128],
                                              W[:, o, c * 128:(c + 1) * 128], ident)
                    mm.then_inc(gw_psum, 1)
                    pe.wait_ge(gw_done, 1)
                    with pe.Fori(0, T // 2) as k:
                        for u in range(2):
                            t = 2 * k + u
                            pe.wait_ge(an_done, t + 1)
                            pe.wait_ge(anT_done, 2 * k * 2 + 2 * u)
                            for c in range(DC):
                                pe.transpose(bank[1][:, c * R:(c + 1) * R], An[:, u, c * 128:(c + 1) * 128], ident[0:R, 0:R])
                            pe.transpose(bank[2][0:1, 0:R], An[:, u, D:D + 1], ident[0:R, 0:R]).then_inc(anT_psum, 1)
                            pe.wait_ge(anT_done, 2 * k * 2 + 2 * u + 2)
                            pe.wait_ge(g_added, t)
                            for c in range(DC):
                                pe.matmul(bank[3][0:R, 0:D], AnT[:, u, c, :], WT[:, c, :], start=c == 0, stop=False)
                            pe.matmul(bank[3][0:R, 0:D], flagT[:, u, :], gb, start=False, stop=True).then_inc(g_psum, 1)

                @block.scalar
                def _(act):
                    with act.Fori(0, T // 2) as k:
                        for u in range(2):
                            t = 2 * k + u
                            act.wait_ge(anT_psum, t + 1)
                            act.wait_ge(g_added, t)
                            act.copy(AnT[:, u].rearrange("p c r -> p (c r)"), bank[1][:, 0:DC * R]).then_inc(anT_done, 1)
                            act.copy(flagT[:, u], bank[2][0:1, 0:R]).then_inc(anT_done, 1)

                @block.vector
                def _(dve):
                    dve.tensor_scalar(sinv, AGG[0:R, 0:T, D], 1e-30, None, ALU.max).then_inc(g_inv, 1)
                    dve.wait_ge(g_inv, 1)
                    dve.reciprocal(sinv, sinv).then_inc(g_inv, 1)
                    dve.wait_ge(gw_psum, 1)
                    dve.tensor_copy(WT.rearrange("p c n -> p (c n)"), bank[0][:, :]).then_inc(gw_done, 1)
                    dve.wait_ge(g_inv, 2)
                    with dve.Fori(0, T // 2) as k:
                        for u in range(2):
                            t = 2 * k + u
                            dve.wait_ge(anT_psum, t)
                            dve.tensor_scalar(An[:, u, :], AGG[0:R, t, 0:D + 1], sinv[:, bass.ds(t, 1)], None,
                                              ALU.mult).then_inc(an_done, 1)
                            dve.wait_ge(g_psum, t + 1)
                            dve.tensor_tensor(X[:, t, :], X[:, t, :], bank[3][0:R, 0:D], ALU.add).then_inc(g_added, 1)
                            dve.wait_ge(g_added, t + 1)
                            dve.bn_stats(stats2[:, t, :], X[:, t, :]).then_inc(g_stats, 1)

        a = Arena(rest, after_stats, REST_W)
        M2 = a.take(128, IC, D)
        mean, rstd, shift = a.take(R, T), a.take(R, T), a.take(R, T)
        after_m2 = a.at
        SW = big[0:R, 0:T * INNER].rearrange("p (t n) -> p t n", t=T)
        with ExitStack() as _:
            var = a.take(R, T)
            WL = a.take(128, DC, INNER)
            bL = a.take(R, INNER)
            y, yT = a.take(R, 2, D + 1), a.take(128, 2, DC, R)
            L = a.take(R, 2, INNER)
            top, tot, inv = a.take(R, 2, FH), a.take(R, 2, FH), a.take(R, 2, FH)
            zero_row = a.take(1, 512)
            WxT = big[0:G, 0:FH * D].rearrange("p (h d) -> p h d", h=FH)
            Wx = big[:, 2048:2048 + DC * INNER].rearrange("p (c n) -> p c n", c=DC)
            Wsl = big[0:G, 3072:3072 + G]
            bx = big[0:G, 3136:3136 + FH]
            bsl = big[:, 3144:3144 + G]
            temp = big[:, 3208:3208 + FH]
            fw_in, fw_psum, fw_done, fs = sem("fw_in"), sem("fw_psum"), sem("fw_done"), sem("fs")
            sq_in, sq_done = sem("sq_in"), sem("sq_done")
            y_done, yT_psum, yT_done, l_psum, l_done = (sem(n) for n in ("y_done", "yT_psum", "yT_done", "l_psum", "l_done"))
            l_top, l_sub, l_exp, l_tot, l_inv, sw_done, sum_psum = (sem(n) for n in (
                "l_top", "l_sub", "l_exp", "l_tot", "l_inv", "sw_done", "sum_psum"))
            zeros, sw_kept = sem("zeros"), sem("sw_kept")
            with nc.Block() as block:
                @block.sync
                def _(sp):
                    with nc.allow_non_contiguous_dma(reason="columns of small vectors"):
                        sp.dma_start(Wx, W_x.rearrange("(c p) n -> p c n", p=128)).then_inc(fw_in, 16)
                        sp.dma_start(Wsl, W_slice).then_inc(fw_in, 16)
                        sp.dma_start(bx, b_x.rearrange("(h j) -> j h", h=FH)).then_inc(fw_in, 16)
                        sp.dma_start(bsl, row(b_slice).to_broadcast([128, G])).then_inc(fw_in, 16)
                        sp.dma_start(temp, temperature.rearrange("a h b c -> (a b c) h").to_broadcast([128, FH])
                                     ).then_inc(fw_in, 16)

                @block.tensor
                def _(pe):
                    pe.wait_ge(fw_in, 80)
                    for h in range(FH):
                        for c in range(DC):
                            i = h * DC + c
                            mm = pe.transpose(bank[i // 4][0:G, (i % 4) * 128:(i % 4 + 1) * 128],
                                              Wx[:, c, h * G:(h + 1) * G], ident)
                    mm.then_inc(fw_psum, 1)
                    pe.wait_ge(fw_done, 4)
                    for c in range(DC):
                        for h in range(FH):
                            pe.matmul(bank[4 + c][:, h * G:(h + 1) * G], WxT[:, h, c * 128:(c + 1) * 128], Wsl,
                                      start=True, stop=True)
                    for h in range(FH):
                        mm = pe.matmul(bank[6][:, h * G:(h + 1) * G], bx[:, h:h + 1].to_broadcast([G, 128]), Wsl,
                                       start=True, stop=True)
                    mm.then_inc(fw_psum, 1)
                    pe.wait_ge(zeros, 1)
                    pe.wait_ge(fw_done, 8)
                    for c in range(IC):
                        pe.matmul(bank[4 + c][:, 0:D + 1], zero_row[:, 0:128], zero_row[:, 0:D + 1], start=True,
                                  stop=False, skip_group_check=True)
                    with pe.Fori(0, T // 2) as k:
                        for u in range(2):
                            t = 2 * k + u
                            pe.wait_ge(y_done, t + 1)
                            pe.wait_ge(yT_done, t)
                            for c in range(DC):
                                mm = pe.transpose(bank[0][:, c * R:(c + 1) * R], y[:, u, c * 128:(c + 1) * 128],
                                                  ident[0:R, 0:R])
                            mm.then_inc(yT_psum, 1)
                            pe.wait_ge(yT_done, t + 1)
                            pe.wait_ge(l_done, t)
                            for c in range(DC):
                                mm = pe.matmul(bank[1][0:R, :], yT[:, u, c, :], WL[:, c, :], start=c == 0, stop=c == DC - 1)
                            mm.then_inc(l_psum, 1)
                            pe.wait_ge(sw_done, t + 1)
                            for c in range(IC):
                                mm = pe.matmul(bank[4 + c][:, 0:D + 1], L[:, u, c * 128:(c + 1) * 128], y[:, u, :],
                                               start=False, stop=False, skip_group_check=True)
                            mm.then_inc(sum_psum, 1)
                    for c in range(IC):
                        mm = pe.matmul(bank[4 + c][:, 0:D + 1], zero_row[:, 0:128], zero_row[:, 0:D + 1], start=False,
                                       stop=True, skip_group_check=True)
                    mm.then_inc(sum_psum, 1)
                    pe.wait_ge(sum_psum, T + 1)

                @block.scalar
                def _(act):
                    act.wait_ge(sq_in, 1)
                    act.activation(rstd, var, ACT.Sqrt).then_inc(sq_done, 1)
                    with act.Fori(0, T // 2) as k:
                        for u in range(2):
                            t = 2 * k + u
                            act.wait_ge(yT_psum, t + 1)
                            act.wait_ge(l_psum, t)
                            act.copy(yT[:, u].rearrange("p c r -> p (c r)"), bank[0][:, 0:DC * R]).then_inc(yT_done, 1)
                            act.wait_ge(l_sub, t + 1)
                            act.activation(L[:, u], L[:, u], ACT.Exp).then_inc(l_exp, 1)

                @block.gpsimd
                def _(pool):
                    pool.memset(zero_row, 0.0).then_inc(zeros, 1)
                    with pool.Fori(0, T // 2) as k:
                        for u in range(2):
                            t = 2 * k + u
                            pool.wait_ge(sw_done, t + 1)
                            pool.tensor_copy(SW[:, t, :], L[:, u]).then_inc(sw_kept, 1)

                @block.vector
                def _(dve):
                    n = [0]

                    def step(ins):
                        n[0] += 1
                        ins.then_inc(fs, 1)
                        dve.wait_ge(fs, n[0])

                    mo, me = stats2[:, :, 4], stats2[:, :, 1]
                    step(dve.tensor_tensor(mean, me, mo, ALU.add))
                    step(dve.tensor_tensor(shift, me, mo, ALU.subtract))
                    step(dve.tensor_scalar(mean, mean, 0.5, None, ALU.mult))
                    step(dve.tensor_tensor(shift, shift, shift, ALU.mult))
                    step(dve.tensor_tensor(var, stats2[:, :, 2], stats2[:, :, 5], ALU.add))
                    step(dve.tensor_scalar(var, var, 1.0 / D, LN_EPS, ALU.mult, ALU.add))
                    step(dve.scalar_tensor_tensor(var, shift, 0.25, var, ALU.mult, ALU.add))
                    dve.memset(y[:, :, D], 1.0).then_inc(sq_in, 1)
                    dve.wait_ge(sq_done, 1)
                    step(dve.reciprocal(rstd, rstd))
                    step(dve.tensor_tensor(shift, rstd, rstd, ALU.mult))
                    step(dve.tensor_tensor(shift, shift, var, ALU.mult))
                    step(dve.tensor_scalar(shift, shift, -0.5, 1.5, ALU.mult, ALU.add))
                    step(dve.tensor_tensor(rstd, rstd, shift, ALU.mult))
                    step(dve.scalar_tensor_tensor(shift, mean, -1.0, rstd, ALU.mult, ALU.mult))
                    dve.wait_ge(fw_in, 80)
                    step(dve.tensor_scalar(temp, temp, 0.1, 5.0, ALU.max, ALU.min))
                    step(dve.reciprocal(temp, temp))
                    dve.wait_ge(fw_psum, 1)
                    for i in range(4):
                        dve.tensor_copy(big[0:G, i * 512:(i + 1) * 512], bank[i][0:G, :]).then_inc(fw_done, 1)
                    dve.wait_ge(fw_psum, 2)

                    def heads(p):
                        return temp[0:p].unsqueeze(2).to_broadcast([p, FH, G])

                    def split(ap):
                        return ap.rearrange("p (h g) -> p h g", h=FH)

                    for c in range(DC):
                        dve.tensor_tensor(split(WL[:, c, :]), split(bank[4 + c][:, :]), heads(128), ALU.mult).then_inc(fw_done, 1)
                    dve.tensor_tensor(split(bL), split(bank[6][0:R, :]), bsl[0:R].unsqueeze(1).to_broadcast([R, FH, G]),
                                      ALU.add).then_inc(fw_done, 1)
                    dve.wait_ge(fw_done, 7)
                    dve.tensor_tensor(split(bL), split(bL), heads(R), ALU.mult).then_inc(fw_done, 1)
                    dve.wait_ge(fw_done, 8)
                    with dve.Fori(0, T // 2) as k:
                        for u in range(2):
                            t = 2 * k + u
                            dve.tensor_scalar(y[:, u, 0:D], X[:, t, :], rstd[:, bass.ds(t, 1)], shift[:, bass.ds(t, 1)],
                                              ALU.mult, ALU.add).then_inc(y_done, 1)
                            dve.wait_ge(l_psum, t + 1)
                            dve.wait_ge(sw_kept, t)
                            dve.tensor_tensor(L[:, u], bank[1][0:R, :], bL, ALU.add).then_inc(l_done, 1)
                            dve.wait_ge(l_done, t + 1)
                            dve.tensor_reduce(top[:, u], split(L[:, u]), AX, ALU.max).then_inc(l_top, 1)
                            dve.wait_ge(l_top, t + 1)
                            dve.tensor_tensor(split(L[:, u]), split(L[:, u]),
                                              top[:, u].unsqueeze(2).to_broadcast([R, FH, G]),
                                              ALU.subtract).then_inc(l_sub, 1)
                            dve.wait_ge(l_exp, t + 1)
                            dve.tensor_reduce(tot[:, u], split(L[:, u]), AX, ALU.add).then_inc(l_tot, 1)
                            dve.wait_ge(l_tot, t + 1)
                            dve.reciprocal(inv[:, u], tot[:, u]).then_inc(l_inv, 1)
                            dve.wait_ge(l_inv, t + 1)
                            dve.tensor_tensor(split(L[:, u]), split(L[:, u]),
                                              inv[:, u].unsqueeze(2).to_broadcast([R, FH, G]),
                                              ALU.mult).then_inc(sw_done, 1)

        with ExitStack() as _:
            a = Arena(rest, after_m2, REST_W)
            tok, tokT = a.take(128, IC, D + 1), a.take(128, DC, INNER)
            normT = a.take(1, INNER)
            den = a.take(128, IC)
            Wfx = a.take(128, DC, INNER)
            bfx = a.take(1, INNER)
            Wq, Wk, Wv = a.take(G, G), a.take(G, G), a.take(G, G)
            Wo = a.take(G, FH, D)
            sT, qT, kT, v = (a.take(G, INNER) for _ in range(4))
            P, PT = a.take(G, INNER), sT
            osT = qT
            ptop, ptot = a.take(G, FH), a.take(G, FH)
            aw_in, ap, ad, ae = sem("aw_in"), sem("attn_psum"), sem("attn_done"), sem("attn_exp")
            ae2 = sem("attn_parts")
            with nc.Block() as block:
                @block.sync
                def _(sp):
                    for to, of in ((Wfx, W_fx.rearrange("(c p) n -> p c n", p=128)), (bfx, row(b_fx)), (Wq, W_q), (Wk, W_k),
                                   (Wv, W_v), (Wo, W_out.rearrange("(h c) d -> c h d", h=FH))):
                        sp.dma_start(to, of).then_inc(aw_in, 16)

                def head(h, of=None):
                    return slice(h * G, (h + 1) * G)

                @block.tensor
                def _(pe):
                    pe.wait_ge(ad, 3)
                    for i in range(IC):
                        for c in range(DC):
                            pe.transpose(bank[c][:, i * 128:(i + 1) * 128], tok[:, i, c * 128:(c + 1) * 128], ident)
                        mm = pe.transpose(bank[2][0:1, i * 128:(i + 1) * 128], tok[:, i, D:D + 1], ident)
                    mm.then_inc(ap, 1)
                    pe.wait_ge(aw_in, 96)
                    pe.wait_ge(ad, 6)
                    for h in range(FH):
                        for c in range(DC):
                            pe.matmul(bank[3][0:G, head(h)], Wfx[:, c, head(h)], tokT[:, c, head(h)], start=c == 0, stop=False)
                        mm = pe.matmul(bank[3][0:G, head(h)], bfx[:, head(h)], normT[:, head(h)], start=False, stop=True)
                    mm.then_inc(ap, 1)
                    pe.wait_ge(ad, 7)
                    pe.matmul(bank[4][0:G, :], Wq, sT, start=True, stop=True)
                    pe.matmul(bank[5][0:G, :], Wk, sT, start=True, stop=True)
                    for h in range(FH):
                        mm = pe.matmul(bank[6][0:G, head(h)], sT[:, head(h)], Wv, start=True, stop=True)
                    mm.then_inc(ap, 1)
                    pe.wait_ge(ad, 10)
                    for h in range(FH):
                        mm = pe.matmul(bank[7][0:G, head(h)], qT[:, head(h)], kT[:, head(h)], start=True, stop=True)
                    mm.then_inc(ap, 1)
                    pe.wait_ge(ad, 15)
                    for h in range(FH):
                        mm = pe.transpose(bank[0][0:G, head(h)], P[:, head(h)], ident[0:G, 0:G])
                    mm.then_inc(ap, 1)
                    pe.wait_ge(ad, 16)
                    for h in range(FH):
                        mm = pe.matmul(bank[1][0:G, head(h)], v[:, head(h)], PT[:, head(h)], start=True, stop=True)
                    mm.then_inc(ap, 1)
                    pe.wait_ge(ad, 17)
                    for h in range(FH):
                        lo = (h % 2) * G
                        mm = pe.matmul(bank[2 + h // 2][lo:lo + G, 0:D], osT[:, head(h)], Wo[:, h, :], start=True, stop=True)
                    mm.then_inc(ap, 1)
                    pe.wait_ge(ap, 7)

                @block.scalar
                def _(act):
                    act.wait_ge(ad, 12)
                    act.activation(P, P, ACT.Exp, scale=SLICE_SCALE).then_inc(ae, 1)

                @block.vector
                def _(dve):
                    n = [0]

                    def step(ins):
                        n[0] += 1
                        ins.then_inc(ad, 1)
                        dve.wait_ge(ad, n[0])

                    def split(ap_):
                        return ap_.rearrange("p (h g) -> p h g", h=FH)

                    for i in range(IC):
                        ins = dve.tensor_scalar(den[:, i:i + 1], bank[4 + i][:, D:D + 1], EPS, None, ALU.add)
                        if i < IC - 1:
                            ins.then_inc(ae2, 1)
                    step(ins)
                    dve.wait_ge(ae2, IC - 1)
                    step(dve.reciprocal(den, den))
                    for i in range(IC):
                        ins = dve.tensor_scalar(tok[:, i, :], bank[4 + i][:, 0:D + 1], den[:, i:i + 1], None, ALU.mult)
                        if i < IC - 1:
                            ins.then_inc(ae2, 1)
                    step(ins)
                    dve.wait_ge(ap, 1)
                    step(dve.tensor_copy(tokT[:, 0, :], bank[0][:, :]))
                    step(dve.tensor_copy(tokT[:, 1, :], bank[1][:, :]))
                    step(dve.tensor_copy(normT, bank[2][0:1, :]))
                    dve.wait_ge(ap, 2)
                    step(dve.tensor_copy(sT, bank[3][0:G, :]))
                    dve.wait_ge(ap, 3)
                    step(dve.tensor_copy(qT, bank[4][0:G, :]))
                    step(dve.tensor_copy(kT, bank[5][0:G, :]))
                    step(dve.tensor_copy(v, bank[6][0:G, :]))
                    dve.wait_ge(ap, 4)
                    step(dve.tensor_reduce(ptop, split(bank[7][0:G, :]), AX, ALU.max))
                    step(dve.tensor_tensor(split(P), split(bank[7][0:G, :]), ptop.unsqueeze(2).to_broadcast([G, FH, G]),
                                           ALU.subtract))
                    dve.wait_ge(ae, 1)
                    step(dve.tensor_reduce(ptot, split(P), AX, ALU.add))
                    step(dve.reciprocal(ptot, ptot))
                    step(dve.tensor_tensor(split(P), split(P), ptot.unsqueeze(2).to_broadcast([G, FH, G]), ALU.mult))
                    dve.wait_ge(ap, 5)
                    step(dve.tensor_copy(PT, bank[0][0:G, :]))
                    dve.wait_ge(ap, 6)
                    step(dve.tensor_copy(osT, bank[1][0:G, :]))
                    dve.wait_ge(ap, 7)
                    for i in range(IC):
                        step(dve.tensor_copy(M2[:, i, :], bank[2 + i][:, 0:D]))

        with ExitStack() as _:
            a = Arena(rest, after_m2, REST_W)
            bout = a.take(R, D)
            sw_in = a.take(R, 2, INNER)
            swT = a.take(128, 2, IC, R)
            res = a.take(R, 2, D)
            bo_in, sw_here, swT_psum, swT_done, o_psum, o_sum, o_done = (sem(n) for n in (
                "bo_in", "sw_here", "swT_psum", "swT_done", "o_psum", "o_sum", "o_done"))
            o_out = [sem("o_out0"), sem("o_out1")]
            with nc.Block() as block:
                @block.sync
                def _(sp):
                    sp.dma_start(bout, row(b_out).to_broadcast([R, D])).then_inc(bo_in, 16)
                    with sp.Fori(0, T // 2) as k:
                        for u in range(2):
                            t = 2 * k + u
                            sp.wait_ge(o_done, t + 1)
                            sp.dma_start(out[bass.ds(t * R, R), :], res[:, u]).then_inc(o_out[u], 16)
                    for u in range(2):
                        sp.wait_ge(o_out[u], 16 * (T // 2))

                @block.gpsimd
                def _(pool):
                    with pool.Fori(0, T // 2) as k:
                        for u in range(2):
                            t = 2 * k + u
                            pool.wait_ge(swT_psum, 2 * k + (u - 1) if u else 2 * k)
                            pool.tensor_copy(sw_in[:, u], SW[:, t, :]).then_inc(sw_here, 1)

                @block.tensor
                def _(pe):
                    with pe.Fori(0, T // 2) as k:
                        for u in range(2):
                            t = 2 * k + u
                            pe.wait_ge(sw_here, t + 1)
                            pe.wait_ge(swT_done, 2 * k + u)
                            for c in range(IC):
                                mm = pe.transpose(bank[u][:, c * R:(c + 1) * R], sw_in[:, u, c * 128:(c + 1) * 128],
                                                  ident[0:R, 0:R])
                            mm.then_inc(swT_psum, 1)
                            pe.wait_ge(swT_done, t + 1)
                            pe.wait_ge(o_sum, t)
                            for c in range(IC):
                                mm = pe.matmul(bank[2 + u][0:R, 0:D], swT[:, u, c, :], M2[:, c, :], start=c == 0,
                                               stop=c == IC - 1)
                            mm.then_inc(o_psum, 1)

                @block.scalar
                def _(act):
                    with act.Fori(0, T // 2) as k:
                        for u in range(2):
                            t = 2 * k + u
                            act.wait_ge(swT_psum, t + 1)
                            act.wait_ge(o_psum, t)
                            act.copy(swT[:, u].rearrange("p c r -> p (c r)"), bank[u][:, 0:IC * R]).then_inc(swT_done, 1)

                @block.vector
                def _(dve):
                    dve.wait_ge(bo_in, 16)
                    with dve.Fori(0, T // 2) as k:
                        for u in range(2):
                            t = 2 * k + u
                            dve.wait_ge(o_out[u], 16 * k)
                            dve.wait_ge(o_psum, t + 1)
                            dve.tensor_tensor(res[:, u], X[:, t, :], bank[2 + u][0:R, 0:D], ALU.add).then_inc(o_sum, 1)
                            dve.wait_ge(o_sum, t + 1)
                            dve.tensor_tensor(res[:, u], res[:, u], bout, ALU.add).then_inc(o_done, 1)


_INS = ["x", "src", "dst", "L0_gnn_W_layer", "L0_gnn_b_layer", "L0_gnn_w_a1", "L0_gnn_b_a1", "L0_gnn_w_a2",
        "L0_gnn_b_a2", "L0_mix_wq", "L0_mix_bq", "L0_mix_wk", "L0_mix_bk", "L0_mix_wv", "L0_mix_bv", "L0_mix_wo",
        "L0_mix_bo", "L0_ffn_W_fx", "L0_ffn_b_fx", "L0_ffn_W_x", "L0_ffn_b_x", "L0_ffn_W_slice", "L0_ffn_b_slice",
        "L0_ffn_W_q", "L0_ffn_W_k", "L0_ffn_W_v", "L0_ffn_W_out", "L0_ffn_b_out", "L0_ffn_temperature"]


def kernel(**inputs):
    import numpy as _np
    import concourse.bacc as _bacc
    from concourse import mybir as _mybir
    from concourse.bass_utils import run_bass_kernel_spmd as _run

    nc = _bacc.Bacc("TRN2", target_bir_lowering=False, num_devices=1)
    arrays, args = {}, []
    for name in _INS:
        a = _np.ascontiguousarray(inputs[name])
        arrays[f"in_{name}_dram"] = a
        args.append(nc.dram_tensor(f"in_{name}_dram", a.shape, _mybir.dt.from_np(a.dtype), kind="ExternalInput").ap())
    result = nc.dram_tensor("out_dram", (N, D), F32, kind="ExternalOutput").ap()
    bass_gps(nc, *args, result)
    r = _run(nc, [arrays], core_ids=[0])
    return r.results[0]["out_dram"]
```

```python
from contextlib import ExitStack

import concourse.bass as bass
from concourse import mybir

F32 = mybir.dt.float32
I32 = mybir.dt.int32
BF16 = mybir.dt.bfloat16
U8 = mybir.dt.uint8
ALU = mybir.AluOpType
ACT = mybir.ActivationFunctionType
AX = mybir.AxisListType.X

N = 6250
D = 256
E = 100000
R = 125
T = N // R
DC = D // 128
EP = 125
EJ = E // EP
TW = D + 2
Q = 17
CH = Q * 128
ITEMS = T + E // CH + 1
U = 3
ITEMS += -ITEMS % U
MIN_ROUNDS = -(-T // U)
NOBODY = 200
SB = 20
HEADS = 8
HD = D // HEADS
FH = 8
G = 64
INNER = FH * G
IC = INNER // 128
EPS = 1e-5
LN_EPS = 1e-5
NORM_EPS = 1e-6
SLICE_SCALE = G ** -0.5


class Arena:

    def __init__(self, tensor, start, end):
        self.tensor, self.at, self.end = tensor, start, end

    def take(self, partitions, *shape, dtype=F32):
        n = 1
        for s in shape:
            n *= s
        words = n if dtype in (F32, I32) else (n + 1) // 2 if dtype == BF16 else (n + 3) // 4
        assert self.at + words <= self.end, (self.at, words, self.end)
        ap = self.tensor[0:partitions, self.at:self.at + words]
        self.at += words
        if dtype != F32:
            ap = ap.bitcast(dtype)
        if len(shape) == 2:
            ap = ap.rearrange("p (a b) -> p a b", a=shape[0])
        if len(shape) == 3:
            ap = ap.rearrange("p (a b c) -> p a b c", a=shape[0], b=shape[1])
        return ap


def bass_gps(nc, x, src, dst, gnn_W, gnn_b, gnn_wa1, gnn_ba1, gnn_wa2, gnn_ba2,
             mix_wq, mix_bq, mix_wk, mix_bk, mix_wv, mix_bv, mix_wo, mix_bo,
             W_fx, b_fx, W_x, b_x, W_slice, b_slice, W_q, W_k, W_v, W_out, b_out, temperature, out):
    ctx = ExitStack()
    with ctx:
        def sem(name):
            return ctx.enter_context(nc.semaphore(name))

        def row(v):
            return v.rearrange("(a d) -> a d", a=1)

        bank = [ctx.enter_context(nc.psum_tensor(f"bank{i}", [128, 512], F32)) for i in range(8)]
        X = ctx.enter_context(nc.sbuf_tensor("X", [R, T, D], F32))
        BIG_W = T * INNER
        REST_W = 14400
        big = ctx.enter_context(nc.sbuf_tensor("big", [128, BIG_W], F32))
        rest = ctx.enter_context(nc.sbuf_tensor("rest", [128, REST_W], F32))

        table = nc.dram_tensor("node_table", [N, TW], F32, kind="Internal").ap()
        slots = nc.dram_tensor("edge_slots", [(ITEMS) * CH, 2], I32, kind="Internal").ap()

        keep = Arena(rest, 0, REST_W)
        ident = keep.take(128, 128)
        ones = keep.take(128, 128)
        iota_r = keep.take(128, 128)
        A12 = keep.take(R, T, 2)
        item_tile = keep.take(1, ITEMS + 1, dtype=I32)
        is_last = keep.take(R, ITEMS + 1)
        is_same = keep.take(R, ITEMS)
        rounds = keep.take(1, 1, dtype=I32)
        WT = keep.take(128, DC, D)
        gb_row = keep.take(1, D)
        a2min = keep.take(128, 1)
        eps = keep.take(128, 1)
        rest_at = keep.at

        with ExitStack() as _:
            a = Arena(rest, rest_at, REST_W)
            payload = a.take(EP, EJ, 2, dtype=I32)
            place = a.take(EP, EJ, dtype=I32)
            after_rank = a.at
            before = a.take(128, 128)
            iota_i = a.take(128, 128, dtype=I32)
            counts = a.take(EP, T)
            first = a.take(EP, T)
            total = a.take(EP, T)
            chunks = a.take(EP, T)
            begun = a.take(EP, T)
            fullness = a.take(EP, T, ITEMS - T)
            item_row = a.take(EP, ITEMS)
            in_use = a.take(1, ITEMS // U)
            scal = a.take(1, 4)
            iota2 = a.take(128, ITEMS)
            iota2_i = a.take(128, ITEMS, dtype=I32)
            b = Arena(big, 0, BIG_W)
            masks = b.take(EP, 2, EJ, dtype=U8)
            is_tile = b.take(EP, 2, EJ, dtype=U8)
            pick = b.take(EP, 2, EJ)
            srci = b.take(EP, EJ, dtype=I32)
            dsti = b.take(EP, EJ, dtype=I32)
            srcf = b.take(EP, EJ)
            tile_i = b.take(EP, EJ, dtype=I32)
            tile_f = b.take(EP, EJ)
            scanned = b.take(EP, 2, EJ)
            placef = b.take(EP, EJ)
            one_row = b.take(EP, EJ)
            cmp = b.take(EP, ITEMS, T)
            empty = b.take(128, Q, 2, dtype=I32)

            edges_in, x_in, slots_empty = sem("edges_in"), sem("x_in"), sem("slots_empty")
            pool_made, empty_made = sem("pool_made"), sem("empty_made")
            rk = sem("rank_step")
            counted, prefixed, flags = sem("counted"), sem("prefixed"), sem("flags")
            masked, scanned_s, picked, pick_free = sem("masked"), sem("scanned"), sem("picked"), sem("pick_free")

            with nc.Block() as block:
                @block.sync
                def _(sp):
                    sp.dma_start(srci, src.rearrange("(p j) -> p j", p=EP)).then_inc(edges_in, 16)
                    sp.dma_start(dsti, dst.rearrange("(p j) -> p j", p=EP)).then_inc(edges_in, 16)
                    xv = x.rearrange("(t p) d -> p t d", p=R)
                    for lo, hi in ((0, 112), (112, R)):
                        sp.dma_start(X[lo:hi], xv[lo:hi]).then_inc(x_in, 16)
                    sp.wait_ge(empty_made, 2)
                    sp.dma_start(slots.rearrange("(c p q) w -> p c (q w)", p=128, q=Q),
                                 empty.rearrange("p q w -> p (q w)").unsqueeze(1).to_broadcast([128, ITEMS, Q * 2])
                                 ).then_inc(slots_empty, 16)
                    sp.wait_ge(x_in, 32)
                    sp.wait_ge(slots_empty, 16)

                @block.gpsimd
                def _(pool):
                    pool.iota(iota_i, [[1, 128]], base=0, channel_multiplier=0).then_inc(pool_made, 1)
                    pool.iota(iota2_i, [[1, ITEMS]], base=0, channel_multiplier=0).then_inc(pool_made, 1)
                    pool.memset(ident, 0.0).then_inc(pool_made, 1)
                    pool.memset(before, 1.0).then_inc(pool_made, 1)
                    pool.memset(ones, 1.0).then_inc(pool_made, 1)
                    pool.wait_ge(pool_made, 5)
                    pool.affine_select(out=ident, in_=ident, compare_op=ALU.not_equal, fill=1.0, base=0,
                                       pattern=[[-1, 128]], channel_multiplier=1).then_inc(pool_made, 1)
                    pool.affine_select(out=before, in_=before, compare_op=ALU.is_gt, fill=0.0, base=0,
                                       pattern=[[1, 128]], channel_multiplier=-1).then_inc(pool_made, 1)
                    pool.memset(empty[:, :, 0], 0).then_inc(empty_made, 1)
                    pool.memset(empty[:, :, 1], NOBODY).then_inc(empty_made, 1)
                    pool.memset(placef, 0.0).then_inc(pick_free, 2)
                    with pool.Fori(0, T // 2) as k:
                        for half in range(2):
                            pool.wait_ge(picked, 2 * k + (half + 1))
                            pool.wait_ge(pick_free, 2 * k + (half + 2))
                            pool.tensor_tensor(placef, placef, pick[:, half], ALU.add).then_inc(pick_free, 1)

                @block.tensor
                def _(pe):
                    pe.wait_ge(pool_made, 7)
                    pe.wait_ge(counted, 2 + T)
                    pe.matmul(bank[0][0:EP, 0:T], before[0:EP, 0:EP], counts, start=True, stop=True)
                    pe.matmul(bank[1][0:EP, 0:T], ones[0:EP, 0:EP], counts, start=True, stop=True).then_inc(prefixed, 1)

                @block.vector
                def _(dve):
                    n = [0]

                    def step(ins):
                        n[0] += 1
                        ins.then_inc(rk, 1)
                        dve.wait_ge(rk, n[0])

                    dve.wait_ge(pool_made, 5)
                    step(dve.tensor_copy(iota_r, iota_i))
                    step(dve.tensor_copy(iota2, iota2_i))
                    dve.memset(one_row, 1.0).then_inc(counted, 1)
                    dve.memset(eps, EPS).then_inc(counted, 1)
                    dve.wait_ge(edges_in, 32)
                    step(dve.tensor_copy(srcf, srci))
                    step(dve.tensor_scalar(tile_i, srcf, 1.0 / R, 0.5 / R - 0.5, ALU.mult, ALU.add))
                    step(dve.tensor_copy(tile_f, tile_i))
                    step(dve.scalar_tensor_tensor(payload[:, :, 1], tile_f, -float(R), srcf, ALU.mult, ALU.add))
                    step(dve.tensor_copy(payload[:, :, 0], dsti))
                    with dve.Fori(0, T // 2) as k:
                        for half in range(2):
                            t = 2 * k + half
                            dve.wait_ge(counted, t + 1)
                            dve.tensor_scalar(is_tile[:, half, :], tile_f, iota_r[0:EP, bass.ds(t, 1)], 0.0,
                                              ALU.is_equal, ALU.add, accum_out=counts[:, bass.ds(t, 1)]
                                              ).then_inc(counted, 1)
                    dve.wait_ge(prefixed, 1)
                    step(dve.tensor_copy(first, bank[0][0:EP, 0:T]))
                    step(dve.tensor_copy(total, bank[1][0:EP, 0:T]))
                    step(dve.tensor_scalar(iota2[:, 0:ITEMS - T], iota2[:, 0:ITEMS - T], float(CH), None, ALU.mult))
                    step(dve.tensor_tensor(fullness, total.unsqueeze(2).to_broadcast([EP, T, ITEMS - T]),
                                           iota2[0:EP, 0:ITEMS - T].unsqueeze(1).to_broadcast([EP, T, ITEMS - T]),
                                           ALU.is_gt))
                    step(dve.tensor_reduce(chunks, fullness, AX, ALU.add))
                    step(dve.tensor_scalar(chunks, chunks, 1.0, None, ALU.max))
                    step(dve.tensor_tensor_scan(begun, one_row[:, 0:T], chunks, 0.0, ALU.mult, ALU.add))
                    step(dve.tensor_tensor(total, begun, chunks, ALU.subtract))
                    step(dve.tensor_scalar(total, total, float(CH), -1.0, ALU.mult, ALU.add))
                    step(dve.tensor_tensor(first, first, total, ALU.add))
                    step(dve.tensor_copy(iota2, iota2_i))
                    step(dve.tensor_tensor(cmp, begun.unsqueeze(1).to_broadcast([EP, ITEMS, T]),
                                           iota2[0:EP].unsqueeze(2).to_broadcast([EP, ITEMS, T]), ALU.is_le))
                    step(dve.tensor_reduce(item_row, cmp, AX, ALU.add))
                    dve.memset(is_same[:, 0:1], 0.0).then_inc(flags, 1)
                    dve.memset(is_last[:, 0:1], 0.0).then_inc(flags, 1)
                    dve.memset(item_tile[:, 0:1], 0).then_inc(flags, 1)
                    dve.tensor_tensor(is_same[:, 1:ITEMS], item_row[:, 1:ITEMS], item_row[:, 0:ITEMS - 1],
                                      ALU.is_equal).then_inc(flags, 1)
                    dve.tensor_tensor(is_last[:, 1:ITEMS], item_row[:, 0:ITEMS - 1], item_row[:, 1:ITEMS],
                                      ALU.is_lt).then_inc(flags, 1)
                    dve.tensor_scalar(is_last[:, ITEMS:ITEMS + 1], item_row[:, ITEMS - 1:ITEMS], float(T), None,
                                      ALU.is_lt).then_inc(flags, 1)
                    dve.tensor_scalar(item_tile[:, 1:ITEMS + 1], item_row[0:1], float(T - 1), None,
                                      ALU.min).then_inc(flags, 1)
                    ev = ITEMS // U
                    step(dve.tensor_scalar(in_use, iota2[0:1, 0:ev], float(U), None, ALU.mult))
                    step(dve.tensor_scalar(in_use, in_use, begun[0:1, T - 1:T], None, ALU.is_lt))
                    step(dve.tensor_reduce(scal[:, 0:1], in_use, AX, ALU.add))
                    step(dve.tensor_scalar(rounds, scal[:, 0:1], -1.0, None, ALU.add))
                    with dve.Fori(0, T // 2) as k:
                        t = 2 * k
                        for half in range(2):
                            mask, run = masks[:, half, :], scanned[:, half]
                            dve.wait_ge(picked, t + half)
                            dve.tensor_scalar(mask, tile_f, iota_r[0:EP, bass.ds(t + half, 1)], None,
                                              ALU.is_equal).then_inc(masked, 1)
                            dve.wait_ge(masked, t + (half + 1))
                            dve.tensor_tensor_scan(run, one_row, mask, first[:, bass.ds(t + half, 1)],
                                                   ALU.mult, ALU.add).then_inc(scanned_s, 1)
                            dve.wait_ge(scanned_s, t + (half + 1))
                            dve.wait_ge(pick_free, t + (half + 1))
                            dve.tensor_tensor(pick[:, half], mask, run, ALU.mult).then_inc(picked, 1)
                    dve.wait_ge(pick_free, T + 2)
                    step(dve.tensor_copy(place, placef))

        with ExitStack() as _:
            a = Arena(rest, after_rank, REST_W)
            same_head = a.take(128, 128)
            slot_buf = a.take(EP, 2, SB, dtype=I32)
            edge_buf = a.take(EP, 2, SB, 2, dtype=I32)
            stats = a.take(R, T, 6)
            mean, var, rstd, shift = a.take(R, T), a.take(R, T), a.take(R, T), a.take(R, T)
            xn = a.take(R, TW)
            xnT = a.take(128, DC, R)
            kb, km, ks = a.take(R, D), a.take(R, D), a.take(R, D)
            qm, qr = a.take(128, DC, R), a.take(128, DC, R)
            qn = a.take(128, DC, R)
            zero_row = a.take(1, 512)
            mins = a.take(128, 4)
            b = Arena(big, 0, BIG_W)
            QT = b.take(128, DC, N)
            wq, wk, wv, wo = (b.take(128, DC, D) for _ in range(4))
            W = b.take(128, DC, D)
            wa = b.take(128, DC, 2)
            va = b.take(128, DC, 2)
            bq, gb = b.take(128, DC), b.take(128, DC)
            ba, ca = b.take(128, 2), b.take(128, 2)
            bk = b.take(R, D)
            bv, bo = b.take(1, D), b.take(1, D)
            kx = b.take(128, DC, D + 1)
            kxT = b.take(128, DC, D)
            ksum = b.take(1, D)
            kvT = b.take(128, DC, 128)
            M = b.take(128, DC, D)
            B = b.take(128, DC, 128)

            weights_in, mix_made, ra = sem("weights_in"), sem("mix_made"), sem("dve_setup_step")
            copied, scattered = [sem("copied0"), sem("copied1")], [sem("scattered0"), sem("scattered1")]
            va_psum, va_done, stats_done, std_done = sem("va_psum"), sem("va_done"), sem("stats_done"), sem("std_done")
            xn_done, xnT_psum, xnT_done = sem("xn_done"), sem("xnT_psum"), sem("xnT_done")
            av_psum, av_done, table_out = sem("av_psum"), sem("av_done"), sem("table_out")
            k_psum, kb_done, km_done, ke_done, ks_done = (sem(n) for n in ("k_psum", "kb_done", "km_done", "ke_done", "ks_done"))
            q_psum, qm_done, qe_done, q_done = (sem(n) for n in ("q_psum", "qm_done", "qe_done", "q_done"))
            kx_psum = sem("kx_psum")
            head_psum, head_done = sem("head_psum"), sem("head_done")
            norm_psum, norm_eps, norm_inv, qn_done = (sem(n) for n in ("norm_psum", "norm_eps", "norm_inv", "qn_done"))
            mix_psum, mixed = sem("mix_psum"), sem("mixed")

            with nc.Block() as block:
                @block.sync
                def _(sp):
                    def chunked(w):
                        return w.rearrange("(c p) n -> p c n", p=128)

                    def column(v):
                        return v.rearrange("(c p) -> p c", p=128)

                    loads = [(wq, chunked(mix_wq)), (wk, chunked(mix_wk)), (wv, chunked(mix_wv)), (wo, chunked(mix_wo)),
                             (W, chunked(gnn_W)), (wa[:, :, 0], column(gnn_wa1.rearrange("a d -> (a d)"))),
                             (wa[:, :, 1], column(gnn_wa2.rearrange("a d -> (a d)"))), (bq, column(mix_bq)),
                             (gb, column(gnn_b)), (ba[:, 0:1], row(gnn_ba1).to_broadcast([128, 1])),
                             (ba[:, 1:2], row(gnn_ba2).to_broadcast([128, 1])),
                             (gb_row, row(gnn_b)), (bk, row(mix_bk).to_broadcast([R, D])), (bv, row(mix_bv)), (bo, row(mix_bo))]
                    with nc.allow_non_contiguous_dma(reason="columns of small vectors"):
                        for to, of in loads:
                            sp.dma_start(to, of).then_inc(weights_in, 16)
                    assert len(loads) == 15
                    with sp.Fori(0, T) as t:
                        sp.wait_ge(av_done, 2 * t + 2)
                        sp.dma_start(table[bass.ds(t * R, R), :], xn).then_inc(table_out, 16)
                    sp.wait_ge(table_out, 16 * T)

                @block.gpsimd
                def _(pool):
                    pool.memset(zero_row, 0.0).then_inc(mix_made, 1)
                    pool.memset(same_head, 0.0).then_inc(mix_made, 1)
                    pool.wait_ge(mix_made, 2)
                    for h in range(128 // HD):
                        pool.memset(same_head[h * HD:(h + 1) * HD, h * HD:(h + 1) * HD], 1.0).then_inc(mix_made, 1)
                    pool.wait_ge(mix_made, 2 + 128 // HD)
                    with pool.Fori(0, EJ // (2 * SB)) as k:
                        for u in range(2):
                            at = (2 * k + u) * SB
                            pool.wait_ge(scattered[u], 16 * SB * k)
                            pool.tensor_copy(slot_buf[:, u], place[:, bass.ds(at, SB)]).then_inc(copied[u], 1)
                            pool.tensor_copy(edge_buf[:, u], payload[:, bass.ds(at, SB), :]).then_inc(copied[u], 1)
                            pool.wait_ge(copied[u], 2)
                            pool.sem_clear(copied[u])
                            for j in range(SB):
                                pool.indirect_dma_start(
                                    slots, bass.IndirectOffsetOnAxis(ap=slot_buf[:, u, j:j + 1], axis=0),
                                    edge_buf[:, u, j, :], None).then_inc(scattered[u], 16)
                    for u in range(2):
                        pool.wait_ge(scattered[u], 16 * EJ // 2)

                @block.tensor
                def _(pe):
                    pe.wait_ge(weights_in, 16 * 15)
                    for c in range(DC):
                        for o in range(DC):
                            pe.matmul(bank[0][:, 2 * c:2 * c + 2], W[:, o, c * 128:(c + 1) * 128], wa[:, o, :],
                                      start=o == 0, stop=o == DC - 1)
                    for o in range(DC):
                        mm = pe.matmul(bank[0][:, 8:10], gb[:, o:o + 1].to_broadcast([128, 128]), wa[:, o, :],
                                       start=o == 0, stop=o == DC - 1)
                    mm.then_inc(va_psum, 1)
                    for o in range(DC):
                        for c in range(DC):
                            mm = pe.transpose(bank[1][:, (c * DC + o) * 128:(c * DC + o + 1) * 128],
                                              W[:, o, c * 128:(c + 1) * 128], ident)
                    mm.then_inc(va_psum, 1)
                    pe.wait_ge(mix_made, 2)
                    for c in range(DC):
                        pe.matmul(bank[6 + c][:, 0:D + 1], zero_row[:, 0:128], zero_row[:, 0:D + 1], start=True,
                                  stop=False, skip_group_check=True)
                    pe.wait_ge(va_done, 3)
                    with pe.Fori(0, T) as t:
                        pe.wait_ge(xn_done, t + 1)
                        pe.wait_ge(xnT_done, t)
                        for c in range(DC):
                            mm = pe.transpose(bank[0][:, c * R:(c + 1) * R], xn[:, c * 128:(c + 1) * 128],
                                              ident[0:R, 0:R])
                        mm.then_inc(xnT_psum, 1)
                        pe.wait_ge(xnT_done, t + 1)
                        pe.wait_ge(av_done, 2 * t)
                        for c in range(DC):
                            mm = pe.matmul(bank[1][0:R, 0:2], xnT[:, c, :], va[:, c, :], start=c == 0, stop=c == DC - 1)
                        mm.then_inc(av_psum, 1)
                        pe.wait_ge(kb_done, t)
                        for c in range(DC):
                            mm = pe.matmul(bank[2][0:R, 0:D], xnT[:, c, :], wk[:, c, :], start=c == 0, stop=c == DC - 1)
                        mm.then_inc(k_psum, 1)
                        pe.wait_ge(qm_done, 2 * t)
                        pe.wait_ge(qe_done, 3 * t)
                        for i in range(DC):
                            for c in range(DC):
                                mm = pe.matmul(bank[3][:, i * R:(i + 1) * R], wq[:, c, i * 128:(i + 1) * 128],
                                               xnT[:, c, :], start=c == 0, stop=c == DC - 1)
                        mm.then_inc(q_psum, 1)
                        pe.wait_ge(ks_done, t + 1)
                        for c in range(DC):
                            mm = pe.matmul(bank[6 + c][:, 0:D + 1], ks[:, c * 128:(c + 1) * 128], xn[:, 0:D + 1],
                                           start=False, stop=False, skip_group_check=True)
                        mm.then_inc(kx_psum, 1)
                    for c in range(DC):
                        mm = pe.matmul(bank[6 + c][:, 0:D + 1], zero_row[:, 0:128], zero_row[:, 0:D + 1], start=False,
                                       stop=True, skip_group_check=True)
                    mm.then_inc(head_psum, 1)
                    pe.wait_ge(head_done, 2)
                    for i in range(DC):
                        for c in range(DC):
                            pe.transpose(bank[0][:, (c * DC + i) * 128:(c * DC + i + 1) * 128],
                                         kx[:, i, c * 128:(c + 1) * 128], ident)
                        mm = pe.transpose(bank[1][0:1, i * 128:(i + 1) * 128], kx[:, i, D:D + 1], ident)
                    mm.then_inc(head_psum, 1)
                    pe.wait_ge(head_done, 4)
                    for c in range(DC):
                        o = bank[2][:, c * 128:(c + 1) * 128]
                        for d in range(DC):
                            pe.matmul(o, wv[:, d, c * 128:(c + 1) * 128], kxT[:, d, c * 128:(c + 1) * 128],
                                      start=d == 0, stop=False)
                        mm = pe.matmul(o, bv[:, c * 128:(c + 1) * 128], ksum[:, c * 128:(c + 1) * 128],
                                       start=False, stop=True)
                    mm.then_inc(head_psum, 1)
                    pe.wait_ge(head_done, 8)
                    for c in range(DC):
                        mm = pe.matmul(bank[3][:, c * D:(c + 1) * D], kvT[:, c, :], wo[:, c, :], start=True, stop=True)
                    mm.then_inc(head_psum, 1)
                    pe.wait_ge(head_done, 9)
                    with pe.Fori(0, T) as t:
                        pe.wait_ge(norm_eps, t)
                        for c in range(DC):
                            mm = pe.matmul(bank[0][:, c * R:(c + 1) * R], B[:, c, :], QT[:, c, bass.ds(t * R, R)],
                                           start=True, stop=True)
                        mm.then_inc(norm_psum, 1)
                        pe.wait_ge(mixed, t)
                        pe.wait_ge(qn_done, t + 1)
                        for c in range(DC):
                            pe.matmul(bank[1][0:R, 0:D], qn[:, c, :], M[:, c, :], start=c == 0, stop=False)
                        pe.matmul(bank[1][0:R, 0:D], ones[0:1, 0:R], bo, start=False, stop=True).then_inc(mix_psum, 1)
                    pe.wait_ge(head_done, 10)
                    pe.transpose(bank[2][0:1, 0:R], mins[0:R, 0:1], ident[0:R, 0:R]).then_inc(head_psum, 1)
                    pe.wait_ge(head_done, 11)
                    pe.matmul(bank[3][:, 0:1], ones[0:1, :], mins[0:1, 1:2], start=True, stop=True).then_inc(head_psum, 1)

                @block.scalar
                def _(act):
                    act.wait_ge(stats_done, 1)
                    act.activation(rstd, var, ACT.Sqrt).then_inc(std_done, 1)
                    with act.Fori(0, T) as t:
                        act.wait_ge(xnT_psum, t + 1)
                        act.wait_ge(q_psum, t)
                        act.copy(xnT.rearrange("p c r -> p (c r)"), bank[0][:, 0:DC * R]).then_inc(xnT_done, 1)
                        act.wait_ge(km_done, t + 1)
                        act.activation(km, km, ACT.Exp).then_inc(ke_done, 1)
                        act.wait_ge(q_done, t)
                        act.wait_ge(qm_done, 2 * t + 2)
                        for c in range(DC):
                            act.activation(qr[:, c, :], bank[3][:, c * R:(c + 1) * R], ACT.Relu,
                                           bias=bq[:, c:c + 1]).then_inc(qe_done, 1)
                        act.activation(qm.rearrange("p c r -> p (c r)"), qm.rearrange("p c r -> p (c r)"),
                                       ACT.Exp).then_inc(qe_done, 1)

                @block.vector
                def _(dve):
                    n = [0]

                    def step(ins):
                        n[0] += 1
                        ins.then_inc(ra, 1)
                        dve.wait_ge(ra, n[0])

                    with dve.Fori(0, T) as t:
                        dve.bn_stats(stats[:, t, :], X[:, t, :]).then_inc(ra, 1)
                    n[0] = T
                    dve.wait_ge(ra, T)
                    mo, me = stats[:, :, 4], stats[:, :, 1]
                    step(dve.tensor_tensor(mean, me, mo, ALU.add))
                    step(dve.tensor_tensor(shift, me, mo, ALU.subtract))
                    step(dve.tensor_scalar(mean, mean, 0.5, None, ALU.mult))
                    step(dve.tensor_tensor(shift, shift, shift, ALU.mult))
                    step(dve.tensor_tensor(var, stats[:, :, 2], stats[:, :, 5], ALU.add))
                    step(dve.tensor_scalar(var, var, 1.0 / D, LN_EPS, ALU.mult, ALU.add))
                    step(dve.scalar_tensor_tensor(var, shift, 0.25, var, ALU.mult, ALU.add))
                    dve.memset(xn[:, D:D + 1], 1.0).then_inc(stats_done, 1)
                    dve.wait_ge(std_done, 1)
                    step(dve.reciprocal(rstd, rstd))
                    step(dve.tensor_tensor(shift, rstd, rstd, ALU.mult))
                    step(dve.tensor_tensor(shift, shift, var, ALU.mult))
                    step(dve.tensor_scalar(shift, shift, -0.5, 1.5, ALU.mult, ALU.add))
                    step(dve.tensor_tensor(rstd, rstd, shift, ALU.mult))
                    step(dve.scalar_tensor_tensor(shift, mean, -1.0, rstd, ALU.mult, ALU.mult))
                    dve.wait_ge(va_psum, 1)
                    dve.tensor_copy(va.rearrange("p c w -> p (c w)"), bank[0][:, 0:2 * DC]).then_inc(va_done, 1)
                    dve.tensor_tensor(ca, bank[0][:, 8:10], ba, ALU.add).then_inc(va_done, 1)
                    dve.wait_ge(va_psum, 2)
                    dve.tensor_copy(WT.rearrange("p c n -> p (c n)"), bank[1][:, :]).then_inc(va_done, 1)
                    with dve.Fori(0, T) as t:
                        dve.wait_ge(table_out, 16 * t)
                        dve.wait_ge(kx_psum, t)
                        dve.tensor_scalar(xn[:, 0:D], X[:, t, :], rstd[:, bass.ds(t, 1)], shift[:, bass.ds(t, 1)],
                                          ALU.mult, ALU.add).then_inc(xn_done, 1)
                        dve.wait_ge(av_psum, t + 1)
                        dve.tensor_tensor(A12[:, t, :], bank[1][0:R, 0:2], ca[0:R], ALU.add).then_inc(av_done, 1)
                        dve.wait_ge(av_done, 2 * t + 1)
                        dve.tensor_copy(xn[:, D + 1:D + 2], A12[:, t, 1:2]).then_inc(av_done, 1)
                        dve.wait_ge(k_psum, t + 1)
                        dve.tensor_tensor(kb, bank[2][0:R, 0:D], bk, ALU.add).then_inc(kb_done, 1)
                        dve.wait_ge(kb_done, t + 1)
                        dve.tensor_scalar(km, kb, 0.0, None, ALU.min).then_inc(km_done, 1)
                        dve.wait_ge(ke_done, t + 1)
                        dve.scalar_tensor_tensor(ks, kb, 0.0, km, ALU.max, ALU.add).then_inc(ks_done, 1)
                        dve.wait_ge(q_psum, t + 1)
                        dve.wait_ge(q_done, t)
                        for c in range(DC):
                            dve.tensor_scalar(qm[:, c, :], bank[3][:, c * R:(c + 1) * R], bq[:, c:c + 1], 0.0,
                                              ALU.add, ALU.min).then_inc(qm_done, 1)
                        dve.wait_ge(qe_done, 3 * t + 3)
                        dve.tensor_tensor(QT[:, :, bass.ds(t * R, R)], qr, qm, ALU.add).then_inc(q_done, 1)
                    dve.wait_ge(head_psum, 1)
                    for c in range(DC):
                        dve.tensor_copy(kx[:, c, :], bank[6 + c][:, 0:D + 1]).then_inc(head_done, 1)
                    dve.wait_ge(head_psum, 2)
                    dve.tensor_copy(kxT.rearrange("p c n -> p (c n)"), bank[0][:, :]).then_inc(head_done, 1)
                    dve.tensor_copy(ksum, bank[1][0:1, 0:D]).then_inc(head_done, 1)
                    dve.wait_ge(mix_made, 2 + 128 // HD)
                    dve.wait_ge(head_psum, 3)
                    for c in range(DC):
                        dve.tensor_tensor(kvT[:, c, :], bank[2][:, c * 128:(c + 1) * 128], same_head,
                                          ALU.mult).then_inc(head_done, 1)
                    for c in range(DC):
                        dve.tensor_scalar(B[:, c, :], same_head, kx[:, c, D:D + 1], None, ALU.mult).then_inc(head_done, 1)
                    dve.wait_ge(head_psum, 4)
                    dve.tensor_copy(M.rearrange("p c n -> p (c n)"), bank[3][:, :]).then_inc(head_done, 1)
                    with dve.Fori(0, T) as t:
                        dve.wait_ge(norm_psum, t + 1)
                        dve.wait_ge(qn_done, t)
                        dve.tensor_scalar(qr.rearrange("p c r -> p (c r)"), bank[0][:, 0:DC * R], NORM_EPS, None,
                                          ALU.add).then_inc(norm_eps, 1)
                        dve.wait_ge(norm_eps, t + 1)
                        dve.reciprocal(qr, qr).then_inc(norm_inv, 1)
                        dve.wait_ge(norm_inv, t + 1)
                        dve.wait_ge(mix_psum, t)
                        dve.tensor_tensor(qn, QT[:, :, bass.ds(t * R, R)], qr, ALU.mult).then_inc(qn_done, 1)
                        dve.wait_ge(mix_psum, t + 1)
                        dve.tensor_tensor(X[:, t, :], X[:, t, :], bank[1][0:R, 0:D], ALU.add).then_inc(mixed, 1)
                    dve.tensor_reduce(mins[0:R, 0:1], A12[:, :, 1], AX, ALU.min).then_inc(head_done, 1)
                    dve.wait_ge(head_psum, 5)
                    dve.tensor_reduce(mins[0:1, 1:2], bank[2][0:1, 0:R], AX, ALU.min).then_inc(head_done, 1)
                    dve.wait_ge(head_psum, 6)
                    dve.tensor_scalar(a2min, bank[3][:, 0:1], -1.0, None, ALU.add).then_inc(head_done, 1)

        a = Arena(rest, rest_at, REST_W)
        stats2 = a.take(R, T, 6)
        after_stats = a.at
        with ExitStack() as _:
            b = Arena(big, 0, BIG_W)
            Gt = b.take(128, U, Q * TW)
            V = b.take(128, U, Q, R)
            own_T = b.take(R, Q * 128, dtype=BF16)
            item = a.take(128, U, Q * 2, dtype=I32)
            score, local = a.take(128, U, Q), a.take(128, U, Q)
            most = a.take(128, R)
            old, new, zn, zo, mo, fade, keepf = (a.take(R, 1) for _ in range(7))
            base = a.take(R, T)
            cm = a.take(R, 2)
            left = a.take(R, 2)
            parts = a.take(R, 3, 2, dtype=BF16)
            ident16 = a.take(128, 128, dtype=BF16)
            cm_e = a.take(128, Q, 2)
            z, weight = a.take(128, Q), a.take(128, Q)
            AGG = a.take(R, D + 1)
            An, AnT, flagT = a.take(R, D + 1), a.take(128, DC, R), a.take(1, R)
            sinv = a.take(R, 1)
            GROUPS = [range(g, min(g + 4, Q)) for g in range(0, Q, 4)]
            NG = len(GROUPS)
            PARTS = [range(8), range(8, Q)]
            assert NG == 5
            bT, bMost, bCM, bAgg, bAnT, bOut = (0, 1, 2), 3, 4, 5, 7, 6

            item_in, half_gathered, rest_gathered, half_used, used = ([sem(f"{n}{u}") for u in range(U)] for n in (
                "item_in", "half_gathered", "rest_gathered", "half_used", "used"))
            (s_set, s_score, s_v, s_most, s_mostT, s_small, s_fade, s_turned, s_cm, s_cme, s_z, s_exp, s_w, s_agg, s_an,
             s_anT, s_anTc, s_out, s_x, s_stat, s_fin) = (sem(n) for n in (
                 "set_up", "scored", "v_built", "most_done", "most_turned", "small_step", "fade_done", "own_turned",
                 "cm_psum", "cm_copied", "z_step", "exp_done", "w_built", "agg_step", "an_step", "anT_psum", "anT_copied",
                 "out_psum", "x_added", "stat_done", "final_step"))
            v_turned, marked = sem("v_turned"), sem("marked")
            mark = a.take(1, 1)
            SM, SZ, SA = 13, 4, 3

            with nc.Block() as block:
                @block.sync
                def _(sp):
                    more = sp.value_load(rounds, min_val=MIN_ROUNDS - 1, max_val=ITEMS // U - 1)
                    view = slots.rearrange("(c p q) w -> c p (q w)", p=128, q=Q)
                    with sp.Fori(0, more + 1) as k:
                        for u in range(U):
                            sp.wait_ge(s_score, 3 * (U * k + u))
                            sp.dma_start(item[:, u, :], view[bass.ds(U * k + u, 1)].rearrange("c p f -> (c p) f")
                                         ).then_inc(item_in[u], 16)

                @block.gpsimd
                def _(pool):
                    more = pool.value_load(rounds, min_val=MIN_ROUNDS - 1, max_val=ITEMS // U - 1)
                    with pool.Fori(0, more + 1) as k:
                        for u in range(U):
                            for part, (freed, gathered) in enumerate(((half_used, half_gathered), (used, rest_gathered))):
                                pool.wait_ge(freed[u], k + 1)
                                pool.wait_ge(marked, 2 * (U * k + u) + part)
                                pool.tensor_tensor(mark, iota_r[0:1, 0:1], iota_r[0:1, 0:1], ALU.add).then_inc(marked, 1)
                                if part == 0:
                                    pool.wait_ge(item_in[u], 16)
                                    pool.sem_clear(item_in[u])
                                for q in PARTS[part]:
                                    pool.indirect_dma_start(
                                        Gt[:, u, q * TW:(q + 1) * TW], None, table,
                                        bass.IndirectOffsetOnAxis(ap=item[:, u, 2 * q:2 * q + 1], axis=0)
                                    ).then_inc(gathered[u], 16)

                @block.tensor
                def _(pe):
                    more = pe.value_load(rounds, min_val=MIN_ROUNDS - 1, max_val=ITEMS // U - 1)
                    bank16 = [bank[i][0:R, 0:256].bitcast(BF16) for i in bT]

                    def upper(ap):
                        return ap.bitcast(BF16).rearrange("p (r w) -> p r w", w=2)[:, :, 1]

                    pe.wait_ge(s_set, 4)

                    def turn(i, u):
                        free = [NG * i + NG - 1, NG * i + NG, NG * i + NG, NG * i + NG + 1, NG * i + NG + 2]
                        for g, qs in enumerate(GROUPS):
                            pe.wait_ge(s_turned, free[g])
                            pe.wait_ge(s_v, Q * i + (qs[-1] + 1))
                            for j, q in enumerate(qs):
                                mm = pe.transpose(bank16[g % 3][:, j * 128:(j + 1) * 128], upper(V[:, u, q, :]), ident16)
                            mm.then_inc(v_turned, 1)

                    def turn_largest(i):
                        pe.wait_ge(s_most, i + 1)
                        pe.transpose(bank[bMost][0:R, 0:128], most, ident).then_inc(s_mostT, 1)

                    def spread(i):
                        pe.wait_ge(s_turned, NG * i + 2 * NG)
                        pe.wait_ge(s_small, SM * i + SM)
                        pe.wait_ge(s_cme, i)
                        for q in range(Q):
                            mm = pe.matmul(bank[bCM][:, 6 * q:6 * q + 6], own_T[:, q * 128:(q + 1) * 128],
                                           parts.rearrange("p s w -> p (s w)"), start=True, stop=True)
                        mm.then_inc(s_cm, 1)

                    def into_x(i):
                        pe.wait_ge(s_an, SA * i + SA)
                        pe.wait_ge(s_anTc, 2 * i)
                        for c in range(DC):
                            pe.transpose(bank[bAnT][:, c * R:(c + 1) * R], An[:, c * 128:(c + 1) * 128], ident[0:R, 0:R])
                        pe.transpose(bank[bAnT][0:1, 256:256 + R], An[:, D:D + 1], ident[0:R, 0:R]).then_inc(s_anT, 1)

                    def out_x(i):
                        pe.wait_ge(s_anTc, 2 * i + 2)
                        pe.wait_ge(s_x, i)
                        for c in range(DC):
                            pe.matmul(bank[bOut][0:R, 0:D], AnT[:, c, :], WT[:, c, :], start=c == 0, stop=False)
                        pe.matmul(bank[bOut][0:R, 0:D], flagT, gb_row, start=False, stop=True).then_inc(s_out, 1)

                    def sum_edges(i, u, groups):
                        for qs in groups:
                            pe.wait_ge(s_w, Q * (i + 1) + (qs[-1] + 1))
                            for q in qs:
                                mm = pe.matmul(bank[bAgg][0:R, 0:D + 1], V[:, u, q, :],
                                               Gt[:, u, q * TW:q * TW + D + 1], start=q == 0, stop=q == Q - 1)
                            if qs[-1] == PARTS[0][-1]:
                                mm.then_inc(half_used[u], 1)
                            if qs[-1] == Q - 1:
                                mm.then_inc(used[u], 1)

                    def step(i, u, ahead):
                        spread(i)
                        if ahead:
                            turn(i + 1, (u + 1) % U)
                        into_x(i)
                        out_x(i)
                        if ahead:
                            turn_largest(i + 1)
                        sum_edges(i, u, GROUPS)

                    sum_edges(-1, U - 1, GROUPS)
                    turn(0, 0)
                    turn_largest(0)
                    with pe.Fori(0, more) as k:
                        for u in range(U):
                            step(U * k + u, u, True)
                    for u in range(U):
                        step(U * more + u, u, u < U - 1)
                    into_x(U * more + U)
                    out_x(U * more + U)

                @block.scalar
                def _(act):
                    more = act.value_load(rounds, min_val=MIN_ROUNDS - 1, max_val=ITEMS // U - 1)

                    def turned(i):
                        act.wait_ge(s_cm, i)
                        for g, qs in enumerate(GROUPS):
                            w = 128 * len(qs)
                            act.wait_ge(v_turned, NG * i + (g + 1))
                            act.activation(own_T[:, g * 512:g * 512 + w], bank[bT[g % 3]][0:R, 0:256].bitcast(BF16)[:, 0:w],
                                           ACT.Sign).then_inc(s_turned, 1)

                    def turn_sums(i):
                        act.wait_ge(s_anT, i + 1)
                        act.wait_ge(s_out, i)
                        act.copy(AnT.rearrange("p c r -> p (c r)"), bank[bAnT][:, 0:DC * R]).then_inc(s_anTc, 1)
                        act.copy(flagT, bank[bAnT][0:1, 256:256 + R]).then_inc(s_anTc, 1)

                    def step(i, u, ahead):
                        act.wait_ge(s_small, SM * i + SM)
                        act.activation(fade, mo, ACT.Exp).then_inc(s_fade, 1)
                        if ahead:
                            turned(i + 1)
                        turn_sums(i)
                        act.wait_ge(s_z, SZ * i + SZ)
                        act.activation(weight, z, ACT.Exp).then_inc(s_exp, 1)

                    turned(0)
                    with act.Fori(0, more) as k:
                        for u in range(U):
                            step(U * k + u, u, True)
                    for u in range(U):
                        step(U * more + u, u, u < U - 1)
                    turn_sums(U * more + U)

                @block.vector
                def _(dve):
                    more = dve.value_load(rounds, min_val=MIN_ROUNDS - 1, max_val=ITEMS // U - 1)
                    dve.memset(V[:, U - 1], 0.0).then_inc(s_set, 1)
                    dve.memset(Gt[:, U - 1], 0.0).then_inc(s_set, 1)
                    dve.memset(z, 0.0).then_inc(s_w, Q)
                    dve.memset(cm_e, 0.0).then_inc(s_set, 1)
                    dve.memset(AGG, 0.0).then_inc(s_fin, 1)
                    dve.tensor_copy(ident16, ident).then_inc(s_set, 1)
                    dve.memset(new, 0.0).then_inc(s_turned, NG)
                    dve.memset(keepf, 0.0).then_inc(used[0], 1)
                    dve.memset(sinv, 0.0).then_inc(used[1], 1)
                    dve.memset(old, 0.0).then_inc(half_used[0], 1)
                    dve.memset(zo, 0.0).then_inc(half_used[1], 1)
                    dve.memset(most, 0.0).then_inc(s_score, 3 * (U - 1))
                    dve.tensor_scalar(base, A12[:, :, 0], a2min[0:R], None, ALU.add).then_inc(s_fin, 1)
                    dve.wait_ge(s_fin, 2)

                    def add_sums(i, done, count):
                        dve.wait_ge(done, count)
                        dve.scalar_tensor_tensor(AGG, AGG, keepf, bank[bAgg][0:R, 0:D + 1], ALU.mult,
                                                 ALU.add).then_inc(s_an, 1)
                        dve.wait_ge(s_an, SA * i + 1)
                        dve.tensor_scalar(sinv, AGG[:, D:D + 1], 1e-30, None, ALU.max).then_inc(s_agg, 1)
                        dve.wait_ge(s_agg, i + 1)
                        dve.reciprocal(sinv, sinv).then_inc(s_an, 1)
                        dve.wait_ge(s_an, SA * i + 2)
                        dve.wait_ge(s_anT, i)
                        dve.tensor_scalar(An, AGG, sinv, None, ALU.mult).then_inc(s_an, 1)

                    def add_x(i):
                        tile = dve.value_load(item_tile[0:1, bass.ds(i, 1)], min_val=0, max_val=T - 1)
                        dve.wait_ge(s_out, i + 1)
                        dve.scalar_tensor_tensor(X[:, tile, :], bank[bOut][0:R, 0:D], is_last[:, bass.ds(i, 1)],
                                                 X[:, tile, :], ALU.mult, ALU.add).then_inc(s_x, 1)
                        dve.wait_ge(s_x, i + 1)
                        dve.bn_stats(stats2[:, tile, :], X[:, tile, :]).then_inc(s_stat, 1)

                    def build(i, u, k):
                        rows = Gt[:, u, :].rearrange("p (q w) -> p q w", q=Q)
                        for part, gathered in enumerate((half_gathered, rest_gathered)):
                            lo, hi = PARTS[part][0], PARTS[part][-1] + 1
                            dve.wait_ge(gathered[u], 16 * (hi - lo) * (k + 1))
                            dve.tensor_scalar(score[:, u, lo:hi], rows[:, lo:hi, D + 1], a2min, None,
                                              ALU.subtract).then_inc(s_score, 1)
                            if part == 0:
                                dve.tensor_copy(local[:, u, :], item[:, u, :].rearrange("p (q w) -> p q w", w=2)[:, :, 1]
                                                ).then_inc(s_score, 1)
                            dve.wait_ge(s_score, 3 * (i + U - 1) + 2 + part)
                            for q in PARTS[part]:
                                dve.tensor_scalar(V[:, u, q, :], iota_r[:, 0:R], local[:, u, q:q + 1],
                                                  score[:, u, q:q + 1], ALU.is_equal, ALU.mult).then_inc(s_v, 1)

                    def largest(i, u):
                        dve.wait_ge(s_v, Q * i + Q)
                        dve.wait_ge(s_mostT, i)
                        dve.tensor_reduce(most, V[:, u].rearrange("p q r -> p r q"), AX, ALU.max).then_inc(s_most, 1)

                    def maxima(i):
                        def small(j, ins):
                            ins.then_inc(s_small, 1)
                            dve.wait_ge(s_small, SM * i + j)

                        tile = dve.value_load(item_tile[0:1, bass.ds(i + 1, 1)], min_val=0, max_val=T - 1)
                        own = base[:, bass.ds(tile, 1)]
                        dve.wait_ge(s_fade, i)
                        dve.wait_ge(s_cm, i)
                        small(1, dve.tensor_tensor(old, new, is_same[:, bass.ds(i, 1)], ALU.mult))
                        dve.wait_ge(s_mostT, i + 1)
                        small(2, dve.tensor_reduce(new, bank[bMost][0:R, 0:128], AX, ALU.max))
                        small(3, dve.tensor_tensor(new, new, old, ALU.max))
                        dve.tensor_tensor(zo, own, old, ALU.add).then_inc(s_small, 1)
                        small(5, dve.tensor_tensor(zn, own, new, ALU.add))
                        dve.tensor_scalar(cm[:, 0:1], own, 0.0, None, ALU.add).then_inc(s_small, 1)
                        dve.scalar_tensor_tensor(mo, zo, 0.01, zo, ALU.mult, ALU.max).then_inc(s_small, 1)
                        small(8, dve.scalar_tensor_tensor(cm[:, 1:2], zn, 0.01, zn, ALU.mult, ALU.max))
                        dve.tensor_tensor(mo, mo, cm[:, 1:2], ALU.subtract).then_inc(s_small, 1)
                        small(10, dve.tensor_copy(parts[:, 0, :], cm))
                        small(11, dve.tensor_tensor(left, cm, parts[:, 0, :], ALU.subtract))
                        small(12, dve.tensor_copy(parts[:, 1, :], left))
                        dve.tensor_tensor(parts[:, 2, :], left, parts[:, 1, :], ALU.subtract).then_inc(s_small, 1)

                    def exponents(i, u):
                        dve.wait_ge(s_cm, i + 1)
                        dve.tensor_reduce(cm_e, bank[bCM][:, 0:6 * Q].rearrange("p (q s w) -> p q w s", q=Q, s=3), AX,
                                          ALU.add).then_inc(s_cme, 1)
                        dve.wait_ge(s_cme, i + 1)
                        dve.tensor_tensor(z, cm_e[:, :, 0], score[:, u, :], ALU.add).then_inc(s_z, 1)
                        dve.wait_ge(s_z, SZ * i + 1)
                        dve.scalar_tensor_tensor(z, z, 0.01, z, ALU.mult, ALU.max).then_inc(s_z, 1)
                        dve.wait_ge(s_z, SZ * i + 2)
                        dve.tensor_tensor(z, z, cm_e[:, :, 1], ALU.subtract).then_inc(s_z, 1)
                        dve.wait_ge(s_z, SZ * i + 3)
                        dve.tensor_scalar(z, z, 0.0, None, ALU.min).then_inc(s_z, 1)

                    def weigh(i, u):
                        dve.wait_ge(s_exp, i + 1)
                        for q in range(Q):
                            dve.tensor_scalar(V[:, u, q, :], iota_r[:, 0:R], local[:, u, q:q + 1], weight[:, q:q + 1],
                                              ALU.is_equal, ALU.mult).then_inc(s_w, 1)

                    def step(i, u, k, ahead):
                        maxima(i)
                        if ahead:
                            build(i + 1, (u + 1) % U, k + 1 if u == U - 1 else k)
                        add_sums(i, used[(u - 1) % U], k + 1 if u == 0 else k + 2)
                        exponents(i, u)
                        if ahead:
                            largest(i + 1, (u + 1) % U)
                        dve.wait_ge(s_fade, i + 1)
                        dve.tensor_tensor(keepf, fade, is_same[:, bass.ds(i, 1)], ALU.mult).then_inc(s_fin, 1)
                        weigh(i, u)
                        add_x(i)

                    build(0, 0, 0)
                    largest(0, 0)
                    with dve.Fori(0, more) as k:
                        for u in range(U):
                            step(U * k + u, u, k, True)
                    for u in range(U):
                        step(U * more + u, u, more, u < U - 1)
                    add_sums(U * more + U, used[U - 1], more + 2)
                    add_x(U * more + U)

        a = Arena(rest, after_stats, REST_W)
        M2 = a.take(128, IC, D)
        mean, rstd, shift = a.take(R, T), a.take(R, T), a.take(R, T)
        after_m2 = a.at
        FB = 4
        SW = big[0:R, 0:T * INNER].rearrange("p (t n) -> p t n", t=T)
        with ExitStack() as _:
            var = a.take(R, T)
            WL = a.take(128, DC, INNER)
            bL = a.take(R, INNER)
            y, yT = a.take(R, FB, D + 1), a.take(128, 2, DC, R)
            L = a.take(R, FB, INNER)
            top, tot, inv = a.take(R, 2, FH), a.take(R, 2, FH), a.take(R, 2, FH)
            zero_row = a.take(1, 512)
            WxT = big[0:G, 0:FH * D].rearrange("p (h d) -> p h d", h=FH)
            Wx = big[:, 2048:2048 + DC * INNER].rearrange("p (c n) -> p c n", c=DC)
            Wsl = big[0:G, 3072:3072 + G]
            bx = big[0:G, 3136:3136 + FH]
            bsl = big[:, 3144:3144 + G]
            temp = big[:, 3208:3208 + FH]
            fw_in, fw_psum, fw_done, fs = sem("fw_in"), sem("fw_psum"), sem("fw_done"), sem("fs")
            sq_in, sq_done = sem("sq_in"), sem("sq_done")
            y_done, yT_psum, yT_done, l_psum, l_done = (sem(n) for n in ("y_done", "yT_psum", "yT_done", "l_psum", "l_done"))
            l_top, l_sub, l_exp, l_tot, l_inv, sw_done, sum_psum = (sem(n) for n in (
                "l_top", "l_sub", "l_exp", "l_tot", "l_inv", "sw_done", "sum_psum"))
            zeros, sw_kept = sem("zeros"), sem("sw_kept")
            with nc.Block() as block:
                @block.sync
                def _(sp):
                    with nc.allow_non_contiguous_dma(reason="columns of small vectors"):
                        sp.dma_start(Wx, W_x.rearrange("(c p) n -> p c n", p=128)).then_inc(fw_in, 16)
                        sp.dma_start(Wsl, W_slice).then_inc(fw_in, 16)
                        sp.dma_start(bx, b_x.rearrange("(h j) -> j h", h=FH)).then_inc(fw_in, 16)
                        sp.dma_start(bsl, row(b_slice).to_broadcast([128, G])).then_inc(fw_in, 16)
                        sp.dma_start(temp, temperature.rearrange("a h b c -> (a b c) h").to_broadcast([128, FH])
                                     ).then_inc(fw_in, 16)

                @block.tensor
                def _(pe):
                    pe.wait_ge(fw_in, 80)
                    for h in range(FH):
                        for c in range(DC):
                            i = h * DC + c
                            mm = pe.transpose(bank[i // 4][0:G, (i % 4) * 128:(i % 4 + 1) * 128],
                                              Wx[:, c, h * G:(h + 1) * G], ident)
                    mm.then_inc(fw_psum, 1)
                    pe.wait_ge(fw_done, 4)
                    for c in range(DC):
                        for h in range(FH):
                            pe.matmul(bank[4 + c][:, h * G:(h + 1) * G], WxT[:, h, c * 128:(c + 1) * 128], Wsl,
                                      start=True, stop=True)
                    for h in range(FH):
                        mm = pe.matmul(bank[6][:, h * G:(h + 1) * G], bx[:, h:h + 1].to_broadcast([G, 128]), Wsl,
                                       start=True, stop=True)
                    mm.then_inc(fw_psum, 1)
                    pe.wait_ge(zeros, 3)
                    pe.wait_ge(fw_done, 8)
                    for c in range(IC):
                        pe.matmul(bank[4 + c][:, 0:D + 1], zero_row[:, 0:128], zero_row[:, 0:D + 1], start=True,
                                  stop=False, skip_group_check=True)

                    def turn(t, u):
                        pe.wait_ge(y_done, t + 1)
                        for c in range(DC):
                            mm = pe.transpose(bank[3 * (u % 2)][:, c * R:(c + 1) * R], y[:, u, c * 128:(c + 1) * 128],
                                              ident[0:R, 0:R])
                        mm.then_inc(yT_psum, 1)

                    def logits(t, u):
                        pe.wait_ge(yT_done, t + 1)
                        for c in range(DC):
                            mm = pe.matmul(bank[1 + u % 2][0:R, :], yT[:, u % 2, c, :], WL[:, c, :], start=c == 0,
                                           stop=c == DC - 1)
                        mm.then_inc(l_psum, 1)

                    def sums(t, u):
                        pe.wait_ge(sw_done, t + 2)
                        for c in range(IC):
                            mm = pe.matmul(bank[4 + c][:, 0:D + 1], L[:, u, c * 128:(c + 1) * 128], y[:, u, :],
                                           start=False, stop=False, skip_group_check=True)
                        mm.then_inc(sum_psum, 1)

                    def step(t, u, ahead):
                        if ahead:
                            pe.wait_ge(yT_done, t + 1)
                            turn(t + 2, (u + 2) % FB)
                        sums(t - 1, (u - 1) % FB)
                        if ahead:
                            pe.wait_ge(l_done, t + 1)
                            logits(t + 2, (u + 2) % FB)

                    for t in range(2):
                        turn(t, t)
                        logits(t, t)
                    with pe.Fori(0, (T - 2) // FB) as k:
                        for u in range(FB):
                            step(FB * k + u, u, True)
                    for t in range(T - 2, T):
                        step(t, t % FB, False)
                    sums(T - 1, (T - 1) % FB)
                    for c in range(IC):
                        mm = pe.matmul(bank[4 + c][:, 0:D + 1], zero_row[:, 0:128], zero_row[:, 0:D + 1], start=False,
                                       stop=True, skip_group_check=True)
                    mm.then_inc(sum_psum, 1)
                    pe.wait_ge(sum_psum, T + 2)

                @block.scalar
                def _(act):
                    act.wait_ge(sq_in, 1)
                    act.activation(rstd, var, ACT.Sqrt).then_inc(sq_done, 1)

                    def turned(t, u):
                        act.wait_ge(yT_psum, t + 1)
                        act.copy(yT[:, u % 2].rearrange("p c r -> p (c r)"), bank[3 * (u % 2)][:, 0:DC * R]
                                 ).then_inc(yT_done, 1)

                    def exp(t, u):
                        act.wait_ge(l_sub, t + 1)
                        act.activation(L[:, u], L[:, u], ACT.Exp).then_inc(l_exp, 1)

                    for t in range(2):
                        turned(t, t)
                    exp(0, 0)
                    with act.Fori(0, (T - 2) // FB) as k:
                        for u in range(FB):
                            t = FB * k + u
                            act.wait_ge(l_psum, t + 1)
                            turned(t + 2, (u + 2) % FB)
                            exp(t + 1, (u + 1) % FB)
                    exp(T - 1, (T - 1) % FB)

                @block.gpsimd
                def _(pool):
                    pool.memset(zero_row, 0.0).then_inc(zeros, 1)
                    pool.memset(L[:, FB - 1], 0.0).then_inc(zeros, 1)
                    pool.memset(y[:, FB - 1], 0.0).then_inc(zeros, 1)

                    def keep_sw(t, u):
                        pool.wait_ge(sw_done, t + 2)
                        pool.tensor_copy(SW[:, t, :], L[:, u]).then_inc(sw_kept, 1)

                    with pool.Fori(0, T // FB) as k:
                        for u in range(FB):
                            keep_sw(FB * k + u, u)
                    for t in range(T - T % FB, T):
                        keep_sw(t, t % FB)

                @block.vector
                def _(dve):
                    n = [0]

                    def step(ins):
                        n[0] += 1
                        ins.then_inc(fs, 1)
                        dve.wait_ge(fs, n[0])

                    mo, me = stats2[:, :, 4], stats2[:, :, 1]
                    step(dve.tensor_tensor(mean, me, mo, ALU.add))
                    step(dve.tensor_tensor(shift, me, mo, ALU.subtract))
                    step(dve.tensor_scalar(mean, mean, 0.5, None, ALU.mult))
                    step(dve.tensor_tensor(shift, shift, shift, ALU.mult))
                    step(dve.tensor_tensor(var, stats2[:, :, 2], stats2[:, :, 5], ALU.add))
                    step(dve.tensor_scalar(var, var, 1.0 / D, LN_EPS, ALU.mult, ALU.add))
                    step(dve.scalar_tensor_tensor(var, shift, 0.25, var, ALU.mult, ALU.add))
                    dve.wait_ge(zeros, 3)
                    dve.memset(y[:, :, D], 1.0).then_inc(sq_in, 1)
                    dve.wait_ge(sq_done, 1)
                    step(dve.reciprocal(rstd, rstd))
                    step(dve.tensor_tensor(shift, rstd, rstd, ALU.mult))
                    step(dve.tensor_tensor(shift, shift, var, ALU.mult))
                    step(dve.tensor_scalar(shift, shift, -0.5, 1.5, ALU.mult, ALU.add))
                    step(dve.tensor_tensor(rstd, rstd, shift, ALU.mult))
                    step(dve.scalar_tensor_tensor(shift, mean, -1.0, rstd, ALU.mult, ALU.mult))
                    dve.wait_ge(fw_in, 80)
                    step(dve.tensor_scalar(temp, temp, 0.1, 5.0, ALU.max, ALU.min))
                    step(dve.reciprocal(temp, temp))
                    dve.wait_ge(fw_psum, 1)
                    for i in range(4):
                        dve.tensor_copy(big[0:G, i * 512:(i + 1) * 512], bank[i][0:G, :]).then_inc(fw_done, 1)
                    dve.wait_ge(fw_psum, 2)

                    def heads(p):
                        return temp[0:p].unsqueeze(2).to_broadcast([p, FH, G])

                    def split(ap):
                        return ap.rearrange("p (h g) -> p h g", h=FH)

                    for c in range(DC):
                        dve.tensor_tensor(split(WL[:, c, :]), split(bank[4 + c][:, :]), heads(128), ALU.mult).then_inc(fw_done, 1)
                    dve.tensor_tensor(split(bL), split(bank[6][0:R, :]), bsl[0:R].unsqueeze(1).to_broadcast([R, FH, G]),
                                      ALU.add).then_inc(fw_done, 1)
                    dve.wait_ge(fw_done, 7)
                    dve.tensor_tensor(split(bL), split(bL), heads(R), ALU.mult).then_inc(fw_done, 1)
                    dve.wait_ge(fw_done, 8)
                    dve.memset(inv, 0.0).then_inc(sw_done, 1)
                    dve.memset(tot, 0.0).then_inc(sw_kept, 2)
                    dve.wait_ge(sw_done, 1)
                    dve.wait_ge(sw_kept, 2)

                    def normalise(t, u):
                        dve.tensor_scalar(y[:, u, 0:D], X[:, t, :], rstd[:, bass.ds(t, 1)], shift[:, bass.ds(t, 1)],
                                          ALU.mult, ALU.add).then_inc(y_done, 1)

                    def biased(t, u):
                        dve.wait_ge(l_psum, t + 1)
                        dve.tensor_tensor(L[:, u], bank[1 + u % 2][0:R, :], bL, ALU.add).then_inc(l_done, 1)

                    def maxima(t, u):
                        dve.wait_ge(l_done, t + 1)
                        dve.tensor_reduce(top[:, u % 2], split(L[:, u]), AX, ALU.max).then_inc(l_top, 1)

                    def below(t, u):
                        dve.wait_ge(l_top, t + 1)
                        dve.tensor_tensor(split(L[:, u]), split(L[:, u]),
                                          top[:, u % 2].unsqueeze(2).to_broadcast([R, FH, G]),
                                          ALU.subtract).then_inc(l_sub, 1)

                    def totals(t, u):
                        dve.wait_ge(l_exp, t + 1)
                        dve.tensor_reduce(tot[:, u % 2], split(L[:, u]), AX, ALU.add).then_inc(l_tot, 1)

                    def inverse(t, u):
                        dve.wait_ge(l_tot, t + 1)
                        dve.reciprocal(inv[:, u % 2], tot[:, u % 2]).then_inc(l_inv, 1)

                    def divide(t, u):
                        dve.wait_ge(l_inv, t + 1)
                        dve.tensor_tensor(split(L[:, u]), split(L[:, u]),
                                          inv[:, u % 2].unsqueeze(2).to_broadcast([R, FH, G]),
                                          ALU.mult).then_inc(sw_done, 1)

                    normalise(0, 0)
                    normalise(1, 1)
                    biased(0, 0)
                    maxima(0, 0)
                    below(0, 0)
                    with dve.Fori(0, (T - 2) // FB) as k:
                        for u in range(FB):
                            t, v1, v2 = FB * k + u, (u + 1) % FB, (u + 2) % FB
                            dve.wait_ge(sum_psum, t)
                            normalise(t + 2, v2)
                            dve.wait_ge(sw_kept, t)
                            biased(t + 1, v1)
                            totals(t, u)
                            maxima(t + 1, v1)
                            inverse(t, u)
                            below(t + 1, v1)
                            divide(t, u)
                    dve.wait_ge(sum_psum, T - 2)
                    dve.wait_ge(sw_kept, T - 2)
                    biased(T - 1, (T - 1) % FB)
                    maxima(T - 1, (T - 1) % FB)
                    below(T - 1, (T - 1) % FB)
                    for t in range(T - 2, T):
                        totals(t, t % FB)
                        inverse(t, t % FB)
                        divide(t, t % FB)

        with ExitStack() as _:
            a = Arena(rest, after_m2, REST_W)
            tok, tokT = a.take(128, IC, D + 1), a.take(128, DC, INNER)
            normT = a.take(1, INNER)
            den = a.take(128, IC)
            Wfx = a.take(128, DC, INNER)
            bfx = a.take(1, INNER)
            Wq, Wk, Wv = a.take(G, G), a.take(G, G), a.take(G, G)
            Wo = a.take(G, FH, D)
            sT, qT, kT, v = (a.take(G, INNER) for _ in range(4))
            P, PT = a.take(G, INNER), sT
            osT = qT
            ptop, ptot = a.take(G, FH), a.take(G, FH)
            aw_in, ap, ad, ae = sem("aw_in"), sem("attn_psum"), sem("attn_done"), sem("attn_exp")
            ae2 = sem("attn_parts")
            with nc.Block() as block:
                @block.sync
                def _(sp):
                    for to, of in ((Wfx, W_fx.rearrange("(c p) n -> p c n", p=128)), (bfx, row(b_fx)), (Wq, W_q), (Wk, W_k),
                                   (Wv, W_v), (Wo, W_out.rearrange("(h c) d -> c h d", h=FH))):
                        sp.dma_start(to, of).then_inc(aw_in, 16)

                def head(h, of=None):
                    return slice(h * G, (h + 1) * G)

                @block.tensor
                def _(pe):
                    pe.wait_ge(ad, 3)
                    for i in range(IC):
                        for c in range(DC):
                            pe.transpose(bank[c][:, i * 128:(i + 1) * 128], tok[:, i, c * 128:(c + 1) * 128], ident)
                        mm = pe.transpose(bank[2][0:1, i * 128:(i + 1) * 128], tok[:, i, D:D + 1], ident)
                    mm.then_inc(ap, 1)
                    pe.wait_ge(aw_in, 96)
                    pe.wait_ge(ad, 6)
                    for h in range(FH):
                        for c in range(DC):
                            pe.matmul(bank[3][0:G, head(h)], Wfx[:, c, head(h)], tokT[:, c, head(h)], start=c == 0, stop=False)
                        mm = pe.matmul(bank[3][0:G, head(h)], bfx[:, head(h)], normT[:, head(h)], start=False, stop=True)
                    mm.then_inc(ap, 1)
                    pe.wait_ge(ad, 7)
                    pe.matmul(bank[4][0:G, :], Wq, sT, start=True, stop=True)
                    pe.matmul(bank[5][0:G, :], Wk, sT, start=True, stop=True)
                    for h in range(FH):
                        mm = pe.matmul(bank[6][0:G, head(h)], sT[:, head(h)], Wv, start=True, stop=True)
                    mm.then_inc(ap, 1)
                    pe.wait_ge(ad, 10)
                    for h in range(FH):
                        mm = pe.matmul(bank[7][0:G, head(h)], qT[:, head(h)], kT[:, head(h)], start=True, stop=True)
                    mm.then_inc(ap, 1)
                    pe.wait_ge(ad, 15)
                    for h in range(FH):
                        mm = pe.transpose(bank[0][0:G, head(h)], P[:, head(h)], ident[0:G, 0:G])
                    mm.then_inc(ap, 1)
                    pe.wait_ge(ad, 16)
                    for h in range(FH):
                        mm = pe.matmul(bank[1][0:G, head(h)], v[:, head(h)], PT[:, head(h)], start=True, stop=True)
                    mm.then_inc(ap, 1)
                    pe.wait_ge(ad, 17)
                    for h in range(FH):
                        lo = (h % 2) * G
                        mm = pe.matmul(bank[2 + h // 2][lo:lo + G, 0:D], osT[:, head(h)], Wo[:, h, :], start=True, stop=True)
                    mm.then_inc(ap, 1)
                    pe.wait_ge(ap, 7)

                @block.scalar
                def _(act):
                    act.wait_ge(ad, 12)
                    act.activation(P, P, ACT.Exp, scale=SLICE_SCALE).then_inc(ae, 1)

                @block.vector
                def _(dve):
                    n = [0]

                    def step(ins):
                        n[0] += 1
                        ins.then_inc(ad, 1)
                        dve.wait_ge(ad, n[0])

                    def split(ap_):
                        return ap_.rearrange("p (h g) -> p h g", h=FH)

                    for i in range(IC):
                        ins = dve.tensor_scalar(den[:, i:i + 1], bank[4 + i][:, D:D + 1], EPS, None, ALU.add)
                        if i < IC - 1:
                            ins.then_inc(ae2, 1)
                    step(ins)
                    dve.wait_ge(ae2, IC - 1)
                    step(dve.reciprocal(den, den))
                    for i in range(IC):
                        ins = dve.tensor_scalar(tok[:, i, :], bank[4 + i][:, 0:D + 1], den[:, i:i + 1], None, ALU.mult)
                        if i < IC - 1:
                            ins.then_inc(ae2, 1)
                    step(ins)
                    dve.wait_ge(ap, 1)
                    step(dve.tensor_copy(tokT[:, 0, :], bank[0][:, :]))
                    step(dve.tensor_copy(tokT[:, 1, :], bank[1][:, :]))
                    step(dve.tensor_copy(normT, bank[2][0:1, :]))
                    dve.wait_ge(ap, 2)
                    step(dve.tensor_copy(sT, bank[3][0:G, :]))
                    dve.wait_ge(ap, 3)
                    step(dve.tensor_copy(qT, bank[4][0:G, :]))
                    step(dve.tensor_copy(kT, bank[5][0:G, :]))
                    step(dve.tensor_copy(v, bank[6][0:G, :]))
                    dve.wait_ge(ap, 4)
                    step(dve.tensor_reduce(ptop, split(bank[7][0:G, :]), AX, ALU.max))
                    step(dve.tensor_tensor(split(P), split(bank[7][0:G, :]), ptop.unsqueeze(2).to_broadcast([G, FH, G]),
                                           ALU.subtract))
                    dve.wait_ge(ae, 1)
                    step(dve.tensor_reduce(ptot, split(P), AX, ALU.add))
                    step(dve.reciprocal(ptot, ptot))
                    step(dve.tensor_tensor(split(P), split(P), ptot.unsqueeze(2).to_broadcast([G, FH, G]), ALU.mult))
                    dve.wait_ge(ap, 5)
                    step(dve.tensor_copy(PT, bank[0][0:G, :]))
                    dve.wait_ge(ap, 6)
                    step(dve.tensor_copy(osT, bank[1][0:G, :]))
                    dve.wait_ge(ap, 7)
                    for i in range(IC):
                        step(dve.tensor_copy(M2[:, i, :], bank[2 + i][:, 0:D]))

        with ExitStack() as _:
            a = Arena(rest, after_m2, REST_W)
            bout = a.take(R, D)
            sw_in = a.take(R, 2, INNER)
            swT = a.take(128, 2, IC, R)
            res = a.take(R, 2, D)
            bo_in, sw_here, swT_psum, swT_done, o_psum, o_sum, o_done = (sem(n) for n in (
                "bo_in", "sw_here", "swT_psum", "swT_done", "o_psum", "o_sum", "o_done"))
            o_out = [sem("o_out0"), sem("o_out1")]
            with nc.Block() as block:
                @block.sync
                def _(sp):
                    sp.dma_start(bout, row(b_out).to_broadcast([R, D])).then_inc(bo_in, 16)
                    with sp.Fori(0, T // 2) as k:
                        for u in range(2):
                            t = 2 * k + u
                            sp.wait_ge(o_done, t + 1)
                            sp.dma_start(out[bass.ds(t * R, R), :], res[:, u]).then_inc(o_out[u], 16)
                    for u in range(2):
                        sp.wait_ge(o_out[u], 16 * (T // 2))

                @block.gpsimd
                def _(pool):
                    for t in range(2):
                        pool.tensor_copy(sw_in[:, t], SW[:, t, :]).then_inc(sw_here, 1)
                    with pool.Fori(0, T // 2 - 1) as k:
                        for u in range(2):
                            t = 2 * k + u
                            pool.wait_ge(swT_psum, t + 1)
                            pool.tensor_copy(sw_in[:, u], SW[:, t + 2, :]).then_inc(sw_here, 1)

                @block.tensor
                def _(pe):
                    def turn(t, u):
                        pe.wait_ge(sw_here, t + 1)
                        for c in range(IC):
                            mm = pe.transpose(bank[u][:, c * R:(c + 1) * R], sw_in[:, u, c * 128:(c + 1) * 128],
                                              ident[0:R, 0:R])
                        mm.then_inc(swT_psum, 1)

                    def out_of(t, u):
                        pe.wait_ge(swT_done, t + 1)
                        for c in range(IC):
                            mm = pe.matmul(bank[2 + u][0:R, 0:D], swT[:, u, c, :], M2[:, c, :], start=c == 0,
                                           stop=c == IC - 1)
                        mm.then_inc(o_psum, 1)

                    turn(0, 0)
                    with pe.Fori(0, T // 2 - 1) as k:
                        for u in range(2):
                            t = 2 * k + u
                            pe.wait_ge(swT_done, t)
                            turn(t + 1, 1 - u)
                            pe.wait_ge(o_sum, 2 * k - 1 + u if u else 2 * k)
                            out_of(t, u)
                    pe.wait_ge(swT_done, T - 2)
                    turn(T - 1, 1)
                    for t in range(T - 2, T):
                        pe.wait_ge(o_sum, t - 1)
                        out_of(t, t % 2)

                @block.scalar
                def _(act):
                    def turned(t, u):
                        act.wait_ge(swT_psum, t + 1)
                        act.copy(swT[:, u].rearrange("p c r -> p (c r)"), bank[u][:, 0:IC * R]).then_inc(swT_done, 1)

                    for t in range(2):
                        turned(t, t)
                    with act.Fori(0, T // 2 - 1) as k:
                        for u in range(2):
                            t = 2 * k + u
                            act.wait_ge(o_psum, t + 1)
                            turned(t + 2, u)

                @block.vector
                def _(dve):
                    dve.wait_ge(bo_in, 16)
                    with dve.Fori(0, T // 2) as k:
                        for u in range(2):
                            t = 2 * k + u
                            dve.wait_ge(o_out[u], 16 * k)
                            dve.wait_ge(o_psum, t + 1)
                            dve.tensor_tensor(res[:, u], X[:, t, :], bank[2 + u][0:R, 0:D], ALU.add).then_inc(o_sum, 1)
                            dve.wait_ge(o_sum, t + 1)
                            dve.tensor_tensor(res[:, u], res[:, u], bout, ALU.add).then_inc(o_done, 1)


_INS = ["x", "src", "dst", "L0_gnn_W_layer", "L0_gnn_b_layer", "L0_gnn_w_a1", "L0_gnn_b_a1", "L0_gnn_w_a2",
        "L0_gnn_b_a2", "L0_mix_wq", "L0_mix_bq", "L0_mix_wk", "L0_mix_bk", "L0_mix_wv", "L0_mix_bv", "L0_mix_wo",
        "L0_mix_bo", "L0_ffn_W_fx", "L0_ffn_b_fx", "L0_ffn_W_x", "L0_ffn_b_x", "L0_ffn_W_slice", "L0_ffn_b_slice",
        "L0_ffn_W_q", "L0_ffn_W_k", "L0_ffn_W_v", "L0_ffn_W_out", "L0_ffn_b_out", "L0_ffn_temperature"]


def kernel(**inputs):
    import numpy as _np
    import concourse.bacc as _bacc
    from concourse import mybir as _mybir
    from concourse.bass_utils import run_bass_kernel_spmd as _run

    nc = _bacc.Bacc("TRN2", target_bir_lowering=False, num_devices=1)
    arrays, args = {}, []
    for name in _INS:
        a = _np.ascontiguousarray(inputs[name])
        arrays[f"in_{name}_dram"] = a
        args.append(nc.dram_tensor(f"in_{name}_dram", a.shape, _mybir.dt.from_np(a.dtype), kind="ExternalInput").ap())
    result = nc.dram_tensor("out_dram", (N, D), F32, kind="ExternalOutput").ap()
    bass_gps(nc, *args, result)
    r = _run(nc, [arrays], core_ids=[0])
    return r.results[0]["out_dram"]
```

```python
from contextlib import ExitStack

import concourse.bass as bass
from concourse import mybir

F32 = mybir.dt.float32
I32 = mybir.dt.int32
BF16 = mybir.dt.bfloat16
U8 = mybir.dt.uint8
ALU = mybir.AluOpType
ACT = mybir.ActivationFunctionType
AX = mybir.AxisListType.X

N = 6250
D = 256
E = 100000
R = 125
T = N // R
DC = D // 128
EP = 125
EJ = E // EP
TW = D + 2
Q = 17
CH = Q * 128
ITEMS = T + E // CH + 1
U = 3
TAIL = T % U or U
ITEMS += (TAIL - ITEMS) % U
MIN_ROUNDS, MAX_ROUNDS = (T - TAIL) // U, (ITEMS - TAIL) // U
NOBODY = 200
CHUNKS = (0, 80, 240, 480, EJ)
CW = max(hi - lo for lo, hi in zip(CHUNKS, CHUNKS[1:]))
H = 5
TA = 26
SB = 40
HEADS = 8
HD = D // HEADS
FH = 8
G = 64
INNER = FH * G
IC = INNER // 128
EPS = 1e-5
LN_EPS = 1e-5
NORM_EPS = 1e-6
SLICE_SCALE = G ** -0.5


class Arena:

    def __init__(self, tensor, start, end):
        self.tensor, self.at, self.end = tensor, start, end

    def take(self, partitions, *shape, dtype=F32):
        n = 1
        for s in shape:
            n *= s
        words = n if dtype in (F32, I32) else (n + 1) // 2 if dtype == BF16 else (n + 3) // 4
        assert self.at + words <= self.end, (self.at, words, self.end)
        ap = self.tensor[0:partitions, self.at:self.at + words]
        self.at += words
        if dtype != F32:
            ap = ap.bitcast(dtype)
        if len(shape) == 2:
            ap = ap.rearrange("p (a b) -> p a b", a=shape[0])
        if len(shape) == 3:
            ap = ap.rearrange("p (a b c) -> p a b c", a=shape[0], b=shape[1])
        return ap


def bass_gps(nc, x, src, dst, gnn_W, gnn_b, gnn_wa1, gnn_ba1, gnn_wa2, gnn_ba2,
             mix_wq, mix_bq, mix_wk, mix_bk, mix_wv, mix_bv, mix_wo, mix_bo,
             W_fx, b_fx, W_x, b_x, W_slice, b_slice, W_q, W_k, W_v, W_out, b_out, temperature, out):
    ctx = ExitStack()
    with ctx:
        def sem(name):
            return ctx.enter_context(nc.semaphore(name))

        def row(v):
            return v.rearrange("(a d) -> a d", a=1)

        bank = [ctx.enter_context(nc.psum_tensor(f"bank{i}", [128, 512], F32)) for i in range(8)]
        X = ctx.enter_context(nc.sbuf_tensor("X", [R, T, D], F32))
        BIG_W = T * INNER
        REST_W = 14400
        big = ctx.enter_context(nc.sbuf_tensor("big", [128, BIG_W], F32))
        rest = ctx.enter_context(nc.sbuf_tensor("rest", [128, REST_W], F32))

        table = nc.dram_tensor("node_table", [N, TW], F32, kind="Internal").ap()
        slots = nc.dram_tensor("edge_slots", [(ITEMS) * CH, 2], I32, kind="Internal").ap()

        keep = Arena(rest, 0, REST_W)
        ident = keep.take(128, 128)
        ones = keep.take(128, 128)
        iota_r = keep.take(128, 128)
        A12 = keep.take(R, T, 2)
        item_tile = keep.take(1, ITEMS + 1, dtype=I32)
        is_last = keep.take(R, ITEMS + 1)
        is_same = keep.take(R, ITEMS)
        rounds = keep.take(1, 1, dtype=I32)
        WT = keep.take(128, DC, D)
        gb_row = keep.take(1, D)
        a2min = keep.take(128, 1)
        rest_at = keep.at

        with ExitStack() as _:
            a = Arena(rest, rest_at, REST_W)
            payload = a.take(EP, EJ, 2, dtype=I32)
            place = a.take(EP, EJ, dtype=I32)
            before = a.take(128, 128)
            iota_i = a.take(128, 128, dtype=I32)
            counts = a.take(EP, T)
            signs = a.take(EP, TA + 1)
            below = a.take(EP, TA)
            first = a.take(EP, T)
            total = a.take(EP, T)
            chunks = a.take(EP, T)
            begun = a.take(EP, T)
            chunks_i = a.take(EP, T, dtype=I32)
            item_row = a.take(EP, ITEMS)
            in_use = a.take(1, MAX_ROUNDS)
            scal = a.take(1, 4)
            iota2 = a.take(128, ITEMS)
            iota2_i = a.take(128, ITEMS, dtype=I32)
            zero_row = a.take(1, 512)
            masks = a.take(EP, H, CW, dtype=U8)
            pick = a.take(EP, H, CW)
            b = Arena(big, 0, T * D)
            is_tile = b.take(EP, 2, EJ, dtype=U8)
            side = b.take(EP, 2, EJ, dtype=BF16)
            srci = b.take(EP, EJ, dtype=I32)
            dsti = b.take(EP, EJ, dtype=I32)
            srcf = b.take(EP, EJ)
            tile_i = b.take(EP, EJ, dtype=I32)
            tile_f = b.take(EP, EJ)
            scanned = b.take(EP, H, CW)
            one_row = b.take(EP, EJ)
            cmp = b.take(EP, ITEMS, T)
            empty = b.take(128, Q, 2, dtype=I32)

            edges_in, x_in, slots_empty = sem("edges_in"), sem("x_in"), sem("slots_empty")
            pool_made, empty_made = sem("pool_made"), sem("empty_made")
            rk = sem("rank_step")
            counted, prefixed, flags = sem("counted"), sem("prefixed"), sem("flags")
            to_count, signed = sem("to_count"), sem("signed")
            masked, scanned_s, picked, added = sem("masked"), sem("scanned"), sem("picked"), sem("added")
            carried, chunk_psum, place_ready = sem("carried"), sem("chunk_psum"), sem("place_ready")

            same_head = a.take(128, 128)
            slot_buf = a.take(EP, 2, SB, dtype=I32)
            edge_buf = a.take(EP, 2, SB, 2, dtype=I32)
            stats = a.take(R, T, 6)
            mean, var, rstd, shift = a.take(R, T), a.take(R, T), a.take(R, T), a.take(R, T)
            xn = a.take(R, 2, TW)
            xnT = a.take(128, 2, DC, R)
            kb, km, ks = a.take(R, D), a.take(R, D), a.take(R, D)
            qm, qr = a.take(128, DC, R), a.take(128, DC, R)
            qn = a.take(128, DC, R)
            mins = a.take(128, 4)
            b = Arena(big, 0, BIG_W)
            QT = b.take(128, DC, N)
            wq, wk, wv, wo = (b.take(128, DC, D) for _ in range(4))
            W = b.take(128, DC, D)
            wa = b.take(128, DC, 2)
            va = b.take(128, DC, 2)
            bq, gb = b.take(128, DC), b.take(128, DC)
            ba, ca = b.take(128, 2), b.take(128, 2)
            bk = b.take(R, D)
            bv, bo = b.take(1, D), b.take(1, D)
            kx = b.take(128, DC, D + 1)
            kxT = b.take(128, DC, D)
            ksum = b.take(1, D)
            kvT = b.take(128, DC, 128)
            M = b.take(128, DC, D)
            B = b.take(128, DC, 128)

            weights_in, mix_made, ra = sem("weights_in"), sem("mix_made"), sem("dve_setup_step")
            copied, scattered = [sem("copied0"), sem("copied1")], [sem("scattered0"), sem("scattered1")]
            va_psum, va_done, stats_done, std_done = sem("va_psum"), sem("va_done"), sem("stats_done"), sem("std_done")
            xn_done, xnT_psum, xnT_done = sem("xn_done"), sem("xnT_psum"), sem("xnT_done")
            av_psum, av_done, table_out = sem("av_psum"), sem("av_done"), [sem("table_out0"), sem("table_out1")]
            k_psum, kb_done, km_done, ke_done, ks_done = (sem(n) for n in ("k_psum", "kb_done", "km_done", "ke_done", "ks_done"))
            q_psum, qm_done, qe_done, q_done = (sem(n) for n in ("q_psum", "qm_done", "qe_done", "q_done"))
            kx_psum = sem("kx_psum")
            head_psum, head_done = sem("head_psum"), sem("head_done")
            norm_psum, norm_eps, norm_inv, qn_done = (sem(n) for n in ("norm_psum", "norm_eps", "norm_inv", "qn_done"))
            mix_psum, mixed = sem("mix_psum"), sem("mixed")

            with nc.Block() as block:
                @block.sync
                def _(sp):
                    sp.dma_start(srci, src.rearrange("(p j) -> p j", p=EP)).then_inc(edges_in, 16)
                    sp.dma_start(dsti, dst.rearrange("(p j) -> p j", p=EP)).then_inc(edges_in, 16)
                    sp.wait_ge(empty_made, 2)
                    sp.dma_start(slots.rearrange("(c p q) w -> p c (q w)", p=128, q=Q),
                                 empty.rearrange("p q w -> p (q w)").unsqueeze(1).to_broadcast([128, ITEMS, Q * 2])
                                 ).then_inc(slots_empty, 16)
                    xv = x.rearrange("(t p) d -> p t d", p=R)
                    for lo, hi in ((0, 112), (112, R)):
                        sp.dma_start(X[lo:hi], xv[lo:hi]).then_inc(x_in, 16)
                    def chunked(w):
                        return w.rearrange("(c p) n -> p c n", p=128)

                    def column(v):
                        return v.rearrange("(c p) -> p c", p=128)

                    loads = [(wq, chunked(mix_wq)), (wk, chunked(mix_wk)), (wv, chunked(mix_wv)), (wo, chunked(mix_wo)),
                             (W, chunked(gnn_W)), (wa[:, :, 0], column(gnn_wa1.rearrange("a d -> (a d)"))),
                             (wa[:, :, 1], column(gnn_wa2.rearrange("a d -> (a d)"))), (bq, column(mix_bq)),
                             (gb, column(gnn_b)), (ba[:, 0:1], row(gnn_ba1).to_broadcast([128, 1])),
                             (ba[:, 1:2], row(gnn_ba2).to_broadcast([128, 1])),
                             (gb_row, row(gnn_b)), (bk, row(mix_bk).to_broadcast([R, D])), (bv, row(mix_bv)), (bo, row(mix_bo))]
                    with nc.allow_non_contiguous_dma(reason="columns of small vectors"):
                        for to, of in loads:
                            sp.dma_start(to, of).then_inc(weights_in, 16)
                    assert len(loads) == 15
                    with sp.Fori(0, T // 2) as k:
                        for u in range(2):
                            t = 2 * k + u
                            sp.wait_ge(av_done, 2 * t + 2)
                            sp.dma_start(table[bass.ds(t * R, R), :], xn[:, u]).then_inc(table_out[u], 16)
                    for u in range(2):
                        sp.wait_ge(table_out[u], 16 * (T // 2))

                @block.gpsimd
                def _(pool):
                    pool.iota(iota_i, [[1, 128]], base=0, channel_multiplier=0).then_inc(pool_made, 1)
                    pool.iota(iota2_i, [[1, ITEMS]], base=0, channel_multiplier=0).then_inc(pool_made, 1)
                    pool.memset(ident, 0.0).then_inc(pool_made, 1)
                    pool.memset(before, 1.0).then_inc(pool_made, 1)
                    pool.memset(ones, 1.0).then_inc(pool_made, 1)
                    pool.wait_ge(pool_made, 5)
                    pool.affine_select(out=ident, in_=ident, compare_op=ALU.not_equal, fill=1.0, base=0,
                                       pattern=[[-1, 128]], channel_multiplier=1).then_inc(pool_made, 1)
                    pool.affine_select(out=before, in_=before, compare_op=ALU.is_gt, fill=0.0, base=0,
                                       pattern=[[1, 128]], channel_multiplier=-1).then_inc(pool_made, 1)
                    pool.memset(empty[:, :, 0], 0).then_inc(empty_made, 1)
                    pool.memset(empty[:, :, 1], NOBODY).then_inc(empty_made, 1)
                    pool.memset(zero_row, 0.0).then_inc(mix_made, 1)
                    pool.memset(same_head, 0.0).then_inc(mix_made, 1)
                    pool.wait_ge(mix_made, 2)
                    for h in range(128 // HD):
                        pool.memset(same_head[h * HD:(h + 1) * HD, h * HD:(h + 1) * HD], 1.0).then_inc(mix_made, 1)
                    pool.wait_ge(mix_made, 2 + 128 // HD)
                    pool.wait_ge(slots_empty, 16)
                    with pool.Fori(0, EJ // (2 * SB)) as k:
                        for u in range(2):
                            at = (2 * k + u) * SB
                            pool.wait_ge(place_ready, k + 1)
                            pool.wait_ge(scattered[u], 16 * SB * k)
                            pool.tensor_copy(slot_buf[:, u], place[:, bass.ds(at, SB)]).then_inc(copied[u], 1)
                            pool.tensor_copy(edge_buf[:, u], payload[:, bass.ds(at, SB), :]).then_inc(copied[u], 1)
                            pool.wait_ge(copied[u], 2)
                            pool.sem_clear(copied[u])
                            for j in range(SB):
                                pool.indirect_dma_start(
                                    slots, bass.IndirectOffsetOnAxis(ap=slot_buf[:, u, j:j + 1], axis=0),
                                    edge_buf[:, u, j, :], None).then_inc(scattered[u], 16)
                    for u in range(2):
                        pool.wait_ge(scattered[u], 16 * EJ // 2)

                @block.tensor
                def _(pe):
                    pe.wait_ge(pool_made, 7)
                    pe.wait_ge(counted, 3 + T - TA)
                    pe.matmul(bank[0][0:EP, 0:T], before[0:EP, 0:EP], counts, start=True, stop=True)
                    pe.matmul(bank[1][0:EP, 0:T], ones[0:EP, 0:EP], counts, start=True, stop=True).then_inc(prefixed, 1)
                    pe.wait_ge(mix_made, 2)
                    for c, (lo, hi) in enumerate(zip(CHUNKS, CHUNKS[1:])):
                        w = hi - lo
                        sums = bank[4 + c % 2][0:EP, 0:w]
                        if c >= 2:
                            pe.wait_ge(place_ready, CHUNKS[c - 1] // (2 * SB))
                        pe.matmul(sums, zero_row[:, 0:EP], zero_row[:, 0:w], start=True, stop=False,
                                  skip_group_check=True)
                        with pe.Fori(0, T // H) as k:
                            for h in range(H):
                                pe.wait_ge(picked, c * T + H * k + (h + 1))
                                pe.matmul(sums, ident[0:EP, 0:EP], pick[:, h, 0:w], start=False, stop=False,
                                          skip_group_check=True).then_inc(added, 1)
                        pe.matmul(sums, zero_row[:, 0:EP], zero_row[:, 0:w], start=False, stop=True,
                                  skip_group_check=True).then_inc(chunk_psum, 1)
                    pe.wait_ge(weights_in, 16 * 15)
                    for c in range(DC):
                        for o in range(DC):
                            pe.matmul(bank[0][:, 2 * c:2 * c + 2], W[:, o, c * 128:(c + 1) * 128], wa[:, o, :],
                                      start=o == 0, stop=o == DC - 1)
                    for o in range(DC):
                        mm = pe.matmul(bank[0][:, 8:10], gb[:, o:o + 1].to_broadcast([128, 128]), wa[:, o, :],
                                       start=o == 0, stop=o == DC - 1)
                    mm.then_inc(va_psum, 1)
                    for o in range(DC):
                        for c in range(DC):
                            mm = pe.transpose(bank[1][:, (c * DC + o) * 128:(c * DC + o + 1) * 128],
                                              W[:, o, c * 128:(c + 1) * 128], ident)
                    mm.then_inc(va_psum, 1)
                    pe.wait_ge(mix_made, 2)
                    for c in range(DC):
                        pe.matmul(bank[6 + c][:, 0:D + 1], zero_row[:, 0:128], zero_row[:, 0:D + 1], start=True,
                                  stop=False, skip_group_check=True)
                    pe.wait_ge(va_done, 3)

                    def turn(t, u):
                        pe.wait_ge(xn_done, t + 1)
                        for c in range(DC):
                            mm = pe.transpose(bank[0][:, c * R:(c + 1) * R], xn[:, u, c * 128:(c + 1) * 128],
                                              ident[0:R, 0:R])
                        mm.then_inc(xnT_psum, 1)

                    def project(t, u, ahead):
                        pe.wait_ge(xnT_done, t + 1)
                        pe.wait_ge(av_done, 2 * t)
                        for c in range(DC):
                            mm = pe.matmul(bank[1][0:R, 0:2], xnT[:, u, c, :], va[:, c, :], start=c == 0,
                                           stop=c == DC - 1)
                        mm.then_inc(av_psum, 1)
                        pe.wait_ge(kb_done, t)
                        for c in range(DC):
                            mm = pe.matmul(bank[2][0:R, 0:D], xnT[:, u, c, :], wk[:, c, :], start=c == 0,
                                           stop=c == DC - 1)
                        mm.then_inc(k_psum, 1)
                        if ahead:
                            turn(t + 1, 1 - u)
                        pe.wait_ge(qm_done, 2 * t)
                        pe.wait_ge(qe_done, 3 * t)
                        for i in range(DC):
                            for c in range(DC):
                                mm = pe.matmul(bank[3][:, i * R:(i + 1) * R], wq[:, c, i * 128:(i + 1) * 128],
                                               xnT[:, u, c, :], start=c == 0, stop=c == DC - 1)
                        mm.then_inc(q_psum, 1)
                        pe.wait_ge(ks_done, t + 1)
                        for c in range(DC):
                            mm = pe.matmul(bank[6 + c][:, 0:D + 1], ks[:, c * 128:(c + 1) * 128], xn[:, u, 0:D + 1],
                                           start=False, stop=False, skip_group_check=True)
                        mm.then_inc(kx_psum, 1)

                    turn(0, 0)
                    with pe.Fori(0, T // 2 - 1) as k:
                        for u in range(2):
                            project(2 * k + u, u, True)
                    for t in range(T - 2, T):
                        project(t, t % 2, t < T - 1)
                    for c in range(DC):
                        mm = pe.matmul(bank[6 + c][:, 0:D + 1], zero_row[:, 0:128], zero_row[:, 0:D + 1], start=False,
                                       stop=True, skip_group_check=True)
                    mm.then_inc(head_psum, 1)
                    pe.wait_ge(head_done, 2)
                    for i in range(DC):
                        for c in range(DC):
                            pe.transpose(bank[0][:, (c * DC + i) * 128:(c * DC + i + 1) * 128],
                                         kx[:, i, c * 128:(c + 1) * 128], ident)
                        mm = pe.transpose(bank[1][0:1, i * 128:(i + 1) * 128], kx[:, i, D:D + 1], ident)
                    mm.then_inc(head_psum, 1)
                    pe.wait_ge(head_done, 4)
                    for c in range(DC):
                        o = bank[2][:, c * 128:(c + 1) * 128]
                        for d in range(DC):
                            pe.matmul(o, wv[:, d, c * 128:(c + 1) * 128], kxT[:, d, c * 128:(c + 1) * 128],
                                      start=d == 0, stop=False)
                        mm = pe.matmul(o, bv[:, c * 128:(c + 1) * 128], ksum[:, c * 128:(c + 1) * 128],
                                       start=False, stop=True)
                    mm.then_inc(head_psum, 1)
                    pe.wait_ge(head_done, 8)
                    for c in range(DC):
                        mm = pe.matmul(bank[3][:, c * D:(c + 1) * D], kvT[:, c, :], wo[:, c, :], start=True, stop=True)
                    mm.then_inc(head_psum, 1)
                    pe.wait_ge(head_done, 9)

                    def norms(t, u):
                        for c in range(DC):
                            mm = pe.matmul(bank[3 * u][:, c * R:(c + 1) * R], B[:, c, :], QT[:, c, bass.ds(t * R, R)],
                                           start=True, stop=True)
                        mm.then_inc(norm_psum, 1)

                    def mix(t):
                        pe.wait_ge(mixed, t)
                        pe.wait_ge(qn_done, t + 1)
                        for c in range(DC):
                            pe.matmul(bank[1][0:R, 0:D], qn[:, c, :], M[:, c, :], start=c == 0, stop=False)
                        pe.matmul(bank[1][0:R, 0:D], ones[0:1, 0:R], bo, start=False, stop=True).then_inc(mix_psum, 1)

                    norms(0, 0)
                    with pe.Fori(0, T // 2 - 1) as k:
                        for u in range(2):
                            t = 2 * k + u
                            pe.wait_ge(norm_eps, t)
                            norms(t + 1, 1 - u)
                            mix(t)
                    pe.wait_ge(norm_eps, T - 2)
                    norms(T - 1, 1)
                    mix(T - 2)
                    mix(T - 1)
                    pe.wait_ge(head_done, 10)
                    pe.transpose(bank[2][0:1, 0:R], mins[0:R, 0:1], ident[0:R, 0:R]).then_inc(head_psum, 1)
                    pe.wait_ge(head_done, 11)
                    pe.matmul(bank[3][:, 0:1], ones[0:1, :], mins[0:1, 1:2], start=True, stop=True).then_inc(head_psum, 1)

                @block.scalar
                def _(act):
                    act.wait_ge(to_count, 2)
                    act.copy(side[:, 0, 0:1], below[:, 0:1]).then_inc(signed, 1)
                    act.copy(side[:, 1, 0:1], below[:, 0:1]).then_inc(signed, 1)
                    with act.Fori(0, TA // 2) as k:
                        for half in range(2):
                            t = 2 * k + half
                            act.wait_ge(signed, t + 1)
                            act.activation(side[:, half, :], tile_f, ACT.Sign, bias=below[:, bass.ds(t, 1)],
                                           accum_out=signs[:, bass.ds(t + 1, 1)]).then_inc(signed, 1)
                    for c, (lo, hi) in enumerate(zip(CHUNKS[:-1], CHUNKS[1:-1])):
                        with act.Fori(0, T // H) as k:
                            for h in range(H):
                                t = H * k + h
                                act.wait_ge(scanned_s, c * T + t + 1)
                                act.copy(first[:, bass.ds(t, 1)], scanned[:, h, hi - lo - 1:hi - lo]).then_inc(carried, 1)
                    act.wait_ge(stats_done, 1)
                    act.activation(rstd, var, ACT.Sqrt).then_inc(std_done, 1)

                    def turned(t, u):
                        act.wait_ge(xnT_psum, t + 1)
                        act.copy(xnT[:, u].rearrange("p c r -> p (c r)"), bank[0][:, 0:DC * R]).then_inc(xnT_done, 1)

                    def k_and_q(t, u, ahead):
                        if ahead:
                            act.wait_ge(q_psum, t)
                            turned(t + 1, 1 - u)
                        act.wait_ge(km_done, t + 1)
                        act.activation(km, km, ACT.Exp).then_inc(ke_done, 1)
                        act.wait_ge(q_done, t)
                        act.wait_ge(qm_done, 2 * t + 2)
                        for c in range(DC):
                            act.activation(qr[:, c, :], bank[3][:, c * R:(c + 1) * R], ACT.Relu,
                                           bias=bq[:, c:c + 1]).then_inc(qe_done, 1)
                        act.activation(qm.rearrange("p c r -> p (c r)"), qm.rearrange("p c r -> p (c r)"),
                                       ACT.Exp).then_inc(qe_done, 1)

                    turned(0, 0)
                    with act.Fori(0, T // 2 - 1) as k:
                        for u in range(2):
                            k_and_q(2 * k + u, u, True)
                    for t in range(T - 2, T):
                        k_and_q(t, t % 2, t < T - 1)

                @block.vector
                def _(dve):
                    n = [0]

                    def step(ins):
                        n[0] += 1
                        ins.then_inc(rk, 1)
                        dve.wait_ge(rk, n[0])

                    dve.wait_ge(pool_made, 5)
                    step(dve.tensor_copy(iota_r, iota_i))
                    step(dve.tensor_copy(iota2, iota2_i))
                    dve.memset(one_row, 1.0).then_inc(counted, 2)
                    dve.wait_ge(edges_in, 32)
                    step(dve.tensor_copy(srcf, srci))
                    step(dve.tensor_scalar(tile_i, srcf, 1.0 / R, 0.5 / R - 0.5, ALU.mult, ALU.add))
                    step(dve.tensor_copy(tile_f, tile_i))
                    step(dve.scalar_tensor_tensor(payload[:, :, 1], tile_f, -float(R), srcf, ALU.mult, ALU.add))
                    step(dve.tensor_copy(payload[:, :, 0], dsti))
                    dve.memset(signs[:, 0:1], float(EJ)).then_inc(to_count, 1)
                    dve.tensor_scalar(below, iota_r[0:EP, 0:TA], -1.0, -0.5, ALU.mult, ALU.add).then_inc(to_count, 1)
                    with dve.Fori(0, (T - TA) // 2) as k:
                        for half in range(2):
                            t = 2 * k + half
                            dve.wait_ge(counted, t + 1)
                            dve.tensor_scalar(is_tile[:, half, :], tile_f, iota_r[0:EP, bass.ds(t + TA, 1)], 0.0,
                                              ALU.is_equal, ALU.add, accum_out=counts[:, bass.ds(t + TA, 1)]
                                              ).then_inc(counted, 1)
                    dve.wait_ge(signed, TA + 2)
                    step(dve.tensor_tensor(counts[:, 0:TA], signs[:, 0:TA], signs[:, 1:TA + 1], ALU.subtract))
                    dve.tensor_scalar(counts[:, 0:TA], counts[:, 0:TA], 0.5, None, ALU.mult).then_inc(counted, 1)
                    dve.wait_ge(prefixed, 1)
                    step(dve.tensor_copy(first, bank[0][0:EP, 0:T]))
                    step(dve.tensor_copy(total, bank[1][0:EP, 0:T]))
                    step(dve.tensor_scalar(chunks_i, total, 1.0 / CH, 0.5 - 0.5 / CH, ALU.mult, ALU.add))
                    step(dve.tensor_copy(chunks, chunks_i))
                    step(dve.tensor_scalar(chunks, chunks, 1.0, None, ALU.max))
                    step(dve.tensor_tensor_scan(begun, one_row[:, 0:T], chunks, 0.0, ALU.mult, ALU.add))
                    step(dve.tensor_tensor(total, begun, chunks, ALU.subtract))
                    step(dve.tensor_scalar(total, total, float(CH), -1.0, ALU.mult, ALU.add))
                    step(dve.tensor_tensor(first, first, total, ALU.add))
                    dve.memset(pick, 0.0).then_inc(added, H)
                    for c, (lo, hi) in enumerate(zip(CHUNKS, CHUNKS[1:])):
                        w = hi - lo
                        tiles = tile_f[:, lo:hi]
                        if c:
                            dve.wait_ge(carried, c * T)
                        with dve.Fori(0, T // H) as k:
                            g = c * T + H * k
                            dve.wait_ge(picked, g)
                            for h in range(H):
                                dve.tensor_scalar(masks[:, h, 0:w], tiles, iota_r[0:EP, bass.ds(H * k + h, 1)], None,
                                                  ALU.is_equal).then_inc(masked, 1)
                            if hi < EJ:
                                dve.wait_ge(carried, g)
                            for h in range(H):
                                dve.wait_ge(masked, g + (h + 1))
                                dve.tensor_tensor_scan(scanned[:, h, 0:w], one_row[:, 0:w], masks[:, h, 0:w],
                                                       first[:, bass.ds(H * k + h, 1)], ALU.mult,
                                                       ALU.add).then_inc(scanned_s, 1)
                            for h in range(H):
                                dve.wait_ge(scanned_s, g + (h + 1))
                                dve.wait_ge(added, g + (h + 1))
                                dve.tensor_tensor(pick[:, h, 0:w], masks[:, h, 0:w], scanned[:, h, 0:w],
                                                  ALU.mult).then_inc(picked, 1)
                        dve.wait_ge(chunk_psum, c + 1)
                        dve.tensor_copy(place[:, lo:hi], bank[4 + c % 2][0:EP, 0:w]
                                        ).then_inc(place_ready, w // (2 * SB))
                    step(dve.tensor_tensor(cmp, begun.unsqueeze(1).to_broadcast([EP, ITEMS, T]),
                                           iota2[0:EP].unsqueeze(2).to_broadcast([EP, ITEMS, T]), ALU.is_le))
                    step(dve.tensor_reduce(item_row, cmp, AX, ALU.add))
                    dve.memset(is_same[:, 0:1], 0.0).then_inc(flags, 1)
                    dve.memset(is_last[:, 0:1], 0.0).then_inc(flags, 1)
                    dve.memset(item_tile[:, 0:1], 0).then_inc(flags, 1)
                    dve.tensor_tensor(is_same[:, 1:ITEMS], item_row[:, 1:ITEMS], item_row[:, 0:ITEMS - 1],
                                      ALU.is_equal).then_inc(flags, 1)
                    dve.tensor_tensor(is_last[:, 1:ITEMS], item_row[:, 0:ITEMS - 1], item_row[:, 1:ITEMS],
                                      ALU.is_lt).then_inc(flags, 1)
                    dve.tensor_scalar(is_last[:, ITEMS:ITEMS + 1], item_row[:, ITEMS - 1:ITEMS], float(T), None,
                                      ALU.is_lt).then_inc(flags, 1)
                    dve.tensor_scalar(item_tile[:, 1:ITEMS + 1], item_row[0:1], float(T - 1), None,
                                      ALU.min).then_inc(flags, 1)
                    step(dve.tensor_scalar(in_use, iota2[0:1, 0:MAX_ROUNDS], float(U), float(TAIL), ALU.mult, ALU.add))
                    step(dve.tensor_scalar(in_use, in_use, begun[0:1, T - 1:T], None, ALU.is_lt))
                    step(dve.tensor_reduce(scal[:, 0:1], in_use, AX, ALU.add))
                    step(dve.tensor_copy(rounds, scal[:, 0:1]))
                    dve.wait_ge(flags, 7)
                    dve.wait_ge(x_in, 32)
                    with dve.Fori(0, T) as t:
                        dve.bn_stats(stats[:, t, :], X[:, t, :]).then_inc(ra, 1)
                    dve.wait_ge(ra, T)
                    mo, me = stats[:, :, 4], stats[:, :, 1]
                    step(dve.tensor_tensor(mean, me, mo, ALU.add))
                    step(dve.tensor_tensor(shift, me, mo, ALU.subtract))
                    step(dve.tensor_scalar(mean, mean, 0.5, None, ALU.mult))
                    step(dve.tensor_tensor(shift, shift, shift, ALU.mult))
                    step(dve.tensor_tensor(var, stats[:, :, 2], stats[:, :, 5], ALU.add))
                    step(dve.tensor_scalar(var, var, 1.0 / D, LN_EPS, ALU.mult, ALU.add))
                    step(dve.scalar_tensor_tensor(var, shift, 0.25, var, ALU.mult, ALU.add))
                    dve.memset(xn[:, :, D], 1.0).then_inc(stats_done, 1)
                    dve.wait_ge(std_done, 1)
                    step(dve.reciprocal(rstd, rstd))
                    step(dve.tensor_tensor(shift, rstd, rstd, ALU.mult))
                    step(dve.tensor_tensor(shift, shift, var, ALU.mult))
                    step(dve.tensor_scalar(shift, shift, -0.5, 1.5, ALU.mult, ALU.add))
                    step(dve.tensor_tensor(rstd, rstd, shift, ALU.mult))
                    step(dve.scalar_tensor_tensor(shift, mean, -1.0, rstd, ALU.mult, ALU.mult))
                    dve.wait_ge(va_psum, 1)
                    dve.tensor_copy(va.rearrange("p c w -> p (c w)"), bank[0][:, 0:2 * DC]).then_inc(va_done, 1)
                    dve.tensor_tensor(ca, bank[0][:, 8:10], ba, ALU.add).then_inc(va_done, 1)
                    dve.wait_ge(va_psum, 2)
                    dve.tensor_copy(WT.rearrange("p c n -> p (c n)"), bank[1][:, :]).then_inc(va_done, 1)

                    def normalise(t, u):
                        dve.tensor_scalar(xn[:, u, 0:D], X[:, t, :], rstd[:, bass.ds(t, 1)], shift[:, bass.ds(t, 1)],
                                          ALU.mult, ALU.add).then_inc(xn_done, 1)

                    def k_and_q(t, u):
                        dve.wait_ge(av_psum, t + 1)
                        dve.tensor_tensor(A12[:, t, :], bank[1][0:R, 0:2], ca[0:R], ALU.add).then_inc(av_done, 1)
                        dve.wait_ge(av_done, 2 * t + 1)
                        dve.tensor_copy(xn[:, u, D + 1:D + 2], A12[:, t, 1:2]).then_inc(av_done, 1)
                        dve.wait_ge(k_psum, t + 1)
                        dve.tensor_tensor(kb, bank[2][0:R, 0:D], bk, ALU.add).then_inc(kb_done, 1)
                        dve.wait_ge(kb_done, t + 1)
                        dve.tensor_scalar(km, kb, 0.0, None, ALU.min).then_inc(km_done, 1)
                        dve.wait_ge(q_psum, t + 1)
                        dve.wait_ge(q_done, t)
                        for c in range(DC):
                            dve.tensor_scalar(qm[:, c, :], bank[3][:, c * R:(c + 1) * R], bq[:, c:c + 1], 0.0,
                                              ALU.add, ALU.min).then_inc(qm_done, 1)
                        dve.wait_ge(ke_done, t + 1)
                        dve.scalar_tensor_tensor(ks, kb, 0.0, km, ALU.max, ALU.add).then_inc(ks_done, 1)
                        dve.wait_ge(qe_done, 3 * t + 3)
                        dve.tensor_tensor(QT[:, :, bass.ds(t * R, R)], qr, qm, ALU.add).then_inc(q_done, 1)

                    normalise(0, 0)
                    with dve.Fori(0, T // 2 - 1) as k:
                        for u in range(2):
                            t = 2 * k + u
                            dve.wait_ge(table_out[1 - u], 16 * k + (16 if u else 0))
                            dve.wait_ge(kx_psum, t)
                            normalise(t + 1, 1 - u)
                            k_and_q(t, u)
                    dve.wait_ge(table_out[1], 16 * (T // 2 - 1))
                    dve.wait_ge(kx_psum, T - 2)
                    normalise(T - 1, 1)
                    k_and_q(T - 2, 0)
                    dve.wait_ge(kx_psum, T - 1)
                    k_and_q(T - 1, 1)
                    dve.wait_ge(head_psum, 1)
                    for c in range(DC):
                        dve.tensor_copy(kx[:, c, :], bank[6 + c][:, 0:D + 1]).then_inc(head_done, 1)
                    dve.wait_ge(head_psum, 2)
                    dve.tensor_copy(kxT.rearrange("p c n -> p (c n)"), bank[0][:, :]).then_inc(head_done, 1)
                    dve.tensor_copy(ksum, bank[1][0:1, 0:D]).then_inc(head_done, 1)
                    dve.wait_ge(mix_made, 2 + 128 // HD)
                    dve.wait_ge(head_psum, 3)
                    for c in range(DC):
                        dve.tensor_tensor(kvT[:, c, :], bank[2][:, c * 128:(c + 1) * 128], same_head,
                                          ALU.mult).then_inc(head_done, 1)
                    for c in range(DC):
                        dve.tensor_scalar(B[:, c, :], same_head, kx[:, c, D:D + 1], None, ALU.mult).then_inc(head_done, 1)
                    dve.wait_ge(head_psum, 4)
                    dve.tensor_copy(M.rearrange("p c n -> p (c n)"), bank[3][:, :]).then_inc(head_done, 1)

                    def inverses(t, u):
                        dve.wait_ge(norm_psum, t + 1)
                        dve.wait_ge(qn_done, t)
                        dve.tensor_scalar(qr.rearrange("p c r -> p (c r)"), bank[3 * u][:, 0:DC * R], NORM_EPS, None,
                                          ALU.add).then_inc(norm_eps, 1)
                        dve.wait_ge(norm_eps, t + 1)
                        dve.reciprocal(qr, qr).then_inc(norm_inv, 1)

                    def divide(t):
                        dve.wait_ge(norm_inv, t + 1)
                        dve.tensor_tensor(qn, QT[:, :, bass.ds(t * R, R)], qr, ALU.mult).then_inc(qn_done, 1)

                    def add(t):
                        dve.wait_ge(mix_psum, t + 1)
                        dve.tensor_tensor(X[:, t, :], X[:, t, :], bank[1][0:R, 0:D], ALU.add).then_inc(mixed, 1)

                    inverses(0, 0)
                    divide(0)
                    with dve.Fori(0, T // 2 - 1) as k:
                        for u in range(2):
                            t = 2 * k + u
                            inverses(t + 1, 1 - u)
                            add(t)
                            divide(t + 1)
                    inverses(T - 1, 1)
                    add(T - 2)
                    divide(T - 1)
                    add(T - 1)
                    dve.tensor_reduce(mins[0:R, 0:1], A12[:, :, 1], AX, ALU.min).then_inc(head_done, 1)
                    dve.wait_ge(head_psum, 5)
                    dve.tensor_reduce(mins[0:1, 1:2], bank[2][0:1, 0:R], AX, ALU.min).then_inc(head_done, 1)
                    dve.wait_ge(head_psum, 6)
                    dve.tensor_scalar(a2min, bank[3][:, 0:1], -1.0, None, ALU.add).then_inc(head_done, 1)

        a = Arena(rest, rest_at, REST_W)
        stats2 = a.take(R, T, 6)
        WL = a.take(128, DC, INNER)
        bL = a.take(R, INNER)
        after_stats = a.at
        with ExitStack() as _:
            b = Arena(big, 0, BIG_W)
            Gt = b.take(128, U, Q * TW)
            V = b.take(128, U, Q, R)
            own_T = b.take(R, Q * 128, dtype=BF16)
            item = a.take(128, U, Q * 2, dtype=I32)
            score, local = a.take(128, U, Q), a.take(128, U, Q)
            most = a.take(128, R)
            WxT, Wx = a.take(G, FH, D), a.take(128, DC, INNER)
            Wsl, bx, bsl, temp = a.take(G, G), a.take(G, FH), a.take(128, G), a.take(128, FH)
            fw_in, fw_psum, fw_done = sem("fw_in"), sem("fw_psum"), sem("fw_done")
            old, new, zn, zo, mo, fade, keepf = (a.take(R, 1) for _ in range(7))
            base = a.take(R, T)
            cm = a.take(R, 2)
            left = a.take(R, 2)
            parts = a.take(R, 3, 2, dtype=BF16)
            ident16 = a.take(128, 128, dtype=BF16)
            cm_e = a.take(128, Q, 2)
            z, weight = a.take(128, Q), a.take(128, Q)
            AGG = a.take(R, D + 1)
            An, AnT, flagT = a.take(R, D + 1), a.take(128, DC, R), a.take(1, R)
            sinv = a.take(R, 1)
            GROUPS = [range(g, min(g + 4, Q)) for g in range(0, Q, 4)]
            NG = len(GROUPS)
            PARTS = [range(8), range(8, Q)]
            assert NG == 5
            bT, bMost, bCM, bAgg, bAnT, bOut = (0, 1, 2), 3, 4, 5, 7, 6

            item_in, half_gathered, rest_gathered, half_used, used = ([sem(f"{n}{u}") for u in range(U)] for n in (
                "item_in", "half_gathered", "rest_gathered", "half_used", "used"))
            (s_set, s_score, s_v, s_most, s_mostT, s_small, s_fade, s_turned, s_cm, s_cme, s_z, s_exp, s_w, s_agg, s_an,
             s_anT, s_anTc, s_out, s_x, s_stat, s_fin) = (sem(n) for n in (
                 "set_up", "scored", "v_built", "most_done", "most_turned", "small_step", "fade_done", "own_turned",
                 "cm_psum", "cm_copied", "z_step", "exp_done", "w_built", "agg_step", "an_step", "anT_psum", "anT_copied",
                 "out_psum", "x_added", "stat_done", "final_step"))
            v_turned, marked, s_temp = sem("v_turned"), sem("marked"), sem("temp_step")
            mark = a.take(1, 1)
            SM, SZ, SA = 13, 4, 3

            with nc.Block() as block:
                @block.sync
                def _(sp):
                    with nc.allow_non_contiguous_dma(reason="columns of small vectors"):
                        sp.dma_start(Wx, W_x.rearrange("(c p) n -> p c n", p=128)).then_inc(fw_in, 16)
                        sp.dma_start(Wsl, W_slice).then_inc(fw_in, 16)
                        sp.dma_start(bx, b_x.rearrange("(h j) -> j h", h=FH)).then_inc(fw_in, 16)
                        sp.dma_start(bsl, row(b_slice).to_broadcast([128, G])).then_inc(fw_in, 16)
                        sp.dma_start(temp, temperature.rearrange("a h b c -> (a b c) h").to_broadcast([128, FH])
                                     ).then_inc(fw_in, 16)
                    more = sp.value_load(rounds, min_val=MIN_ROUNDS, max_val=MAX_ROUNDS)
                    view = slots.rearrange("(c p q) w -> c p (q w)", p=128, q=Q)

                    def load(i, u):
                        sp.wait_ge(s_score, 3 * i)
                        sp.dma_start(item[:, u, :], view[bass.ds(i, 1)].rearrange("c p f -> (c p) f")
                                     ).then_inc(item_in[u], 16)

                    with sp.Fori(0, more) as k:
                        for u in range(U):
                            load(U * k + u, u)
                    for u in range(TAIL):
                        load(U * more + u, u)

                @block.gpsimd
                def _(pool):
                    more = pool.value_load(rounds, min_val=MIN_ROUNDS, max_val=MAX_ROUNDS)
                    def gather(k, u):
                        for part, (freed, gathered) in enumerate(((half_used, half_gathered), (used, rest_gathered))):
                            pool.wait_ge(freed[u], k + 1)
                            pool.wait_ge(marked, 2 * (U * k + u) + part)
                            pool.tensor_tensor(mark, iota_r[0:1, 0:1], iota_r[0:1, 0:1], ALU.add).then_inc(marked, 1)
                            if part == 0:
                                pool.wait_ge(item_in[u], 16)
                                pool.sem_clear(item_in[u])
                            for q in PARTS[part]:
                                pool.indirect_dma_start(
                                    Gt[:, u, q * TW:(q + 1) * TW], None, table,
                                    bass.IndirectOffsetOnAxis(ap=item[:, u, 2 * q:2 * q + 1], axis=0)
                                ).then_inc(gathered[u], 16)

                    with pool.Fori(0, more) as k:
                        for u in range(U):
                            gather(k, u)
                    for u in range(TAIL):
                        gather(more, u)

                @block.tensor
                def _(pe):
                    more = pe.value_load(rounds, min_val=MIN_ROUNDS, max_val=MAX_ROUNDS)
                    pe.wait_ge(fw_in, 80)
                    for h in range(FH):
                        for c in range(DC):
                            i = h * DC + c
                            mm = pe.transpose(bank[i // 4][0:G, (i % 4) * 128:(i % 4 + 1) * 128],
                                              Wx[:, c, h * G:(h + 1) * G], ident)
                    mm.then_inc(fw_psum, 1)
                    pe.wait_ge(fw_done, 4)
                    for c in range(DC):
                        for h in range(FH):
                            pe.matmul(bank[4 + c][:, h * G:(h + 1) * G], WxT[:, h, c * 128:(c + 1) * 128], Wsl,
                                      start=True, stop=True)
                    for h in range(FH):
                        mm = pe.matmul(bank[6][:, h * G:(h + 1) * G], bx[:, h:h + 1].to_broadcast([G, 128]), Wsl,
                                       start=True, stop=True)
                    mm.then_inc(fw_psum, 1)
                    pe.wait_ge(fw_done, 8)
                    bank16 = [bank[i][0:R, 0:256].bitcast(BF16) for i in bT]

                    def upper(ap):
                        return ap.bitcast(BF16).rearrange("p (r w) -> p r w", w=2)[:, :, 1]

                    pe.wait_ge(s_set, 4)

                    def turn(i, u):
                        free = [NG * i + NG - 1, NG * i + NG, NG * i + NG, NG * i + NG + 1, NG * i + NG + 2]
                        for g, qs in enumerate(GROUPS):
                            pe.wait_ge(s_turned, free[g])
                            pe.wait_ge(s_v, Q * i + (qs[-1] + 1))
                            for j, q in enumerate(qs):
                                mm = pe.transpose(bank16[g % 3][:, j * 128:(j + 1) * 128], upper(V[:, u, q, :]), ident16)
                            mm.then_inc(v_turned, 1)

                    def turn_largest(i):
                        pe.wait_ge(s_most, i + 1)
                        pe.transpose(bank[bMost][0:R, 0:128], most, ident).then_inc(s_mostT, 1)

                    def spread(i):
                        pe.wait_ge(s_turned, NG * i + 2 * NG)
                        pe.wait_ge(s_small, SM * i + SM)
                        pe.wait_ge(s_cme, i)
                        for q in range(Q):
                            mm = pe.matmul(bank[bCM][:, 6 * q:6 * q + 6], own_T[:, q * 128:(q + 1) * 128],
                                           parts.rearrange("p s w -> p (s w)"), start=True, stop=True)
                        mm.then_inc(s_cm, 1)

                    def into_x(i):
                        pe.wait_ge(s_an, SA * i + SA)
                        pe.wait_ge(s_anTc, 2 * i)
                        for c in range(DC):
                            pe.transpose(bank[bAnT][:, c * R:(c + 1) * R], An[:, c * 128:(c + 1) * 128], ident[0:R, 0:R])
                        pe.transpose(bank[bAnT][0:1, 256:256 + R], An[:, D:D + 1], ident[0:R, 0:R]).then_inc(s_anT, 1)

                    def out_x(i):
                        pe.wait_ge(s_anTc, 2 * i + 2)
                        pe.wait_ge(s_x, i)
                        for c in range(DC):
                            pe.matmul(bank[bOut][0:R, 0:D], AnT[:, c, :], WT[:, c, :], start=c == 0, stop=False)
                        pe.matmul(bank[bOut][0:R, 0:D], flagT, gb_row, start=False, stop=True).then_inc(s_out, 1)

                    def sum_edges(i, u, groups):
                        for qs in groups:
                            pe.wait_ge(s_w, Q * (i + 1) + (qs[-1] + 1))
                            for q in qs:
                                mm = pe.matmul(bank[bAgg][0:R, 0:D + 1], V[:, u, q, :],
                                               Gt[:, u, q * TW:q * TW + D + 1], start=q == 0, stop=q == Q - 1)
                            if qs[-1] == PARTS[0][-1]:
                                mm.then_inc(half_used[u], 1)
                            if qs[-1] == Q - 1:
                                mm.then_inc(used[u], 1)

                    def step(i, u, ahead):
                        spread(i)
                        if ahead:
                            turn(i + 1, (u + 1) % U)
                        into_x(i)
                        out_x(i)
                        if ahead:
                            turn_largest(i + 1)
                        sum_edges(i, u, GROUPS)

                    sum_edges(-1, U - 1, GROUPS)
                    turn(0, 0)
                    turn_largest(0)
                    with pe.Fori(0, more) as k:
                        for u in range(U):
                            step(U * k + u, u, True)
                    for u in range(TAIL):
                        step(U * more + u, u, u < TAIL - 1)
                    into_x(U * more + TAIL)
                    out_x(U * more + TAIL)

                @block.scalar
                def _(act):
                    more = act.value_load(rounds, min_val=MIN_ROUNDS, max_val=MAX_ROUNDS)

                    def turned(i):
                        act.wait_ge(s_cm, i)
                        for g, qs in enumerate(GROUPS):
                            w = 128 * len(qs)
                            act.wait_ge(v_turned, NG * i + (g + 1))
                            act.activation(own_T[:, g * 512:g * 512 + w], bank[bT[g % 3]][0:R, 0:256].bitcast(BF16)[:, 0:w],
                                           ACT.Sign).then_inc(s_turned, 1)

                    def turn_sums(i):
                        act.wait_ge(s_anT, i + 1)
                        act.wait_ge(s_out, i)
                        act.copy(AnT.rearrange("p c r -> p (c r)"), bank[bAnT][:, 0:DC * R]).then_inc(s_anTc, 1)
                        act.copy(flagT, bank[bAnT][0:1, 256:256 + R]).then_inc(s_anTc, 1)

                    def step(i, u, ahead):
                        act.wait_ge(s_small, SM * i + SM)
                        act.activation(fade, mo, ACT.Exp).then_inc(s_fade, 1)
                        if ahead:
                            turned(i + 1)
                        turn_sums(i)
                        act.wait_ge(s_z, SZ * i + SZ)
                        act.activation(weight, z, ACT.Exp).then_inc(s_exp, 1)

                    turned(0)
                    with act.Fori(0, more) as k:
                        for u in range(U):
                            step(U * k + u, u, True)
                    for u in range(TAIL):
                        step(U * more + u, u, u < TAIL - 1)
                    turn_sums(U * more + TAIL)

                @block.vector
                def _(dve):
                    more = dve.value_load(rounds, min_val=MIN_ROUNDS, max_val=MAX_ROUNDS)
                    dve.memset(keepf, 0.0).then_inc(used[0], 1)
                    dve.memset(sinv, 0.0).then_inc(used[1], 1)
                    dve.memset(old, 0.0).then_inc(half_used[0], 1)
                    dve.memset(zo, 0.0).then_inc(half_used[1], 1)
                    dve.memset(most, 0.0).then_inc(s_score, 3 * (U - 1))
                    dve.memset(V[:, U - 1], 0.0).then_inc(s_set, 1)
                    dve.memset(Gt[:, U - 1], 0.0).then_inc(s_set, 1)
                    dve.memset(z, 0.0).then_inc(s_w, Q)
                    dve.memset(cm_e, 0.0).then_inc(s_set, 1)
                    dve.memset(AGG, 0.0).then_inc(s_fin, 1)
                    dve.tensor_copy(ident16, ident).then_inc(s_set, 1)
                    dve.memset(new, 0.0).then_inc(s_turned, NG)
                    dve.tensor_scalar(base, A12[:, :, 0], a2min[0:R], None, ALU.add).then_inc(s_fin, 1)
                    dve.wait_ge(s_fin, 2)
                    dve.wait_ge(fw_in, 80)
                    dve.tensor_scalar(temp, temp, 0.1, 5.0, ALU.max, ALU.min).then_inc(s_temp, 1)
                    dve.wait_ge(s_temp, 1)
                    dve.reciprocal(temp, temp).then_inc(s_temp, 1)
                    dve.wait_ge(s_temp, 2)
                    dve.wait_ge(fw_psum, 1)
                    for i in range(4):
                        dve.tensor_copy(WxT[:, 2 * i:2 * i + 2, :].rearrange("p h d -> p (h d)"), bank[i][0:G, :]
                                        ).then_inc(fw_done, 1)
                    dve.wait_ge(fw_psum, 2)

                    def heads(p):
                        return temp[0:p].unsqueeze(2).to_broadcast([p, FH, G])

                    def split(ap):
                        return ap.rearrange("p (h g) -> p h g", h=FH)

                    for c in range(DC):
                        dve.tensor_tensor(split(WL[:, c, :]), split(bank[4 + c][:, :]), heads(128), ALU.mult).then_inc(fw_done, 1)
                    dve.tensor_tensor(split(bL), split(bank[6][0:R, :]), bsl[0:R].unsqueeze(1).to_broadcast([R, FH, G]),
                                      ALU.add).then_inc(fw_done, 1)
                    dve.wait_ge(fw_done, 7)
                    dve.tensor_tensor(split(bL), split(bL), heads(R), ALU.mult).then_inc(fw_done, 1)
                    dve.wait_ge(fw_done, 8)

                    def add_sums(i, done, count):
                        dve.wait_ge(done, count)
                        dve.scalar_tensor_tensor(AGG, AGG, keepf, bank[bAgg][0:R, 0:D + 1], ALU.mult,
                                                 ALU.add).then_inc(s_an, 1)
                        dve.wait_ge(s_an, SA * i + 1)
                        dve.tensor_scalar(sinv, AGG[:, D:D + 1], 1e-30, None, ALU.max).then_inc(s_agg, 1)
                        dve.wait_ge(s_agg, i + 1)
                        dve.reciprocal(sinv, sinv).then_inc(s_an, 1)
                        dve.wait_ge(s_an, SA * i + 2)
                        dve.wait_ge(s_anT, i)
                        dve.tensor_scalar(An, AGG, sinv, None, ALU.mult).then_inc(s_an, 1)

                    def add_x(i):
                        tile = dve.value_load(item_tile[0:1, bass.ds(i, 1)], min_val=0, max_val=T - 1)
                        dve.wait_ge(s_out, i + 1)
                        dve.scalar_tensor_tensor(X[:, tile, :], bank[bOut][0:R, 0:D], is_last[:, bass.ds(i, 1)],
                                                 X[:, tile, :], ALU.mult, ALU.add).then_inc(s_x, 1)
                        dve.wait_ge(s_x, i + 1)
                        dve.bn_stats(stats2[:, tile, :], X[:, tile, :]).then_inc(s_stat, 1)

                    def build(i, u, k):
                        rows = Gt[:, u, :].rearrange("p (q w) -> p q w", q=Q)
                        for part, gathered in enumerate((half_gathered, rest_gathered)):
                            lo, hi = PARTS[part][0], PARTS[part][-1] + 1
                            dve.wait_ge(gathered[u], 16 * (hi - lo) * (k + 1))
                            dve.tensor_scalar(score[:, u, lo:hi], rows[:, lo:hi, D + 1], a2min, None,
                                              ALU.subtract).then_inc(s_score, 1)
                            if part == 0:
                                dve.tensor_copy(local[:, u, :], item[:, u, :].rearrange("p (q w) -> p q w", w=2)[:, :, 1]
                                                ).then_inc(s_score, 1)
                            dve.wait_ge(s_score, 3 * (i + U - 1) + 2 + part)
                            for q in PARTS[part]:
                                dve.tensor_scalar(V[:, u, q, :], iota_r[:, 0:R], local[:, u, q:q + 1],
                                                  score[:, u, q:q + 1], ALU.is_equal, ALU.mult).then_inc(s_v, 1)

                    def largest(i, u):
                        dve.wait_ge(s_v, Q * i + Q)
                        dve.wait_ge(s_mostT, i)
                        dve.tensor_reduce(most, V[:, u].rearrange("p q r -> p r q"), AX, ALU.max).then_inc(s_most, 1)

                    def maxima(i):
                        def small(j, ins):
                            ins.then_inc(s_small, 1)
                            dve.wait_ge(s_small, SM * i + j)

                        tile = dve.value_load(item_tile[0:1, bass.ds(i + 1, 1)], min_val=0, max_val=T - 1)
                        own = base[:, bass.ds(tile, 1)]
                        dve.wait_ge(s_fade, i)
                        dve.wait_ge(s_cm, i)
                        small(1, dve.tensor_tensor(old, new, is_same[:, bass.ds(i, 1)], ALU.mult))
                        dve.wait_ge(s_mostT, i + 1)
                        small(2, dve.tensor_reduce(new, bank[bMost][0:R, 0:128], AX, ALU.max))
                        small(3, dve.tensor_tensor(new, new, old, ALU.max))
                        dve.tensor_tensor(zo, own, old, ALU.add).then_inc(s_small, 1)
                        small(5, dve.tensor_tensor(zn, own, new, ALU.add))
                        dve.tensor_scalar(cm[:, 0:1], own, 0.0, None, ALU.add).then_inc(s_small, 1)
                        dve.scalar_tensor_tensor(mo, zo, 0.01, zo, ALU.mult, ALU.max).then_inc(s_small, 1)
                        small(8, dve.scalar_tensor_tensor(cm[:, 1:2], zn, 0.01, zn, ALU.mult, ALU.max))
                        dve.tensor_tensor(mo, mo, cm[:, 1:2], ALU.subtract).then_inc(s_small, 1)
                        small(10, dve.tensor_copy(parts[:, 0, :], cm))
                        small(11, dve.tensor_tensor(left, cm, parts[:, 0, :], ALU.subtract))
                        small(12, dve.tensor_copy(parts[:, 1, :], left))
                        dve.tensor_tensor(parts[:, 2, :], left, parts[:, 1, :], ALU.subtract).then_inc(s_small, 1)

                    def exponents(i, u):
                        dve.wait_ge(s_cm, i + 1)
                        dve.tensor_reduce(cm_e, bank[bCM][:, 0:6 * Q].rearrange("p (q s w) -> p q w s", q=Q, s=3), AX,
                                          ALU.add).then_inc(s_cme, 1)
                        dve.wait_ge(s_cme, i + 1)
                        dve.tensor_tensor(z, cm_e[:, :, 0], score[:, u, :], ALU.add).then_inc(s_z, 1)
                        dve.wait_ge(s_z, SZ * i + 1)
                        dve.scalar_tensor_tensor(z, z, 0.01, z, ALU.mult, ALU.max).then_inc(s_z, 1)
                        dve.wait_ge(s_z, SZ * i + 2)
                        dve.tensor_tensor(z, z, cm_e[:, :, 1], ALU.subtract).then_inc(s_z, 1)
                        dve.wait_ge(s_z, SZ * i + 3)
                        dve.tensor_scalar(z, z, 0.0, None, ALU.min).then_inc(s_z, 1)

                    def weigh(i, u):
                        dve.wait_ge(s_exp, i + 1)
                        for q in range(Q):
                            dve.tensor_scalar(V[:, u, q, :], iota_r[:, 0:R], local[:, u, q:q + 1], weight[:, q:q + 1],
                                              ALU.is_equal, ALU.mult).then_inc(s_w, 1)

                    def step(i, u, k, ahead):
                        maxima(i)
                        if ahead:
                            build(i + 1, (u + 1) % U, k + 1 if u == U - 1 else k)
                        add_sums(i, used[(u - 1) % U], k + 1 if u == 0 else k + 2)
                        exponents(i, u)
                        if ahead:
                            largest(i + 1, (u + 1) % U)
                        dve.wait_ge(s_fade, i + 1)
                        dve.tensor_tensor(keepf, fade, is_same[:, bass.ds(i, 1)], ALU.mult).then_inc(s_fin, 1)
                        weigh(i, u)
                        add_x(i)

                    build(0, 0, 0)
                    largest(0, 0)
                    with dve.Fori(0, more) as k:
                        for u in range(U):
                            step(U * k + u, u, k, True)
                    for u in range(TAIL):
                        step(U * more + u, u, more, u < TAIL - 1)
                    add_sums(U * more + TAIL, used[TAIL - 1], more + 2)
                    add_x(U * more + TAIL)

        a = Arena(rest, after_stats, REST_W)
        M2 = a.take(128, IC, D)
        mean, rstd, shift = a.take(R, T), a.take(R, T), a.take(R, T)
        after_m2 = a.at
        FB, FU = 4, 8
        SW = big[0:R, 0:T * INNER].rearrange("p (t n) -> p t n", t=T)
        with ExitStack() as _:
            var = a.take(R, T)
            y, yT = a.take(R, FU, D + 1), a.take(128, 2, DC, R)
            L = a.take(R, FB, INNER)
            top, tot, inv = a.take(R, 2, FH), a.take(R, 2, FH), a.take(R, 2, FH)
            zero_row = a.take(1, 512)
            fs = sem("fs")
            sq_in, sq_done = sem("sq_in"), sem("sq_done")
            y_done, yT_psum, yT_done, l_psum, l_done = (sem(n) for n in ("y_done", "yT_psum", "yT_done", "l_psum", "l_done"))
            l_top, l_sub, l_exp, l_tot, l_inv, sw_done, sum_psum = (sem(n) for n in (
                "l_top", "l_sub", "l_exp", "l_tot", "l_inv", "sw_done", "sum_psum"))
            zeros, sw_kept = sem("zeros"), sem("sw_kept")
            with nc.Block() as block:
                @block.tensor
                def _(pe):
                    pe.wait_ge(zeros, 3)
                    for c in range(IC):
                        pe.matmul(bank[4 + c][:, 0:D + 1], zero_row[:, 0:128], zero_row[:, 0:D + 1], start=True,
                                  stop=False, skip_group_check=True)

                    def turn(t, u):
                        pe.wait_ge(y_done, t + 1)
                        for c in range(DC):
                            mm = pe.transpose(bank[3 * (u % 2)][:, c * R:(c + 1) * R], y[:, u, c * 128:(c + 1) * 128],
                                              ident[0:R, 0:R])
                        mm.then_inc(yT_psum, 1)

                    def logits(t, u):
                        pe.wait_ge(yT_done, t + 1)
                        for c in range(DC):
                            mm = pe.matmul(bank[1 + u % 2][0:R, :], yT[:, u % 2, c, :], WL[:, c, :], start=c == 0,
                                           stop=c == DC - 1)
                        mm.then_inc(l_psum, 1)

                    def sums(t, u):
                        pe.wait_ge(sw_done, t + 2)
                        for c in range(IC):
                            mm = pe.matmul(bank[4 + c][:, 0:D + 1], L[:, u % FB, c * 128:(c + 1) * 128], y[:, u, :],
                                           start=False, stop=False, skip_group_check=True)
                        mm.then_inc(sum_psum, 1)

                    def step(t, u, ahead):
                        if ahead:
                            pe.wait_ge(yT_done, t + 1)
                            turn(t + 2, (u + 2) % FU)
                        sums(t - 1, (u - 1) % FU)
                        if ahead:
                            pe.wait_ge(l_done, t + 1)
                            logits(t + 2, (u + 2) % FU)

                    for t in range(2):
                        turn(t, t)
                        logits(t, t)
                    with pe.Fori(0, (T - 2) // FU) as k:
                        for i in range(FU):
                            step(FU * k + i, i, True)
                    for t in range(T - 2, T):
                        step(t, t % FU, False)
                    sums(T - 1, (T - 1) % FU)
                    for c in range(IC):
                        mm = pe.matmul(bank[4 + c][:, 0:D + 1], zero_row[:, 0:128], zero_row[:, 0:D + 1], start=False,
                                       stop=True, skip_group_check=True)
                    mm.then_inc(sum_psum, 1)
                    pe.wait_ge(sum_psum, T + 2)

                @block.scalar
                def _(act):
                    act.wait_ge(sq_in, 1)
                    act.activation(rstd, var, ACT.Sqrt).then_inc(sq_done, 1)

                    def turned(t, u):
                        act.wait_ge(yT_psum, t + 1)
                        act.copy(yT[:, u % 2].rearrange("p c r -> p (c r)"), bank[3 * (u % 2)][:, 0:DC * R]
                                 ).then_inc(yT_done, 1)

                    def exp(t, u):
                        act.wait_ge(l_sub, t + 1)
                        act.activation(L[:, u], L[:, u], ACT.Exp).then_inc(l_exp, 1)

                    for t in range(2):
                        turned(t, t)
                    exp(0, 0)
                    with act.Fori(0, (T - 2) // FB) as k:
                        for u in range(FB):
                            t = FB * k + u
                            act.wait_ge(l_psum, t + 1)
                            turned(t + 2, (u + 2) % FB)
                            exp(t + 1, (u + 1) % FB)
                    exp(T - 1, (T - 1) % FB)

                @block.gpsimd
                def _(pool):
                    pool.memset(zero_row, 0.0).then_inc(zeros, 1)
                    pool.memset(L[:, FB - 1], 0.0).then_inc(zeros, 1)
                    pool.memset(y[:, FU - 1], 0.0).then_inc(zeros, 1)

                    def keep_sw(t, u):
                        pool.wait_ge(sw_done, t + 2)
                        pool.tensor_copy(SW[:, t, :], L[:, u]).then_inc(sw_kept, 1)

                    with pool.Fori(0, T // FB) as k:
                        for u in range(FB):
                            keep_sw(FB * k + u, u)
                    for t in range(T - T % FB, T):
                        keep_sw(t, t % FB)

                @block.vector
                def _(dve):
                    n = [0]

                    def step(ins):
                        n[0] += 1
                        ins.then_inc(fs, 1)
                        dve.wait_ge(fs, n[0])

                    mo, me = stats2[:, :, 4], stats2[:, :, 1]
                    step(dve.tensor_tensor(mean, me, mo, ALU.add))
                    step(dve.tensor_tensor(shift, me, mo, ALU.subtract))
                    step(dve.tensor_scalar(mean, mean, 0.5, None, ALU.mult))
                    step(dve.tensor_tensor(shift, shift, shift, ALU.mult))
                    step(dve.tensor_tensor(var, stats2[:, :, 2], stats2[:, :, 5], ALU.add))
                    step(dve.tensor_scalar(var, var, 1.0 / D, LN_EPS, ALU.mult, ALU.add))
                    step(dve.scalar_tensor_tensor(var, shift, 0.25, var, ALU.mult, ALU.add))
                    dve.wait_ge(zeros, 3)
                    dve.memset(y[:, :, D], 1.0).then_inc(sq_in, 1)
                    dve.wait_ge(sq_done, 1)
                    step(dve.reciprocal(rstd, rstd))
                    step(dve.tensor_tensor(shift, rstd, rstd, ALU.mult))
                    step(dve.tensor_tensor(shift, shift, var, ALU.mult))
                    step(dve.tensor_scalar(shift, shift, -0.5, 1.5, ALU.mult, ALU.add))
                    step(dve.tensor_tensor(rstd, rstd, shift, ALU.mult))
                    step(dve.scalar_tensor_tensor(shift, mean, -1.0, rstd, ALU.mult, ALU.mult))
                    def split(ap):
                        return ap.rearrange("p (h g) -> p h g", h=FH)

                    dve.memset(inv, 0.0).then_inc(sw_done, 1)
                    dve.memset(tot, 0.0).then_inc(sw_kept, 2)
                    dve.wait_ge(sw_done, 1)
                    dve.wait_ge(sw_kept, 2)

                    def normalise(t, u):
                        dve.tensor_scalar(y[:, u, 0:D], X[:, t, :], rstd[:, bass.ds(t, 1)], shift[:, bass.ds(t, 1)],
                                          ALU.mult, ALU.add).then_inc(y_done, 1)

                    def biased(t, u):
                        dve.wait_ge(l_psum, t + 1)
                        dve.tensor_tensor(L[:, u], bank[1 + u % 2][0:R, :], bL, ALU.add).then_inc(l_done, 1)

                    def maxima(t, u):
                        dve.wait_ge(l_done, t + 1)
                        dve.tensor_reduce(top[:, u % 2], split(L[:, u]), AX, ALU.max).then_inc(l_top, 1)

                    def below(t, u):
                        dve.wait_ge(l_top, t + 1)
                        dve.tensor_tensor(split(L[:, u]), split(L[:, u]),
                                          top[:, u % 2].unsqueeze(2).to_broadcast([R, FH, G]),
                                          ALU.subtract).then_inc(l_sub, 1)

                    def totals(t, u):
                        dve.wait_ge(l_exp, t + 1)
                        dve.tensor_reduce(tot[:, u % 2], split(L[:, u]), AX, ALU.add).then_inc(l_tot, 1)

                    def inverse(t, u):
                        dve.wait_ge(l_tot, t + 1)
                        dve.reciprocal(inv[:, u % 2], tot[:, u % 2]).then_inc(l_inv, 1)

                    def divide(t, u):
                        dve.wait_ge(l_inv, t + 1)
                        dve.tensor_tensor(split(L[:, u]), split(L[:, u]),
                                          inv[:, u % 2].unsqueeze(2).to_broadcast([R, FH, G]),
                                          ALU.mult).then_inc(sw_done, 1)

                    for t in range(3):
                        normalise(t, t)
                    biased(0, 0)
                    maxima(0, 0)
                    below(0, 0)

                    def soften(t, i, ahead=True, further=True):
                        u, v = i % FB, (i + 1) % FB
                        if ahead:
                            dve.wait_ge(sum_psum, t)
                            dve.wait_ge(sw_kept, t)
                            biased(t + 1, v)
                        if further:
                            normalise(t + 3, (i + 3) % FU)
                        totals(t, u)
                        if ahead:
                            maxima(t + 1, v)
                        inverse(t, u)
                        if ahead:
                            below(t + 1, v)
                        divide(t, u)

                    looped = (T - 3) // FU * FU
                    with dve.Fori(0, looped // FU) as k:
                        for i in range(FU):
                            soften(FU * k + i, i)
                    for t in range(looped, T):
                        soften(t, t % FU, t < T - 1, t < T - 3)

        with ExitStack() as _:
            a = Arena(rest, after_m2, REST_W)
            tok, tokT = a.take(128, IC, D + 1), a.take(128, DC, INNER)
            normT = a.take(1, INNER)
            den = a.take(128, IC)
            Wfx = a.take(128, DC, INNER)
            bfx = a.take(1, INNER)
            Wq, Wk, Wv = a.take(G, G), a.take(G, G), a.take(G, G)
            Wo = a.take(G, FH, D)
            sT, qT, kT, v = (a.take(G, INNER) for _ in range(4))
            P, PT = a.take(G, INNER), sT
            osT = qT
            ptop, ptot = a.take(G, FH), a.take(G, FH)
            aw_in, ap, ad, ae = sem("aw_in"), sem("attn_psum"), sem("attn_done"), sem("attn_exp")
            ae2 = sem("attn_parts")
            with nc.Block() as block:
                @block.sync
                def _(sp):
                    for to, of in ((Wfx, W_fx.rearrange("(c p) n -> p c n", p=128)), (bfx, row(b_fx)), (Wq, W_q), (Wk, W_k),
                                   (Wv, W_v), (Wo, W_out.rearrange("(h c) d -> c h d", h=FH))):
                        sp.dma_start(to, of).then_inc(aw_in, 16)

                def head(h, of=None):
                    return slice(h * G, (h + 1) * G)

                @block.tensor
                def _(pe):
                    pe.wait_ge(ad, 3)
                    for i in range(IC):
                        for c in range(DC):
                            pe.transpose(bank[c][:, i * 128:(i + 1) * 128], tok[:, i, c * 128:(c + 1) * 128], ident)
                        mm = pe.transpose(bank[2][0:1, i * 128:(i + 1) * 128], tok[:, i, D:D + 1], ident)
                    mm.then_inc(ap, 1)
                    pe.wait_ge(aw_in, 96)
                    pe.wait_ge(ad, 6)
                    for h in range(FH):
                        for c in range(DC):
                            pe.matmul(bank[3][0:G, head(h)], Wfx[:, c, head(h)], tokT[:, c, head(h)], start=c == 0, stop=False)
                        mm = pe.matmul(bank[3][0:G, head(h)], bfx[:, head(h)], normT[:, head(h)], start=False, stop=True)
                    mm.then_inc(ap, 1)
                    pe.wait_ge(ad, 7)
                    pe.matmul(bank[4][0:G, :], Wq, sT, start=True, stop=True)
                    pe.matmul(bank[5][0:G, :], Wk, sT, start=True, stop=True)
                    for h in range(FH):
                        mm = pe.matmul(bank[6][0:G, head(h)], sT[:, head(h)], Wv, start=True, stop=True)
                    mm.then_inc(ap, 1)
                    pe.wait_ge(ad, 10)
                    for h in range(FH):
                        mm = pe.matmul(bank[7][0:G, head(h)], qT[:, head(h)], kT[:, head(h)], start=True, stop=True)
                    mm.then_inc(ap, 1)
                    pe.wait_ge(ad, 15)
                    for h in range(FH):
                        mm = pe.transpose(bank[0][0:G, head(h)], P[:, head(h)], ident[0:G, 0:G])
                    mm.then_inc(ap, 1)
                    pe.wait_ge(ad, 16)
                    for h in range(FH):
                        mm = pe.matmul(bank[1][0:G, head(h)], v[:, head(h)], PT[:, head(h)], start=True, stop=True)
                    mm.then_inc(ap, 1)
                    pe.wait_ge(ad, 17)
                    for h in range(FH):
                        lo = (h % 2) * G
                        mm = pe.matmul(bank[2 + h // 2][lo:lo + G, 0:D], osT[:, head(h)], Wo[:, h, :], start=True, stop=True)
                    mm.then_inc(ap, 1)
                    pe.wait_ge(ap, 7)

                @block.scalar
                def _(act):
                    act.wait_ge(ad, 12)
                    act.activation(P, P, ACT.Exp, scale=SLICE_SCALE).then_inc(ae, 1)

                @block.vector
                def _(dve):
                    n = [0]

                    def step(ins):
                        n[0] += 1
                        ins.then_inc(ad, 1)
                        dve.wait_ge(ad, n[0])

                    def split(ap_):
                        return ap_.rearrange("p (h g) -> p h g", h=FH)

                    for i in range(IC):
                        ins = dve.tensor_scalar(den[:, i:i + 1], bank[4 + i][:, D:D + 1], EPS, None, ALU.add)
                        if i < IC - 1:
                            ins.then_inc(ae2, 1)
                    step(ins)
                    dve.wait_ge(ae2, IC - 1)
                    step(dve.reciprocal(den, den))
                    for i in range(IC):
                        ins = dve.tensor_scalar(tok[:, i, :], bank[4 + i][:, 0:D + 1], den[:, i:i + 1], None, ALU.mult)
                        if i < IC - 1:
                            ins.then_inc(ae2, 1)
                    step(ins)
                    dve.wait_ge(ap, 1)
                    step(dve.tensor_copy(tokT[:, 0, :], bank[0][:, :]))
                    step(dve.tensor_copy(tokT[:, 1, :], bank[1][:, :]))
                    step(dve.tensor_copy(normT, bank[2][0:1, :]))
                    dve.wait_ge(ap, 2)
                    step(dve.tensor_copy(sT, bank[3][0:G, :]))
                    dve.wait_ge(ap, 3)
                    step(dve.tensor_copy(qT, bank[4][0:G, :]))
                    step(dve.tensor_copy(kT, bank[5][0:G, :]))
                    step(dve.tensor_copy(v, bank[6][0:G, :]))
                    dve.wait_ge(ap, 4)
                    step(dve.tensor_reduce(ptop, split(bank[7][0:G, :]), AX, ALU.max))
                    step(dve.tensor_tensor(split(P), split(bank[7][0:G, :]), ptop.unsqueeze(2).to_broadcast([G, FH, G]),
                                           ALU.subtract))
                    dve.wait_ge(ae, 1)
                    step(dve.tensor_reduce(ptot, split(P), AX, ALU.add))
                    step(dve.reciprocal(ptot, ptot))
                    step(dve.tensor_tensor(split(P), split(P), ptot.unsqueeze(2).to_broadcast([G, FH, G]), ALU.mult))
                    dve.wait_ge(ap, 5)
                    step(dve.tensor_copy(PT, bank[0][0:G, :]))
                    dve.wait_ge(ap, 6)
                    step(dve.tensor_copy(osT, bank[1][0:G, :]))
                    dve.wait_ge(ap, 7)
                    for i in range(IC):
                        step(dve.tensor_copy(M2[:, i, :], bank[2 + i][:, 0:D]))

        with ExitStack() as _:
            a = Arena(rest, after_m2, REST_W)
            bout = a.take(R, D)
            sw_in = a.take(R, 2, INNER)
            swT = a.take(128, 2, IC, R)
            res = a.take(R, 2, D)
            bo_in, sw_here, swT_psum, swT_done, o_psum, o_sum, o_done = (sem(n) for n in (
                "bo_in", "sw_here", "swT_psum", "swT_done", "o_psum", "o_sum", "o_done"))
            o_out = [sem("o_out0"), sem("o_out1")]
            with nc.Block() as block:
                @block.sync
                def _(sp):
                    sp.dma_start(bout, row(b_out).to_broadcast([R, D])).then_inc(bo_in, 16)
                    with sp.Fori(0, T // 2) as k:
                        for u in range(2):
                            t = 2 * k + u
                            sp.wait_ge(o_done, t + 1)
                            sp.dma_start(out[bass.ds(t * R, R), :], res[:, u]).then_inc(o_out[u], 16)
                    for u in range(2):
                        sp.wait_ge(o_out[u], 16 * (T // 2))

                @block.gpsimd
                def _(pool):
                    for t in range(2):
                        pool.tensor_copy(sw_in[:, t], SW[:, t, :]).then_inc(sw_here, 1)
                    with pool.Fori(0, T // 2 - 1) as k:
                        for u in range(2):
                            t = 2 * k + u
                            pool.wait_ge(swT_psum, t + 1)
                            pool.tensor_copy(sw_in[:, u], SW[:, t + 2, :]).then_inc(sw_here, 1)

                @block.tensor
                def _(pe):
                    def turn(t, u):
                        pe.wait_ge(sw_here, t + 1)
                        for c in range(IC):
                            mm = pe.transpose(bank[u][:, c * R:(c + 1) * R], sw_in[:, u, c * 128:(c + 1) * 128],
                                              ident[0:R, 0:R])
                        mm.then_inc(swT_psum, 1)

                    def out_of(t, u):
                        pe.wait_ge(swT_done, t + 1)
                        for c in range(IC):
                            mm = pe.matmul(bank[2 + u][0:R, 0:D], swT[:, u, c, :], M2[:, c, :], start=c == 0,
                                           stop=c == IC - 1)
                        mm.then_inc(o_psum, 1)

                    turn(0, 0)
                    with pe.Fori(0, (T - 2) // FU) as k:
                        for i in range(FU):
                            t, u = FU * k + i, i % 2
                            pe.wait_ge(swT_done, t)
                            turn(t + 1, 1 - u)
                            pe.wait_ge(o_sum, FU * k + (i - 1) if i else FU * k)
                            out_of(t, u)
                    pe.wait_ge(swT_done, T - 2)
                    turn(T - 1, 1)
                    for t in range(T - 2, T):
                        pe.wait_ge(o_sum, t - 1)
                        out_of(t, t % 2)

                @block.scalar
                def _(act):
                    def turned(t, u):
                        act.wait_ge(swT_psum, t + 1)
                        act.copy(swT[:, u].rearrange("p c r -> p (c r)"), bank[u][:, 0:IC * R]).then_inc(swT_done, 1)

                    for t in range(2):
                        turned(t, t)
                    with act.Fori(0, T // 2 - 1) as k:
                        for u in range(2):
                            t = 2 * k + u
                            act.wait_ge(o_psum, t + 1)
                            turned(t + 2, u)

                @block.vector
                def _(dve):
                    dve.wait_ge(bo_in, 16)
                    with dve.Fori(0, T // 2) as k:
                        for u in range(2):
                            t = 2 * k + u
                            dve.wait_ge(o_out[u], 16 * k)
                            dve.wait_ge(o_psum, t + 1)
                            dve.tensor_tensor(res[:, u], X[:, t, :], bank[2 + u][0:R, 0:D], ALU.add).then_inc(o_sum, 1)
                            dve.wait_ge(o_sum, t + 1)
                            dve.tensor_tensor(res[:, u], res[:, u], bout, ALU.add).then_inc(o_done, 1)


_INS = ["x", "src", "dst", "L0_gnn_W_layer", "L0_gnn_b_layer", "L0_gnn_w_a1", "L0_gnn_b_a1", "L0_gnn_w_a2",
        "L0_gnn_b_a2", "L0_mix_wq", "L0_mix_bq", "L0_mix_wk", "L0_mix_bk", "L0_mix_wv", "L0_mix_bv", "L0_mix_wo",
        "L0_mix_bo", "L0_ffn_W_fx", "L0_ffn_b_fx", "L0_ffn_W_x", "L0_ffn_b_x", "L0_ffn_W_slice", "L0_ffn_b_slice",
        "L0_ffn_W_q", "L0_ffn_W_k", "L0_ffn_W_v", "L0_ffn_W_out", "L0_ffn_b_out", "L0_ffn_temperature"]


def kernel(**inputs):
    import numpy as _np
    import concourse.bacc as _bacc
    from concourse import mybir as _mybir
    from concourse.bass_utils import run_bass_kernel_spmd as _run

    nc = _bacc.Bacc("TRN2", target_bir_lowering=False, num_devices=1)
    arrays, args = {}, []
    for name in _INS:
        a = _np.ascontiguousarray(inputs[name])
        arrays[f"in_{name}_dram"] = a
        args.append(nc.dram_tensor(f"in_{name}_dram", a.shape, _mybir.dt.from_np(a.dtype), kind="ExternalInput").ap())
    result = nc.dram_tensor("out_dram", (N, D), F32, kind="ExternalOutput").ap()
    bass_gps(nc, *args, result)
    r = _run(nc, [arrays], core_ids=[0])
    return r.results[0]["out_dram"]
```
